# Optimizing a Trainium2 kernel written in Bass

```python
import numpy as np
import jax
import jax.numpy as jnp

def _softmax(x, axis=-1):
    return jax.nn.softmax(x, axis=axis)

def _gelu(x):
    return jax.nn.gelu(x, approximate=True)

def _silu(x):
    return jax.nn.silu(x)

def _sigmoid(x):
    return jax.nn.sigmoid(x)

def _layernorm(x, axis=-1, eps=1e-05):
    m = jnp.mean(x, axis=axis, keepdims=True)
    v = jnp.var(x, axis=axis, keepdims=True)
    return (x - m) / jnp.sqrt(v + eps)

def _scatter_add(tgt, idx, src, axis=0):
    return tgt.at[idx].add(src)

def _segment_sum(src, seg, n):
    return jax.ops.segment_sum(src, seg, n)
kernel_name = 'mk_xattn_seq_d4_seqx_r8_cc76fb'

def setup_inputs(seed: int=0):
    np.random.seed(seed)
    _w = jnp.asarray

    def _rec_inputs():
        import jax
        import jax.numpy as jnp
        _rk = jax.random.key(seed)
        x = 4.671e-05 + 0.9998 * jax.random.normal(jax.random.fold_in(_rk, 1), (64, 128, 128), jnp.float32)
        _lenS = 128 - jax.random.randint(jax.random.fold_in(_rk, 7), (64,), 0, max(1, 128 // 4) + 1, jnp.int32)
        _lenS2 = 77 - jax.random.randint(jax.random.fold_in(_rk, 8), (64,), 0, max(1, 77 // 4) + 1, jnp.int32)
        _ctx_1024P = jax.random.normal(jax.random.fold_in(_rk, 11), (64, 16, 128), jnp.float32)
        _ctx_1024c = jax.random.dirichlet(jax.random.fold_in(_rk, 511), 0.3 * jnp.ones((16,), jnp.float32), (64, 77))
        _ctx_1024t = jnp.einsum('bsk,bkd->bsd', _ctx_1024c, _ctx_1024P)
        _ctx_1024t = _ctx_1024t * jax.lax.rsqrt(jnp.mean(jnp.square(_ctx_1024t)) + 1e-12) * 0.953939
        ctx_1024 = -0.000171981 + 0.999946 * (_ctx_1024t + 0.3 * jax.random.normal(jax.random.fold_in(_rk, 611), (64, 77, 128), jnp.float32))
        return (x, ctx_1024)
    x, ctx_1024 = _rec_inputs()

    def _L0_xattn_setup():
        import jax, jax.numpy as jnp
        import numpy as np
        EMBED_DIM = 128
        LN_EPS = 1e-05

        def _layernorm(x, w, b):
            m = jnp.mean(x, axis=-1, keepdims=True)
            v = jnp.mean(jnp.square(x - m), axis=-1, keepdims=True)
            return (x - m) * jax.lax.rsqrt(v + LN_EPS) * w + b

        def _attention(q, k, v, scale):
            scores = jnp.einsum('bqd,bkd->bqk', q, k) * scale
            probs = jax.nn.softmax(scores, axis=-1)
            return jnp.einsum('bqk,bkd->bqd', probs, v)
        key = jax.random.key(seed)
        ks = jax.random.split(key, 16)
        B, SQ, SK, D, H = (8, 577, 13271, EMBED_DIM, 4)
        return {'input_features': jax.random.normal(ks[0], (B, SK, D), jnp.float32), 'query_feature': jax.random.normal(ks[1], (B, SQ, D), jnp.float32), 'norm1_w': jax.random.uniform(ks[2], (D,), jnp.float32, 0.5, 1.5), 'norm1_b': jax.random.normal(ks[3], (D,), jnp.float32) * 0.1, 'norm2_w': jax.random.uniform(ks[4], (D,), jnp.float32, 0.5, 1.5), 'norm2_b': jax.random.normal(ks[5], (D,), jnp.float32) * 0.1, 'norm3_w': jax.random.uniform(ks[6], (D,), jnp.float32, 0.5, 1.5), 'norm3_b': jax.random.normal(ks[7], (D,), jnp.float32) * 0.1, 'gamma1': jax.random.uniform(ks[8], (D,), jnp.float32, 0.5, 1.5), 'gamma2': jax.random.uniform(ks[9], (D,), jnp.float32, 0.5, 1.5), 'fc1_w': jax.random.normal(ks[10], (H, D), jnp.float32) * (1.0 / np.sqrt(D)), 'fc1_b': jax.random.normal(ks[11], (H,), jnp.float32) * 0.01, 'fc2_w': jax.random.normal(ks[12], (D, H), jnp.float32) * (1.0 / np.sqrt(H)), 'fc2_b': jax.random.normal(ks[13], (D,), jnp.float32) * 0.01}
    _L0_xattn_all = _L0_xattn_setup()
    _L0_xattn_in = {k: v for k, v in _L0_xattn_all.items() if k in ('norm1_w', 'norm1_b', 'norm2_w', 'norm2_b', 'norm3_w', 'norm3_b', 'gamma1', 'gamma2', 'fc1_w', 'fc1_b', 'fc2_w', 'fc2_b')}
    del _L0_xattn_all

    def _L1_xattn_setup():
        import jax, jax.numpy as jnp
        import numpy as np
        LN_EPS = 1e-05
        ATTN_EPS = 1e-06
        key = jax.random.key(seed)
        k1, k2, k3 = jax.random.split(key, 3)
        B, Nq, Nk, D = (8, 256, 256, 128)
        return {'query': jax.random.normal(k1, (B, Nq, D), dtype=jnp.float32), 'key': jax.random.normal(k2, (B, Nk, D), dtype=jnp.float32), 'value': jax.random.normal(k3, (B, Nk, D), dtype=jnp.float32), 'gamma': jnp.ones((D,), dtype=jnp.float32), 'beta': jnp.zeros((D,), dtype=jnp.float32)}
    _L1_xattn_all = _L1_xattn_setup()
    _L1_xattn_in = {k: v for k, v in _L1_xattn_all.items() if k in ('gamma', 'beta')}
    del _L1_xattn_all

    def _L2_xattn_setup():
        import jax, jax.numpy as jnp
        import numpy as np
        D, H, E, K, DFF = (128, 16, 8, 2, 512)
        B, L, T = (4, 64, 256)
        EPS = 1e-05

        def _xavier(key, shape):
            fan_in, fan_out = (shape[-1], shape[-2])
            a = jnp.sqrt(6.0 / (fan_in + fan_out))
            return jax.random.uniform(key, shape, jnp.float32, -a, a)

        def _ln(x, g, b):
            m = x.mean(-1, keepdims=True)
            v = ((x - m) ** 2).mean(-1, keepdims=True)
            return (x - m) / jnp.sqrt(v + EPS) * g + b

        def _mha(q_in, kv_in, in_w, in_b, out_w, out_b):
            wq, wk, wv = jnp.split(in_w, 3, axis=0)
            bq, bk, bv = jnp.split(in_b, 3, axis=0)
            dh = D // H

            def heads(x, w, b):
                y = x @ w.T + b
                return y.reshape(x.shape[0], x.shape[1], H, dh).transpose(0, 2, 1, 3)
            q = heads(q_in, wq, bq)
            k = heads(kv_in, wk, bk)
            v = heads(kv_in, wv, bv)
            scores = jnp.einsum('bhqd,bhkd->bhqk', q, k) / jnp.sqrt(jnp.float32(dh))
            attn = jax.nn.softmax(scores, axis=-1)
            out = jnp.einsum('bhqk,bhkd->bhqd', attn, v)
            out = out.transpose(0, 2, 1, 3).reshape(q_in.shape[0], q_in.shape[1], D)
            return out @ out_w.T + out_b

        def _fuse_moe(x, ln_g, ln_b, rw, rb, fc1_w, fc1_b, fc2_w, fc2_b):
            h = _ln(x, ln_g, ln_b)
            logits = h @ rw.T + rb
            vals, idx = jax.lax.top_k(logits, K)
            gates = jax.nn.softmax(vals, axis=-1)
            N = x.shape[0] * x.shape[1]
            hf = h.reshape(N, D)
            h1 = jax.nn.gelu(jnp.einsum('nd,efd->enf', hf, fc1_w) + fc1_b[:, None, :], approximate=False)
            eo = jnp.einsum('enf,edf->end', h1, fc2_w) + fc2_b[:, None, :]
            idx_f = idx.reshape(N, K)
            gates_f = gates.reshape(N, K)
            gathered = eo[idx_f, jnp.arange(N)[:, None], :]
            mixed = (gathered * gates_f[..., None]).sum(axis=1).reshape(x.shape)
            return x + mixed
        key = jax.random.key(seed)
        ks = jax.random.split(key, 16)
        inp = {'latents': jax.random.normal(ks[0], (B, L, D), jnp.float32), 'tokens': jax.random.normal(ks[1], (B, T, D), jnp.float32), 'sa_ln_g': jnp.ones((D,)), 'sa_ln_b': jnp.zeros((D,)), 'sa_in_w': _xavier(ks[2], (3 * D, D)), 'sa_in_b': jnp.zeros((3 * D,)), 'sa_out_w': _xavier(ks[3], (D, D)), 'sa_out_b': jnp.zeros((D,)), 'ca_q_ln_g': jnp.ones((D,)), 'ca_q_ln_b': jnp.zeros((D,)), 'ca_kv_ln_g': jnp.ones((D,)), 'ca_kv_ln_b': jnp.zeros((D,)), 'ca_in_w': _xavier(ks[4], (3 * D, D)), 'ca_in_b': jnp.zeros((3 * D,)), 'ca_out_w': _xavier(ks[5], (D, D)), 'ca_out_b': jnp.zeros((D,)), 'moe_ln_g': jnp.ones((D,)), 'moe_ln_b': jnp.zeros((D,)), 'router_w': _xavier(ks[6], (E, D)), 'router_b': jnp.zeros((E,)), 'e_fc1_w': jax.vmap(lambda k: _xavier(k, (DFF, D)))(jax.random.split(ks[7], E)), 'e_fc1_b': jnp.zeros((E, DFF)), 'e_fc2_w': jax.vmap(lambda k: _xavier(k, (D, DFF)))(jax.random.split(ks[8], E)), 'e_fc2_b': jnp.zeros((E, D))}
        return inp
    _L2_xattn_all = _L2_xattn_setup()
    _L2_xattn_in = {k: v for k, v in _L2_xattn_all.items() if k in ('sa_ln_g', 'sa_ln_b', 'sa_in_w', 'sa_in_b', 'sa_out_w', 'sa_out_b', 'ca_q_ln_g', 'ca_q_ln_b', 'ca_kv_ln_g', 'ca_kv_ln_b', 'ca_in_w', 'ca_in_b', 'ca_out_w', 'ca_out_b', 'moe_ln_g', 'moe_ln_b', 'router_w', 'router_b', 'e_fc1_w', 'e_fc1_b', 'e_fc2_w', 'e_fc2_b')}
    del _L2_xattn_all

    def _L3_xattn_setup():
        import jax, jax.numpy as jnp
        import numpy as np
        D_MODEL = 128
        N_HEADS = 16
        D_K = D_MODEL // N_HEADS
        D_FF = 512
        B = 2
        T = 256

        def _layernorm(x, gamma, beta, eps=1e-05):
            mu = jnp.mean(x, axis=-1, keepdims=True)
            var = jnp.var(x, axis=-1, keepdims=True)
            return (x - mu) * jax.lax.rsqrt(var + eps) * gamma + beta

        def _attention(q_in, kv_in, Wq, bq, Wk, bk, Wv, bv, mask):
            Q = jnp.einsum('btd,hdk->bhtk', q_in, Wq) + bq[None, :, None, :]
            K = jnp.einsum('bsd,hdk->bhsk', kv_in, Wk) + bk[None, :, None, :]
            V = jnp.einsum('bsd,hdk->bhsk', kv_in, Wv) + bv[None, :, None, :]
            scores = jnp.einsum('bhtk,bhsk->bhts', Q, K) / jnp.sqrt(jnp.asarray(D_K, Q.dtype))
            if mask is not None:
                scores = jnp.where(mask, scores, jnp.finfo(scores.dtype).min)
            attn = jax.nn.softmax(scores, axis=-1)
            out = jnp.einsum('bhts,bhsk->bhtk', attn, V)
            return out.transpose(0, 2, 1, 3).reshape(q_in.shape[0], q_in.shape[1], -1)
        key = jax.random.key(seed)
        ks = jax.random.split(key, 24)
        s = 0.02
        inp = {'dec_input': jax.random.normal(ks[0], (B, T, D_MODEL), jnp.float32), 'enc_output': jax.random.normal(ks[1], (B, T, D_MODEL), jnp.float32), 'Wq_s': jax.random.normal(ks[2], (N_HEADS, D_MODEL, D_K), jnp.float32) * s, 'bq_s': jnp.zeros((N_HEADS, D_K), jnp.float32), 'Wk_s': jax.random.normal(ks[3], (N_HEADS, D_MODEL, D_K), jnp.float32) * s, 'bk_s': jnp.zeros((N_HEADS, D_K), jnp.float32), 'Wv_s': jax.random.normal(ks[4], (N_HEADS, D_MODEL, D_K), jnp.float32) * s, 'bv_s': jnp.zeros((N_HEADS, D_K), jnp.float32), 'Wo_s': jax.random.normal(ks[5], (D_MODEL, D_MODEL), jnp.float32) * s, 'bo_s': jnp.zeros((D_MODEL,), jnp.float32), 'Wq_c': jax.random.normal(ks[6], (N_HEADS, D_MODEL, D_K), jnp.float32) * s, 'bq_c': jnp.zeros((N_HEADS, D_K), jnp.float32), 'Wk_c': jax.random.normal(ks[7], (N_HEADS, D_MODEL, D_K), jnp.float32) * s, 'bk_c': jnp.zeros((N_HEADS, D_K), jnp.float32), 'Wv_c': jax.random.normal(ks[8], (N_HEADS, D_MODEL, D_K), jnp.float32) * s, 'bv_c': jnp.zeros((N_HEADS, D_K), jnp.float32), 'Wo_c': jax.random.normal(ks[9], (D_MODEL, D_MODEL), jnp.float32) * s, 'bo_c': jnp.zeros((D_MODEL,), jnp.float32), 'W1': jax.random.normal(ks[10], (D_MODEL, D_FF), jnp.float32) * s, 'b1': jnp.zeros((D_FF,), jnp.float32), 'W2': jax.random.normal(ks[11], (D_FF, D_MODEL), jnp.float32) * s, 'b2': jnp.zeros((D_MODEL,), jnp.float32), 'g1': jnp.ones((D_MODEL,), jnp.float32), 'be1': jnp.zeros((D_MODEL,), jnp.float32), 'g2': jnp.ones((D_MODEL,), jnp.float32), 'be2': jnp.zeros((D_MODEL,), jnp.float32), 'g3': jnp.ones((D_MODEL,), jnp.float32), 'be3': jnp.zeros((D_MODEL,), jnp.float32)}
        return inp
    _L3_xattn_all = _L3_xattn_setup()
    _L3_xattn_in = {k: v for k, v in _L3_xattn_all.items() if k in ('Wq_s', 'bq_s', 'Wk_s', 'bk_s', 'Wv_s', 'bv_s', 'Wo_s', 'bo_s', 'Wq_c', 'bq_c', 'Wk_c', 'bk_c', 'Wv_c', 'bv_c', 'Wo_c', 'bo_c', 'W1', 'b1', 'W2', 'b2', 'g1', 'be1', 'g2', 'be2', 'g3', 'be3')}
    del _L3_xattn_all
    return {'x': x, 'ctx_1024': ctx_1024, 'L0_xattn_norm1_w': _L0_xattn_in['norm1_w'], 'L0_xattn_norm1_b': _L0_xattn_in['norm1_b'], 'L0_xattn_norm2_w': _L0_xattn_in['norm2_w'], 'L0_xattn_norm2_b': _L0_xattn_in['norm2_b'], 'L0_xattn_norm3_w': _L0_xattn_in['norm3_w'], 'L0_xattn_norm3_b': _L0_xattn_in['norm3_b'], 'L0_xattn_gamma1': _L0_xattn_in['gamma1'], 'L0_xattn_gamma2': _L0_xattn_in['gamma2'], 'L0_xattn_fc1_w': _L0_xattn_in['fc1_w'], 'L0_xattn_fc1_b': _L0_xattn_in['fc1_b'], 'L0_xattn_fc2_w': _L0_xattn_in['fc2_w'], 'L0_xattn_fc2_b': _L0_xattn_in['fc2_b'], 'L1_xattn_gamma': _L1_xattn_in['gamma'], 'L1_xattn_beta': _L1_xattn_in['beta'], 'L2_xattn_sa_ln_g': _L2_xattn_in['sa_ln_g'], 'L2_xattn_sa_ln_b': _L2_xattn_in['sa_ln_b'], 'L2_xattn_sa_in_w': _L2_xattn_in['sa_in_w'], 'L2_xattn_sa_in_b': _L2_xattn_in['sa_in_b'], 'L2_xattn_sa_out_w': _L2_xattn_in['sa_out_w'], 'L2_xattn_sa_out_b': _L2_xattn_in['sa_out_b'], 'L2_xattn_ca_q_ln_g': _L2_xattn_in['ca_q_ln_g'], 'L2_xattn_ca_q_ln_b': _L2_xattn_in['ca_q_ln_b'], 'L2_xattn_ca_kv_ln_g': _L2_xattn_in['ca_kv_ln_g'], 'L2_xattn_ca_kv_ln_b': _L2_xattn_in['ca_kv_ln_b'], 'L2_xattn_ca_in_w': _L2_xattn_in['ca_in_w'], 'L2_xattn_ca_in_b': _L2_xattn_in['ca_in_b'], 'L2_xattn_ca_out_w': _L2_xattn_in['ca_out_w'], 'L2_xattn_ca_out_b': _L2_xattn_in['ca_out_b'], 'L2_xattn_moe_ln_g': _L2_xattn_in['moe_ln_g'], 'L2_xattn_moe_ln_b': _L2_xattn_in['moe_ln_b'], 'L2_xattn_router_w': _L2_xattn_in['router_w'], 'L2_xattn_router_b': _L2_xattn_in['router_b'], 'L2_xattn_e_fc1_w': _L2_xattn_in['e_fc1_w'], 'L2_xattn_e_fc1_b': _L2_xattn_in['e_fc1_b'], 'L2_xattn_e_fc2_w': _L2_xattn_in['e_fc2_w'], 'L2_xattn_e_fc2_b': _L2_xattn_in['e_fc2_b'], 'L3_xattn_Wq_s': _L3_xattn_in['Wq_s'], 'L3_xattn_bq_s': _L3_xattn_in['bq_s'], 'L3_xattn_Wk_s': _L3_xattn_in['Wk_s'], 'L3_xattn_bk_s': _L3_xattn_in['bk_s'], 'L3_xattn_Wv_s': _L3_xattn_in['Wv_s'], 'L3_xattn_bv_s': _L3_xattn_in['bv_s'], 'L3_xattn_Wo_s': _L3_xattn_in['Wo_s'], 'L3_xattn_bo_s': _L3_xattn_in['bo_s'], 'L3_xattn_Wq_c': _L3_xattn_in['Wq_c'], 'L3_xattn_bq_c': _L3_xattn_in['bq_c'], 'L3_xattn_Wk_c': _L3_xattn_in['Wk_c'], 'L3_xattn_bk_c': _L3_xattn_in['bk_c'], 'L3_xattn_Wv_c': _L3_xattn_in['Wv_c'], 'L3_xattn_bv_c': _L3_xattn_in['bv_c'], 'L3_xattn_Wo_c': _L3_xattn_in['Wo_c'], 'L3_xattn_bo_c': _L3_xattn_in['bo_c'], 'L3_xattn_W1': _L3_xattn_in['W1'], 'L3_xattn_b1': _L3_xattn_in['b1'], 'L3_xattn_W2': _L3_xattn_in['W2'], 'L3_xattn_b2': _L3_xattn_in['b2'], 'L3_xattn_g1': _L3_xattn_in['g1'], 'L3_xattn_be1': _L3_xattn_in['be1'], 'L3_xattn_g2': _L3_xattn_in['g2'], 'L3_xattn_be2': _L3_xattn_in['be2'], 'L3_xattn_g3': _L3_xattn_in['g3'], 'L3_xattn_be3': _L3_xattn_in['be3']}

def reference(x, ctx_1024, L0_xattn_norm1_w, L0_xattn_norm1_b, L0_xattn_norm2_w, L0_xattn_norm2_b, L0_xattn_norm3_w, L0_xattn_norm3_b, L0_xattn_gamma1, L0_xattn_gamma2, L0_xattn_fc1_w, L0_xattn_fc1_b, L0_xattn_fc2_w, L0_xattn_fc2_b, L1_xattn_gamma, L1_xattn_beta, L2_xattn_sa_ln_g, L2_xattn_sa_ln_b, L2_xattn_sa_in_w, L2_xattn_sa_in_b, L2_xattn_sa_out_w, L2_xattn_sa_out_b, L2_xattn_ca_q_ln_g, L2_xattn_ca_q_ln_b, L2_xattn_ca_kv_ln_g, L2_xattn_ca_kv_ln_b, L2_xattn_ca_in_w, L2_xattn_ca_in_b, L2_xattn_ca_out_w, L2_xattn_ca_out_b, L2_xattn_moe_ln_g, L2_xattn_moe_ln_b, L2_xattn_router_w, L2_xattn_router_b, L2_xattn_e_fc1_w, L2_xattn_e_fc1_b, L2_xattn_e_fc2_w, L2_xattn_e_fc2_b, L3_xattn_Wq_s, L3_xattn_bq_s, L3_xattn_Wk_s, L3_xattn_bk_s, L3_xattn_Wv_s, L3_xattn_bv_s, L3_xattn_Wo_s, L3_xattn_bo_s, L3_xattn_Wq_c, L3_xattn_bq_c, L3_xattn_Wk_c, L3_xattn_bk_c, L3_xattn_Wv_c, L3_xattn_bv_c, L3_xattn_Wo_c, L3_xattn_bo_c, L3_xattn_W1, L3_xattn_b1, L3_xattn_W2, L3_xattn_b2, L3_xattn_g1, L3_xattn_be1, L3_xattn_g2, L3_xattn_be2, L3_xattn_g3, L3_xattn_be3):
    import jax
    import jax.numpy as jnp

    def _L0_xattn_ref(input_features, query_feature, norm1_w, norm1_b, norm2_w, norm2_b, norm3_w, norm3_b, gamma1, gamma2, fc1_w, fc1_b, fc2_w, fc2_b):
        import jax, jax.numpy as jnp
        import numpy as np
        EMBED_DIM = 128
        LN_EPS = 1e-05

        def _layernorm(x, w, b):
            m = jnp.mean(x, axis=-1, keepdims=True)
            v = jnp.mean(jnp.square(x - m), axis=-1, keepdims=True)
            return (x - m) * jax.lax.rsqrt(v + LN_EPS) * w + b

        def _attention(q, k, v, scale):
            scores = jnp.einsum('bqd,bkd->bqk', q, k) * scale
            probs = jax.nn.softmax(scores, axis=-1)
            return jnp.einsum('bqk,bkd->bqd', probs, v)
        scale = EMBED_DIM ** (-0.5)
        norm_X = _layernorm(input_features, norm1_w, norm1_b)
        norm_F_L = _layernorm(query_feature, norm2_w, norm2_b)
        attended = _attention(norm_F_L, norm_X, norm_X, scale)
        h = jax.nn.gelu(attended @ fc1_w.T + fc1_b, approximate=False)
        cross_attended = h @ fc2_w.T + fc2_b
        norm_cross = _layernorm(cross_attended, norm3_w, norm3_b)
        self_attended = _attention(norm_cross, norm_cross, norm_cross, scale)
        skip_connect = cross_attended + gamma1 * self_attended
        return norm_F_L + gamma2 * skip_connect

    def _L1_xattn_ref(query, key, value, gamma, beta):
        import jax, jax.numpy as jnp
        import numpy as np
        LN_EPS = 1e-05
        ATTN_EPS = 1e-06
        Q_phi = jax.nn.elu(query)
        K_phi = jax.nn.elu(key)
        KV = jnp.einsum('bnd,bne->bde', K_phi, value)
        Z = 1.0 / (jnp.einsum('bnd,bd->bn', Q_phi, K_phi.sum(axis=1)) + ATTN_EPS)
        attn = jnp.einsum('bnd,bde->bne', Q_phi, KV) * Z[..., None]
        x = query + attn
        mean = jnp.mean(x, axis=-1, keepdims=True)
        var = jnp.mean(jnp.square(x - mean), axis=-1, keepdims=True)
        return (x - mean) * jax.lax.rsqrt(var + LN_EPS) * gamma + beta

    def _L2_xattn_ref(latents, tokens, sa_ln_g, sa_ln_b, sa_in_w, sa_in_b, sa_out_w, sa_out_b, ca_q_ln_g, ca_q_ln_b, ca_kv_ln_g, ca_kv_ln_b, ca_in_w, ca_in_b, ca_out_w, ca_out_b, moe_ln_g, moe_ln_b, router_w, router_b, e_fc1_w, e_fc1_b, e_fc2_w, e_fc2_b):
        import jax, jax.numpy as jnp
        import numpy as np
        D, H, E, K, DFF = (128, 16, 8, 2, 512)
        B, L, T = (4, 64, 256)
        EPS = 1e-05

        def _xavier(key, shape):
            fan_in, fan_out = (shape[-1], shape[-2])
            a = jnp.sqrt(6.0 / (fan_in + fan_out))
            return jax.random.uniform(key, shape, jnp.float32, -a, a)

        def _ln(x, g, b):
            m = x.mean(-1, keepdims=True)
            v = ((x - m) ** 2).mean(-1, keepdims=True)
            return (x - m) / jnp.sqrt(v + EPS) * g + b

        def _mha(q_in, kv_in, in_w, in_b, out_w, out_b):
            wq, wk, wv = jnp.split(in_w, 3, axis=0)
            bq, bk, bv = jnp.split(in_b, 3, axis=0)
            dh = D // H

            def heads(x, w, b):
                y = x @ w.T + b
                return y.reshape(x.shape[0], x.shape[1], H, dh).transpose(0, 2, 1, 3)
            q = heads(q_in, wq, bq)
            k = heads(kv_in, wk, bk)
            v = heads(kv_in, wv, bv)
            scores = jnp.einsum('bhqd,bhkd->bhqk', q, k) / jnp.sqrt(jnp.float32(dh))
            attn = jax.nn.softmax(scores, axis=-1)
            out = jnp.einsum('bhqk,bhkd->bhqd', attn, v)
            out = out.transpose(0, 2, 1, 3).reshape(q_in.shape[0], q_in.shape[1], D)
            return out @ out_w.T + out_b

        def _fuse_moe(x, ln_g, ln_b, rw, rb, fc1_w, fc1_b, fc2_w, fc2_b):
            h = _ln(x, ln_g, ln_b)
            logits = h @ rw.T + rb
            vals, idx = jax.lax.top_k(logits, K)
            gates = jax.nn.softmax(vals, axis=-1)
            N = x.shape[0] * x.shape[1]
            hf = h.reshape(N, D)
            h1 = jax.nn.gelu(jnp.einsum('nd,efd->enf', hf, fc1_w) + fc1_b[:, None, :], approximate=False)
            eo = jnp.einsum('enf,edf->end', h1, fc2_w) + fc2_b[:, None, :]
            idx_f = idx.reshape(N, K)
            gates_f = gates.reshape(N, K)
            gathered = eo[idx_f, jnp.arange(N)[:, None], :]
            mixed = (gathered * gates_f[..., None]).sum(axis=1).reshape(x.shape)
            return x + mixed
        q = _ln(latents, sa_ln_g, sa_ln_b)
        x = latents + _mha(q, q, sa_in_w, sa_in_b, sa_out_w, sa_out_b)
        qc = _ln(x, ca_q_ln_g, ca_q_ln_b)
        kv = _ln(tokens, ca_kv_ln_g, ca_kv_ln_b)
        x = x + _mha(qc, kv, ca_in_w, ca_in_b, ca_out_w, ca_out_b)
        return _fuse_moe(x, moe_ln_g, moe_ln_b, router_w, router_b, e_fc1_w, e_fc1_b, e_fc2_w, e_fc2_b)

    def _L3_xattn_ref(dec_input, enc_output, Wq_s, bq_s, Wk_s, bk_s, Wv_s, bv_s, Wo_s, bo_s, Wq_c, bq_c, Wk_c, bk_c, Wv_c, bv_c, Wo_c, bo_c, W1, b1, W2, b2, g1, be1, g2, be2, g3, be3):
        import jax, jax.numpy as jnp
        import numpy as np
        D_MODEL = 128
        N_HEADS = 16
        D_K = D_MODEL // N_HEADS
        D_FF = 512
        B = 2
        T = 256

        def _layernorm(x, gamma, beta, eps=1e-05):
            mu = jnp.mean(x, axis=-1, keepdims=True)
            var = jnp.var(x, axis=-1, keepdims=True)
            return (x - mu) * jax.lax.rsqrt(var + eps) * gamma + beta

        def _attention(q_in, kv_in, Wq, bq, Wk, bk, Wv, bv, mask):
            Q = jnp.einsum('btd,hdk->bhtk', q_in, Wq) + bq[None, :, None, :]
            K = jnp.einsum('bsd,hdk->bhsk', kv_in, Wk) + bk[None, :, None, :]
            V = jnp.einsum('bsd,hdk->bhsk', kv_in, Wv) + bv[None, :, None, :]
            scores = jnp.einsum('bhtk,bhsk->bhts', Q, K) / jnp.sqrt(jnp.asarray(D_K, Q.dtype))
            if mask is not None:
                scores = jnp.where(mask, scores, jnp.finfo(scores.dtype).min)
            attn = jax.nn.softmax(scores, axis=-1)
            out = jnp.einsum('bhts,bhsk->bhtk', attn, V)
            return out.transpose(0, 2, 1, 3).reshape(q_in.shape[0], q_in.shape[1], -1)
        Tq = dec_input.shape[1]
        causal = jnp.tril(jnp.ones((Tq, Tq), bool))[None, None, :, :]
        sa = _attention(dec_input, dec_input, Wq_s, bq_s, Wk_s, bk_s, Wv_s, bv_s, causal)
        sa = sa @ Wo_s.T if False else jnp.einsum('btd,ed->bte', sa, Wo_s.T) if False else sa @ Wo_s + bo_s
        x1 = _layernorm(dec_input + sa, g1, be1)
        ca = _attention(x1, enc_output, Wq_c, bq_c, Wk_c, bk_c, Wv_c, bv_c, None)
        ca = ca @ Wo_c + bo_c
        x2 = _layernorm(x1 + ca, g2, be2)
        ffn = jax.nn.relu(x2 @ W1 + b1) @ W2 + b2
        x3 = _layernorm(x2 + ffn, g3, be3)
        return x3
    x = _L0_xattn_ref(ctx_1024, x, L0_xattn_norm1_w, L0_xattn_norm1_b, L0_xattn_norm2_w, L0_xattn_norm2_b, L0_xattn_norm3_w, L0_xattn_norm3_b, L0_xattn_gamma1, L0_xattn_gamma2, L0_xattn_fc1_w, L0_xattn_fc1_b, L0_xattn_fc2_w, L0_xattn_fc2_b)
    x = _L1_xattn_ref(x, ctx_1024, ctx_1024, L1_xattn_gamma, L1_xattn_beta)
    x = _L2_xattn_ref(x, ctx_1024, L2_xattn_sa_ln_g, L2_xattn_sa_ln_b, L2_xattn_sa_in_w, L2_xattn_sa_in_b, L2_xattn_sa_out_w, L2_xattn_sa_out_b, L2_xattn_ca_q_ln_g, L2_xattn_ca_q_ln_b, L2_xattn_ca_kv_ln_g, L2_xattn_ca_kv_ln_b, L2_xattn_ca_in_w, L2_xattn_ca_in_b, L2_xattn_ca_out_w, L2_xattn_ca_out_b, L2_xattn_moe_ln_g, L2_xattn_moe_ln_b, L2_xattn_router_w, L2_xattn_router_b, L2_xattn_e_fc1_w, L2_xattn_e_fc1_b, L2_xattn_e_fc2_w, L2_xattn_e_fc2_b)
    x = _L3_xattn_ref(x, ctx_1024, L3_xattn_Wq_s, L3_xattn_bq_s, L3_xattn_Wk_s, L3_xattn_bk_s, L3_xattn_Wv_s, L3_xattn_bv_s, L3_xattn_Wo_s, L3_xattn_bo_s, L3_xattn_Wq_c, L3_xattn_bq_c, L3_xattn_Wk_c, L3_xattn_bk_c, L3_xattn_Wv_c, L3_xattn_bv_c, L3_xattn_Wo_c, L3_xattn_bo_c, L3_xattn_W1, L3_xattn_b1, L3_xattn_W2, L3_xattn_b2, L3_xattn_g1, L3_xattn_be1, L3_xattn_g2, L3_xattn_be2, L3_xattn_g3, L3_xattn_be3)
    return x

_drawn_inputs = setup_inputs


def setup_inputs(seed=0):
    import zlib

    import numpy as np

    out = dict(_drawn_inputs(seed))
    spreads = {'L1_xattn_gamma': (1.0, 0.2),
     'L1_xattn_beta': (0.0, 0.1),
     'L2_xattn_sa_ln_g': (1.0, 0.2),
     'L2_xattn_sa_ln_b': (0.0, 0.1),
     'L2_xattn_sa_in_b': (0.0, 0.1),
     'L2_xattn_sa_out_b': (0.0, 0.1),
     'L2_xattn_ca_q_ln_g': (1.0, 0.6),
     'L2_xattn_ca_q_ln_b': (0.0, 0.534),
     'L2_xattn_ca_kv_ln_g': (1.0, 0.2),
     'L2_xattn_ca_kv_ln_b': (0.0, 0.1),
     'L2_xattn_ca_in_b': (0.0, 0.1),
     'L2_xattn_ca_out_b': (0.0, 0.1),
     'L2_xattn_moe_ln_g': (1.0, 0.2),
     'L2_xattn_moe_ln_b': (0.0, 0.1),
     'L2_xattn_router_b': (0.0, 0.1),
     'L2_xattn_e_fc1_b': (0.0, 0.1),
     'L2_xattn_e_fc2_b': (0.0, 0.1),
     'L3_xattn_bq_s': (0.0, 2.0),
     'L3_xattn_bk_s': (0.0, 2.0),
     'L3_xattn_bv_s': (0.0, 0.549),
     'L3_xattn_bo_s': (0.0, 0.1),
     'L3_xattn_bq_c': (0.0, 2.0),
     'L3_xattn_bk_c': (0.0, 2.0),
     'L3_xattn_bv_c': (0.0, 0.425),
     'L3_xattn_bo_c': (0.0, 0.1),
     'L3_xattn_b1': (0.0, 0.288),
     'L3_xattn_b2': (0.0, 0.1),
     'L3_xattn_g1': (1.0, 0.2),
     'L3_xattn_be1': (0.0, 0.1),
     'L3_xattn_g2': (1.0, 0.2),
     'L3_xattn_be2': (0.0, 0.1),
     'L3_xattn_g3': (1.0, 0.2),
     'L3_xattn_be3': (0.0, 0.1)}
    factors = {'L3_xattn_Wq_s': 22.971,
     'L3_xattn_Wk_s': 22.403,
     'L3_xattn_Wq_c': 8.0,
     'L3_xattn_Wk_c': 8.0}
    for name, (base, spread) in spreads.items():
        noise = np.random.default_rng([zlib.crc32(name.encode()), seed]).standard_normal(out[name].shape)
        drawn = base * np.exp(spread * noise) if base else spread * noise
        out[name] = jnp.asarray(drawn.astype(out[name].dtype))
    for name, factor in factors.items():
        out[name] = (out[name] * factor).astype(out[name].dtype)
    return out
```

```python
from contextlib import ExitStack

import concourse.bass as bass
from concourse import mybir

F32 = mybir.dt.float32
F16 = mybir.dt.float16
BF16 = mybir.dt.bfloat16
U32 = mybir.dt.uint32
ACT = mybir.ActivationFunctionType
ALU = mybir.AluOpType
AX = mybir.AxisListType

P = 128
D = 128
T = 128
C = 77
GROUP = 4
N = GROUP * T
HEADS = 16
DH = D // HEADS
SLOTS = 4
PARTS = 4
TILES = HEADS // SLOTS
VW = 32
EXPERTS = 8
CHUNKS = 4
LN_EPS = 1e-5
ATTN_EPS = 1e-6
MAX_SCALE = 256.0
MASKED = -1e30

COLS = ["norm1_w", "norm1_b", "norm2_w", "norm2_b", "norm3_w", "norm3_b", "sa_g", "sa_b", "caq_g", "caq_b",
        "cakv_g", "cakv_b", "moe_g", "moe_b", "g1", "be1", "g2", "be2"]
COLS += [f"b{w}{m}" for m in range(4) for w in "qkv"]
COLS += [f"ffn_b1_{c}" for c in range(CHUNKS)] + [f"moe_b1_{e}_{c}" for e in range(EXPERTS) for c in range(CHUNKS)]
ROWS = ["norm2_w", "norm2_b", "gamma1", "gamma2", "norm3_w", "norm3_b", "l1_gamma", "l1_beta",
        "sa_out_b", "ca_out_b", "bo_s", "bo_c", "ffn_b2", "g1", "be1", "g2", "be2", "g3", "be3"]
MATS = [f"w{w}{m}" for m in range(4) for w in "qkvo"]

SELF2, CROSS2, SELF3, CROSS3 = range(4)
KEYS = [T, C, T, C]
CAUSAL = [False, False, True, False]
UNITS = 2 * GROUP

LN_CTX, LN_X, LN_CROSS, LN_L1, LN_SA, LN_CAQ, LN_MOE, LN_31, LN_32, LN_33 = range(10)
T_CTX, T_RAW, T_X, T_CROSS, T_L1, T_SA, T_CAQ, T_MOE, T_L3, T_31, T_32 = range(11)

PER = dict(
    x_in=16, ctx_in=16, out_stored=16,
    ln_stats=40, ln_mean=40, ln_var=10, ln_rstd=10, ln_hat=10,
    turned=11, feat=10,
    ctx_min=1, ctx_exp=1, ctx_phi=1, v0=1, v0_sb=1, kv=1, kv_sb=1,
    s0=1, max0=1, max0_t=1, max0_sb=1, s0_t=1, p0=1, hpre=1, h_rden=1, h_mul=1, h_in=1, h=1, h_t=1, h_t_sb=1,
    cross=1, cross_g=1, s1=1, max1=1, max1_t=1, max1_sb=1, s1_t=1, p1=1, pv1=1, pv1_rden=2, pv1_n=1, x1=1,
    x_scaled=1, x_affine=1, skip=1,
    x1_min=1, x1_exp=1, x1_phi=1, num=1, num_den=2, num_rden=2, l1_sum=1, l1_scaled=1, x2=1,
    k_proj=4, q_proj=4, v_proj=4, k_hi=4, q_hi=4, v_sb=4, k_split=8, q_split=8,
    k_shift=4 * 64, q_shift=4 * 64, m_shift=4 * 64, k_blk=16,
    scores=4 * UNITS, smax=4 * UNITS, m_t=4, m_sb=4, scores_t=4 * UNITS, probs=4 * UNITS, pv=4 * UNITS,
    o_sb=16, o_t=16, o_rden=16, o_norm=16, on_t=4, on_sb=4, attn=4, attn_sum=4,
    res_scaled=3, residual=5,
    router=1, logits=1, top=4, top_at=4, top_f=1, gap=1, gap_exp=1, gap_den=1, gate1=1, gate2=1, hot1=1, hot2=1,
    pick1=1, pick2=1, gates=1, gates_t=1, gates_sb=1, gate_bias=1, fc1=32, gelu=32, fc2=8, moe_acc=9,
    ffn1=4, ffn_relu=4, ffn2=1, ffn_sum=1, out_ready=1,
)

START = dict(ffn_sum=1, out_ready=1, out_stored=16)


def build(nc, a, out, steps):
    with ExitStack() as ctx:
        def sb(name, shape, dt=F32):
            return ctx.enter_context(nc.sbuf_tensor(name, shape, dt))

        S = {n: ctx.enter_context(nc.semaphore(n)) for n in PER}
        s_weights = ctx.enter_context(nc.semaphore("weights_in"))
        s_fill = ctx.enter_context(nc.semaphore("filled"))
        s_select = ctx.enter_context(nc.semaphore("selected"))
        s_held = ctx.enter_context(nc.semaphore("held"))
        s_const = ctx.enter_context(nc.semaphore("row_constants"))

        def at(it, name, count):
            return it * PER[name] + (START.get(name, 0) + count)

        score_ps = [ctx.enter_context(nc.psum_tensor(f"score_ps{i}", [P, 2, 512], F32)) for i in range(2)]
        bank = {i: ctx.enter_context(nc.psum_tensor(f"bank{i}", [P, 512], F32)) for i in range(4, 8)}
        low = {i: score_ps[i // 2][:, i % 2, :] for i in range(4)}

        cols = sb("cols", [P, len(COLS)])
        rows = sb("rows", [P, len(ROWS), D])
        mats = sb("mats", [P, len(MATS), D])
        fc1_w = sb("fc1_w", [P, 4])
        fc1_b = sb("fc1_b", [P, 4])
        fc2_aug = sb("fc2_aug", [5, D])
        router_w = sb("router_w", [P, EXPERTS])
        router_b = sb("router_b", [P, EXPERTS])
        moe_w1 = sb("moe_w1", [P, EXPERTS, CHUNKS, P])
        moe_w2 = sb("moe_w2", [P, EXPERTS, CHUNKS, D])
        moe_b2 = sb("moe_b2", [EXPERTS, D])
        ffn_w1 = sb("ffn_w1", [P, CHUNKS, P])
        ffn_w2 = sb("ffn_w2", [P, CHUNKS, D])
        slot_mask = sb("slot_mask", [P, SLOTS])
        expert_id = sb("expert_id", [P, EXPERTS])
        pick_seq = sb("pick_seq", [GROUP, GROUP, T])
        ident = sb("ident", [P, P])
        ident_bf = sb("ident_bf", [P, P], BF16)
        mask_q = sb("mask_q", [P, SLOTS, T], BF16)
        mask_k = sb("mask_k", [P, SLOTS, T], BF16)
        ln_eps = sb("ln_eps", [P, GROUP])
        minus_half = sb("minus_half", [P, GROUP])
        self_scale = sb("self_scale", [P, D])
        x_shift = sb("x_shift", [P, D])
        shift31 = sb("shift31", [P, D])
        shift32 = sb("shift32", [P, D])

        def col(name):
            i = COLS.index(name)
            return cols[:, i:i + 1]

        def row(name, n=GROUP):
            return rows[:, ROWS.index(name), :].unsqueeze(1).broadcast_to([P, n, D])

        def mat(name):
            return mats[:, MATS.index(name), :]

        x_tok = sb("x_tok", [P, GROUP, D])
        ctx_tok = sb("ctx_tok", [C, GROUP, D + 1])
        stats = sb("stats", [P, GROUP, 6])
        mean_var = sb("mean_var", [P, GROUP, 2])
        rstd = sb("rstd", [P, GROUP])
        var_eps = sb("var_eps", [P, GROUP])
        ctx_hat = sb("ctx_hat", [C, GROUP, D])
        ctx_neg = sb("ctx_neg", [C, GROUP, D])
        ctx_pow = sb("ctx_pow", [C, GROUP, D])
        ctx_phi = sb("ctx_phi", [C, GROUP, D])
        norm1_f = sb("norm1_f", [P, GROUP * C])
        cakv_f = sb("cakv_f", [P, GROUP * C])
        ctx_f = sb("ctx_f", [P, GROUP * C])
        v0 = sb("v0", [C, GROUP, 5])
        kv = sb("kv", [P, GROUP, D + 1])
        hat = sb("hat", [P, GROUP, D])
        feat = sb("feat", [P, N])
        max0 = sb("max0", [P, GROUP])
        max0_t = sb("max0_t", [GROUP, P])
        p0 = sb("p0", [C, N])
        h_rden = sb("h_rden", [P, GROUP])
        h_mul = sb("h_mul", [P, GROUP, 4])
        h_in = sb("h_in", [P, GROUP, 4])
        h = sb("h", [P, GROUP, 5])
        h_t = sb("h_t", [5, N])
        cross_g = sb("cross_g", [P, GROUP, D])
        cross_hat = sb("cross_hat", [P, GROUP, D + 1])
        max1 = sb("max1", [P, GROUP])
        max1_t = sb("max1_t", [GROUP, P])
        p1 = sb("p1", [P, N])
        pv1_rden = sb("pv1_rden", [P, GROUP])
        pv1_n = sb("pv1_n", [P, GROUP, D])
        x_scaled = sb("x_scaled", [P, GROUP, D])
        x_affine = sb("x_affine", [P, GROUP, D])
        skip = sb("skip", [P, GROUP, D])
        x1 = sb("x1", [P, GROUP, D])
        x1_neg = sb("x1_neg", [P, N])
        x1_pow = sb("x1_pow", [P, N])
        x1_phi = sb("x1_phi", [P, N])
        num_den = sb("num_den", [P, GROUP])
        num_rden = sb("num_rden", [P, GROUP])
        l1_sum = sb("l1_sum", [P, GROUP, D])
        l1_scaled = sb("l1_scaled", [P, GROUP, D])
        x_res = sb("x_res", [P, GROUP, D])
        residual = sb("residual", [P, GROUP, D])
        res_scaled = sb("res_scaled", [P, GROUP, D])
        k_nat = sb("k_nat", [P, PARTS, N], F16)
        q_nat = sb("q_nat", [P, PARTS, N], F16)
        k_int = sb("k_int", [P, TILES, N], F16)
        q_int = sb("q_int", [P, TILES, N], F16)
        k_blk = sb("k_blk", [P, TILES, SLOTS, N], F16)
        v_pad = sb("v_pad", [P, GROUP, HEADS, VW])
        smax = sb("smax", [P, GROUP, P])
        m_nat = sb("m_nat", [P, N], F16)
        probs = [sb(f"probs{i}", [P, 2, SLOTS * T]) for i in range(2)]
        o_sb = [sb(f"o_sb{i}", [P, TILES * T]) for i in range(2)]
        o_rden = sb("o_rden", [P, GROUP, HEADS])
        o_norm = sb("o_norm", [P, GROUP, D])
        on_f = sb("on_f", [P, N])
        logits = sb("logits", [P, GROUP, EXPERTS])
        top = sb("top", [P, GROUP, 8])
        top_at = sb("top_at", [P, GROUP, 8], U32)
        top_f = sb("top_f", [P, GROUP, 8])
        gap = sb("gap", [P, GROUP])
        gap_exp = sb("gap_exp", [P, GROUP])
        gap_den = sb("gap_den", [P, GROUP])
        gate1 = sb("gate1", [P, GROUP])
        gate2 = sb("gate2", [P, GROUP])
        hot1 = sb("hot1", [P, GROUP, EXPERTS])
        hot2 = sb("hot2", [P, GROUP, EXPERTS])
        pick1 = sb("pick1", [P, GROUP, EXPERTS])
        pick2 = sb("pick2", [P, GROUP, EXPERTS])
        gates = sb("gates", [P, GROUP, EXPERTS])
        gates_t = sb("gates_t", [EXPERTS, N])
        hidden = [sb(f"hidden{i}", [P, CHUNKS, N]) for i in range(2)]
        out_hat = sb("out_hat", [P, GROUP, D])
        out_scaled = sb("out_scaled", [P, GROUP, D])
        out_tok = sb("out_tok", [P, GROUP, D])

        loads = [(cols[:], a["cols"]), (rows[:], a["rows"]), (mats[:], a["mats"]), (fc1_w[:], a["fc1_w"]),
                 (fc1_b[:], a["fc1_b"]), (fc2_aug[:], a["fc2_aug"]), (router_w[:], a["router_w"]),
                 (router_b[:], a["router_b"]), (moe_w1[:], a["moe_w1"]), (moe_w2[:], a["moe_w2"]),
                 (moe_b2[:], a["moe_b2"]), (ffn_w1[:], a["ffn_w1"]), (ffn_w2[:], a["ffn_w2"]),
                 (slot_mask[:], a["slot_mask"]), (expert_id[:], a["expert_id"]), (pick_seq[:], a["pick_seq"])]
        weights_in = 16 * len(loads)
        fills = [(ident[:], 0.0), (ident_bf[:], 0.0), (mask_q[:], 0.0), (mask_k[:], 0.0),
                 (ctx_tok[:, :, D:], 1.0), (v0[:, :, 4:], 1.0), (h[:, :, 4:], 1.0), (cross_hat[:, :, D:], 1.0),
                 (k_nat[:, 3, :], MAX_SCALE), (q_nat[:, 3, :], 0.0), (v_pad[:], 0.0), (smax[:], 0.0),
                 (ln_eps[:], LN_EPS), (minus_half[:], -0.5)]
        selects = 4
        filled = len(fills) + 1

        block = ctx.enter_context(nc.Block())

        def seq_keys(b, nk):
            return slice(b * nk, (b + 1) * nk)

        def seq_tok(b):
            return slice(b * T, (b + 1) * T)

        def head_at(u, jj, i):
            j = 2 * (u % 2) + jj
            return j, SLOTS * j + i

        @block.sync
        def _(sp):
            sp.dma_start(x_tok[:], a["x"][0].rearrange("b t d -> t b d")).then_inc(S["x_in"], 16)
            sp.dma_start(ctx_tok[:, :, 0:D], a["ctx"][0].rearrange("b t d -> t b d")).then_inc(S["ctx_in"], 16)
            for dst, src in loads:
                sp.dma_start(dst, src).then_inc(s_weights, 16)

            def attention(it, m):
                nk = KEYS[m]
                sp.wait_ge(S["k_split"], at(it, "k_split", 2 * (m + 1)))
                for j in range(TILES):
                    sp.dma_start(k_int[:, j, 0:GROUP * nk],
                                 k_nat[32 * j:32 * j + 32, :, 0:GROUP * nk]).then_inc(S["k_shift"], 16)
                sp.wait_ge(S["q_split"], at(it, "q_split", 2 * (m + 1)))
                for j in range(TILES):
                    sp.dma_start(q_int[:, j, :], q_nat[32 * j:32 * j + 32, :, :]).then_inc(S["q_shift"], 16)
                sp.wait_ge(S["m_sb"], at(it, "m_sb", m + 1))
                for j in range(TILES):
                    sp.dma_start(q_int[3::4, j, :], m_nat[32 * j:32 * j + 32, :]).then_inc(S["m_shift"], 16)

            sp.sem_inc(S["out_stored"], START["out_stored"])
            with sp.Fori(0, steps) as it:
                attention(it, SELF2)
                sp.wait_ge(S["kv"], at(it, "kv", 1))
                sp.wait_ge(S["ln_hat"], at(it, "ln_hat", LN_CAQ + 1))
                sp.sem_inc(s_held, 1)
                sp.dma_start(x_tok[:], a["x"][it + 1].rearrange("b t d -> t b d")).then_inc(S["x_in"], 16)
                sp.dma_start(ctx_tok[:, :, 0:D],
                             a["ctx"][it + 1].rearrange("b t d -> t b d")).then_inc(S["ctx_in"], 16)
                attention(it, CROSS2)
                attention(it, SELF3)
                attention(it, CROSS3)
                sp.wait_ge(S["out_ready"], at(it, "out_ready", 1))
                sp.dma_start(out[it].rearrange("b t d -> t b d"), out_tok[:]).then_inc(S["out_stored"], 16)
            sp.wait_ge(S["out_stored"], START["out_stored"] + 16 * steps)
            sp.wait_ge(S["x_in"], 16 * (steps + 1))
            sp.wait_ge(S["ctx_in"], 16 * (steps + 1))

        @block.gpsimd
        def _(pool):
            for ap, value in fills:
                pool.memset(ap, value).then_inc(s_fill, 1)
            pool.wait_ge(s_fill, len(fills))
            pool.memset(v_pad[:, :, :, DH:DH + 1], 1.0).then_inc(s_fill, 1)
            for m in (ident, ident_bf):
                pool.affine_select(out=m[:], in_=m[:], compare_op=ALU.not_equal, fill=1.0, base=0,
                                   pattern=[[-1, P]], channel_multiplier=1).then_inc(s_select, 1)
            pool.affine_select(out=mask_q[:], in_=mask_q[:], compare_op=ALU.is_ge, fill=MASKED, base=0,
                               pattern=[[0, SLOTS], [-1, T]], channel_multiplier=1).then_inc(s_select, 1)
            pool.affine_select(out=mask_k[:], in_=mask_k[:], compare_op=ALU.is_ge, fill=MASKED, base=0,
                               pattern=[[0, SLOTS], [1, T]], channel_multiplier=-1).then_inc(s_select, 1)
            pool.wait_ge(s_weights, weights_in)
            pool.wait_ge(s_const, 6)

            def shifted(t):
                return t[:].unsqueeze(1).broadcast_to([P, GROUP, D])

            def root(it, n, p=P):
                pool.wait_ge(S["ln_mean"], at(it, "ln_mean", GROUP * (n + 1)))
                pool.tensor_tensor(var_eps[0:p, :], mean_var[0:p, :, 1], ln_eps[0:p, :], ALU.add)\
                    .then_inc(S["ln_var"], 1)
                pool.wait_ge(S["ln_var"], at(it, "ln_var", n + 1))
                pool.tensor_tensor(rstd[0:p, :], var_eps[0:p, :], minus_half[0:p, :], ALU.pow)\
                    .then_inc(S["ln_rstd"], 1)

            pool.sem_inc(S["out_ready"], START["out_ready"])
            with pool.Fori(0, steps) as it:
                root(it, LN_CTX, C)
                root(it, LN_X)
                pool.wait_ge(S["ln_hat"], at(it, "ln_hat", LN_X + 1))
                pool.tensor_tensor(x_scaled[:], hat[:], row("norm2_w"), ALU.mult).then_inc(S["x_scaled"], 1)
                pool.wait_ge(S["x_scaled"], at(it, "x_scaled", 1))
                pool.tensor_tensor(x_affine[:], x_scaled[:], shifted(x_shift), ALU.add).then_inc(S["x_affine"], 1)
                pool.wait_ge(S["x_affine"], at(it, "x_affine", 1))
                root(it, LN_CROSS)
                pool.wait_ge(S["cross_g"], at(it, "cross_g", 1))
                pool.tensor_tensor(skip[:], x_affine[:], cross_g[:], ALU.add).then_inc(S["skip"], 1)
                root(it, LN_L1)
                pool.wait_ge(S["x2"], at(it, "x2", 1))
                root(it, LN_SA)
                pool.tensor_tensor(residual[:], x_res[:], row("sa_out_b"), ALU.add).then_inc(S["residual"], 1)
                pool.wait_ge(S["attn_sum"], at(it, "attn_sum", SELF2 + 1))
                root(it, LN_CAQ)
                pool.tensor_tensor(residual[:], x_res[:], row("ca_out_b"), ALU.add).then_inc(S["residual"], 1)
                root(it, LN_MOE)
                pool.wait_ge(S["moe_acc"], at(it, "moe_acc", EXPERTS + 1))
                pool.tensor_tensor(residual[:], x_res[:], row("bo_s"), ALU.add).then_inc(S["residual"], 1)
                for n, (ln, scale, shift) in enumerate(((LN_31, "g1", shift31), (LN_32, "g2", shift32))):
                    root(it, ln)
                    pool.wait_ge(S["ln_hat"], at(it, "ln_hat", ln + 1))
                    pool.tensor_tensor(res_scaled[:], hat[:], row(scale), ALU.mult).then_inc(S["res_scaled"], 1)
                    pool.wait_ge(S["res_scaled"], at(it, "res_scaled", n + 1))
                    pool.tensor_tensor(residual[:], res_scaled[:], shifted(shift), ALU.add)\
                        .then_inc(S["residual"], 1)
                root(it, LN_33)
                pool.wait_ge(S["ln_hat"], at(it, "ln_hat", LN_33 + 1))
                pool.tensor_tensor(out_scaled[:], out_hat[:], row("g3"), ALU.mult).then_inc(S["res_scaled"], 1)
                pool.wait_ge(S["res_scaled"], at(it, "res_scaled", 3))
                pool.wait_ge(S["out_stored"], at(it, "out_stored", 0))
                pool.tensor_tensor(out_tok[:], out_scaled[:], row("be3"), ALU.add).then_inc(S["out_ready"], 1)

        @block.scalar
        def _(act):
            act.wait_ge(s_weights, weights_in)
            act.wait_ge(s_fill, filled)

            def affine(it, t, scale, shift):
                act.wait_ge(S["turned"], at(it, "turned", t + 1))
                act.activation(feat[:], bank[4][:], ACT.Identity, bias=col(shift), scale=col(scale))\
                    .then_inc(S["feat"], 1)

            def attention(it, m):
                nk = KEYS[m]
                act.wait_ge(S["k_proj"], at(it, "k_proj", m + 1))
                act.activation(k_nat[:, 0, 0:GROUP * nk], bank[6][:, 0:GROUP * nk], ACT.Identity,
                               bias=col(f"bk{m}")).then_inc(S["k_hi"], 1)
                act.wait_ge(S["q_proj"], at(it, "q_proj", m + 1))
                act.activation(q_nat[:, 0, :], bank[5][:], ACT.Identity, bias=col(f"bq{m}")).then_inc(S["q_hi"], 1)
                act.wait_ge(S["v_proj"], at(it, "v_proj", m + 1))
                act.activation(v_pad[0:nk, :, :, 0:DH],
                               bank[7][0:nk, :].rearrange("k (b h d) -> k b h d", b=GROUP, h=HEADS),
                               ACT.Copy).then_inc(S["v_sb"], 1)
                act.wait_ge(S["m_t"], at(it, "m_t", m + 1))
                act.activation(m_nat[:], bank[6][:], ACT.Copy, scale=1.0 / MAX_SCALE).then_inc(S["m_sb"], 1)

                def copy_out(b):
                    act.wait_ge(S["pv"], at(it, "pv", m * UNITS + 2 * b + 2))
                    act.activation(o_sb[b % 2][:], bank[4 + b % 2][:], ACT.Copy).then_inc(S["o_sb"], 1)

                for u in range(UNITS):
                    act.wait_ge(S["scores_t"], at(it, "scores_t", m * UNITS + u + 1))
                    if u >= 2:
                        act.wait_ge(S["pv"], at(it, "pv", m * UNITS + u - 1))
                    act.activation(probs[u % 2][0:nk], score_ps[u % 2][0:nk], ACT.Exp, scale=DH ** -0.5)\
                        .then_inc(S["probs"], 1)
                    if u % 2 == 0 and u >= 2:
                        copy_out(u // 2 - 1)
                copy_out(GROUP - 1)
                act.wait_ge(S["on_t"], at(it, "on_t", m + 1))
                act.activation(on_f[:], bank[4][:], ACT.Identity, bias=col(f"bv{m}")).then_inc(S["on_sb"], 1)

            with act.Fori(0, steps) as it:
                act.wait_ge(S["ctx_min"], at(it, "ctx_min", 1))
                act.activation(ctx_pow[:], ctx_neg[:], ACT.Exp).then_inc(S["ctx_exp"], 1)
                act.wait_ge(S["turned"], at(it, "turned", T_CTX + 1))
                act.activation(norm1_f[:], bank[4][:, 0:GROUP * C], ACT.Identity, bias=col("norm1_b"),
                               scale=col("norm1_w"))
                act.activation(cakv_f[:], bank[4][:, 0:GROUP * C], ACT.Identity, bias=col("cakv_b"),
                               scale=col("cakv_g")).then_inc(S["feat"], 1)
                act.wait_ge(S["turned"], at(it, "turned", T_RAW + 1))
                act.activation(ctx_f[:], bank[5][:, 0:GROUP * C], ACT.Copy).then_inc(S["feat"], 1)
                act.wait_ge(S["v0"], at(it, "v0", 1))
                act.activation(v0[:, :, 0:4], bank[6][0:C, 0:4 * GROUP].rearrange("k (b f) -> k b f", b=GROUP),
                               ACT.Copy).then_inc(S["v0_sb"], 1)
                affine(it, T_X, "norm2_w", "norm2_b")
                act.wait_ge(S["kv"], at(it, "kv", 1))
                act.activation(kv[:].rearrange("d (s b) e -> d s (b e)", s=2), score_ps[0][:, :, 0:2 * (D + 1)],
                               ACT.Copy).then_inc(S["kv_sb"], 1)
                act.wait_ge(S["max0_t"], at(it, "max0_t", 1))
                act.activation(max0_t[:], bank[5][0:GROUP, 0:P], ACT.Copy).then_inc(S["max0_sb"], 1)
                act.wait_ge(S["s0_t"], at(it, "s0_t", 1))
                act.activation(p0[:], low[2][0:C, :], ACT.Exp, scale=D ** -0.5).then_inc(S["p0"], 1)
                act.wait_ge(S["h_in"], at(it, "h_in", 1))
                act.activation(h[:, :, 0:4], h_in[:], ACT.Gelu).then_inc(S["h"], 1)
                act.wait_ge(S["h_t"], at(it, "h_t", 1))
                act.activation(h_t[:], bank[6][0:5, :], ACT.Copy).then_inc(S["h_t_sb"], 1)
                affine(it, T_CROSS, "norm3_w", "norm3_b")
                act.wait_ge(S["max1_t"], at(it, "max1_t", 1))
                act.activation(max1_t[:], bank[6][0:GROUP, 0:P], ACT.Copy).then_inc(S["max1_sb"], 1)
                act.wait_ge(S["s1_t"], at(it, "s1_t", 1))
                act.activation(p1[:], low[2], ACT.Exp, scale=D ** -0.5).then_inc(S["p1"], 1)
                act.wait_ge(S["x1_min"], at(it, "x1_min", 1))
                act.activation(x1_pow[:], x1_neg[:], ACT.Exp).then_inc(S["x1_exp"], 1)
                affine(it, T_SA, "sa_g", "sa_b")
                attention(it, SELF2)
                affine(it, T_CAQ, "caq_g", "caq_b")
                attention(it, CROSS2)
                affine(it, T_MOE, "moe_g", "moe_b")
                act.wait_ge(S["gap"], at(it, "gap", 1))
                act.activation(gap_exp[:], gap[:], ACT.Exp).then_inc(S["gap_exp"], 1)
                for e in range(EXPERTS):
                    if e == 1:
                        act.wait_ge(S["gates_t"], at(it, "gates_t", 1))
                        act.activation(gates_t[:], bank[6][0:EXPERTS, :], ACT.Copy).then_inc(S["gates_sb"], 1)
                    if e >= 2:
                        act.wait_ge(S["fc2"], at(it, "fc2", e - 1))
                    for c in range(CHUNKS):
                        act.wait_ge(S["fc1"], at(it, "fc1", CHUNKS * e + c + 1))
                        act.activation(hidden[e % 2][:, c, :], low[c], ACT.Gelu, bias=col(f"moe_b1_{e}_{c}"))\
                            .then_inc(S["gelu"], 1)
                act.wait_ge(S["turned"], at(it, "turned", T_L3 + 1))
                act.activation(feat[:], bank[4][:], ACT.Copy).then_inc(S["feat"], 1)
                attention(it, SELF3)
                affine(it, T_31, "g1", "be1")
                attention(it, CROSS3)
                affine(it, T_32, "g2", "be2")
                for c in range(CHUNKS):
                    act.wait_ge(S["ffn1"], at(it, "ffn1", c + 1))
                    act.activation(hidden[0][:, c, :], low[c], ACT.Relu, bias=col(f"ffn_b1_{c}"))\
                        .then_inc(S["ffn_relu"], 1)

        @block.vector
        def _(dve):
            dve.wait_ge(s_weights, weights_in)
            dve.wait_ge(s_fill, filled)
            r = {n: rows[:, i, :] for i, n in enumerate(ROWS)}
            dve.tensor_tensor(self_scale[:], r["gamma1"], r["gamma2"], ALU.mult).then_inc(s_const, 1)
            dve.wait_ge(s_const, 1)
            dve.tensor_tensor(x_shift[:], self_scale[:], r["norm3_b"], ALU.mult).then_inc(s_const, 1)
            dve.wait_ge(s_const, 2)
            dve.tensor_tensor(x_shift[:], x_shift[:], r["norm2_b"], ALU.add).then_inc(s_const, 1)
            dve.tensor_tensor(self_scale[:], self_scale[:], r["norm3_w"], ALU.mult).then_inc(s_const, 1)
            dve.tensor_tensor(shift31[:], r["be1"], r["bo_c"], ALU.add).then_inc(s_const, 1)
            dve.tensor_tensor(shift32[:], r["be2"], r["ffn_b2"], ALU.add).then_inc(s_const, 1)
            dve.wait_ge(s_const, 6)

            def normalise(it, n, src, dst, p=P):
                for b in range(GROUP):
                    dve.bn_stats(stats[0:p, b, :], src(b)).then_inc(S["ln_stats"], 1)
                dve.wait_ge(S["ln_stats"], at(it, "ln_stats", GROUP * (n + 1)))
                dve.sem_inc(s_held, 1)
                for b in range(GROUP):
                    dve.bn_aggr(mean_var[0:p, b, :], stats[0:p, b, :]).then_inc(S["ln_mean"], 1)
                dve.wait_ge(S["ln_rstd"], at(it, "ln_rstd", n + 1))
                for b in range(GROUP):
                    last = dve.tensor_scalar(dst(b), src(b), mean_var[0:p, b, 0:1], rstd[0:p, b:b + 1],
                                             ALU.subtract, ALU.mult)
                last.then_inc(S["ln_hat"], 1)

            def hat_of(b):
                return hat[:, b, :]

            def attention(it, m):
                nk = KEYS[m]
                keys = GROUP * nk
                dve.wait_ge(S["k_hi"], at(it, "k_hi", m + 1))
                dve.scalar_tensor_tensor(k_nat[:, 1, 0:keys], bank[6][:, 0:keys], col(f"bk{m}"),
                                         k_nat[:, 0, 0:keys], ALU.add, ALU.subtract).then_inc(S["k_split"], 1)
                dve.tensor_copy(k_nat[:, 2, 0:keys], k_nat[:, 0, 0:keys]).then_inc(S["k_split"], 1)
                dve.wait_ge(S["q_hi"], at(it, "q_hi", m + 1))
                dve.scalar_tensor_tensor(q_nat[:, 2, :], bank[5][:], col(f"bq{m}"), q_nat[:, 0, :],
                                         ALU.add, ALU.subtract).then_inc(S["q_split"], 1)
                dve.tensor_copy(q_nat[:, 1, :], q_nat[:, 0, :]).then_inc(S["q_split"], 1)
                dve.wait_ge(S["k_shift"], at(it, "k_shift", 64 * (m + 1)))
                for i in range(SLOTS):
                    dve.tensor_scalar(k_blk[:, :, i, 0:keys], k_int[:, :, 0:keys], slot_mask[:, i:i + 1], None,
                                      ALU.mult).then_inc(S["k_blk"], 1)
                for u in range(UNITS):
                    b, hf = divmod(u, 2)
                    dve.wait_ge(S["scores"], at(it, "scores", m * UNITS + u + 1))
                    dve.tensor_reduce(
                        smax[:, b, 64 * hf:64 * hf + 64:DH],
                        score_ps[u % 2][:, :, 0:SLOTS * nk].rearrange("q j (i k) -> q j i k", i=SLOTS),
                        AX.X, ALU.max, negate=True).then_inc(S["smax"], 1)
                for b in range(GROUP):
                    n = GROUP * m + b
                    o_t = bank[6 + b % 2][:].rearrange("q (h r) -> q h r", r=VW)
                    dve.wait_ge(S["o_t"], at(it, "o_t", n + 1))
                    dve.reciprocal(o_rden[:, b, :], o_t[:, :, DH]).then_inc(S["o_rden"], 1)
                    dve.wait_ge(S["o_rden"], at(it, "o_rden", n + 1))
                    dve.tensor_tensor(o_norm[:, b, :].rearrange("q (h d) -> q h d", d=DH), o_t[:, :, 0:DH],
                                      o_rden[:, b, :].unsqueeze(2).broadcast_to([P, HEADS, DH]),
                                      ALU.mult).then_inc(S["o_norm"], 1)
                dve.wait_ge(S["attn"], at(it, "attn", m + 1))
                dve.wait_ge(S["residual"], at(it, "residual", m + 1))
                dve.tensor_tensor(x_res[:], bank[5][:].rearrange("q (b d) -> q b d", b=GROUP), residual[:], ALU.add)\
                    .then_inc(S["attn_sum"], 1)
                dve.wait_ge(S["attn_sum"], at(it, "attn_sum", m + 1))

            dve.sem_inc(S["ffn_sum"], START["ffn_sum"])
            with dve.Fori(0, steps) as it:
                dve.wait_ge(S["ctx_in"], at(it, "ctx_in", 16))
                dve.tensor_scalar(ctx_neg[:], ctx_tok[:, :, 0:D], 0.0, None, ALU.min).then_inc(S["ctx_min"], 1)
                normalise(it, LN_CTX, lambda b: ctx_tok[:, b, 0:D], lambda b: ctx_hat[:, b, :], C)
                dve.wait_ge(S["x_in"], at(it, "x_in", 16))
                normalise(it, LN_X, lambda b: x_tok[:, b, :], hat_of)
                dve.wait_ge(S["ctx_exp"], at(it, "ctx_exp", 1))
                dve.scalar_tensor_tensor(ctx_phi[:], ctx_pow[:], -1.0, ctx_tok[:, :, 0:D], ALU.add, ALU.max)\
                    .then_inc(S["ctx_phi"], 1)
                dve.wait_ge(S["s0"], at(it, "s0", 1))
                dve.tensor_reduce(max0[:], bank[7][:, 0:GROUP * C].rearrange("q (b k) -> q b k", b=GROUP),
                                  AX.X, ALU.max, negate=True).then_inc(S["max0"], 1)
                dve.wait_ge(S["hpre"], at(it, "hpre", 1))
                hpre = low[3][:, 0:5 * GROUP].rearrange("q (b f) -> q b f", b=GROUP)
                dve.reciprocal(h_rden[:], hpre[:, :, 4]).then_inc(S["h_rden"], 1)
                dve.wait_ge(S["h_rden"], at(it, "h_rden", 1))
                dve.tensor_tensor(h_mul[:], hpre[:, :, 0:4], h_rden[:].unsqueeze(2).broadcast_to([P, GROUP, 4]),
                                  ALU.mult).then_inc(S["h_mul"], 1)
                dve.wait_ge(S["h_mul"], at(it, "h_mul", 1))
                dve.tensor_tensor(h_in[:], h_mul[:], fc1_b[:].unsqueeze(1).broadcast_to([P, GROUP, 4]), ALU.add)\
                    .then_inc(S["h_in"], 1)
                dve.wait_ge(S["cross"], at(it, "cross", 1))
                cross = bank[7][:].rearrange("q (b d) -> q b d", b=GROUP)
                normalise(it, LN_CROSS, lambda b: cross[:, b, :], lambda b: cross_hat[:, b, 0:D])
                dve.tensor_tensor(cross_g[:], cross, row("gamma2"), ALU.mult).then_inc(S["cross_g"], 1)
                dve.wait_ge(S["s1"], at(it, "s1", 1))
                dve.tensor_reduce(max1[:], bank[5][:].rearrange("q (b k) -> q b k", b=GROUP),
                                  AX.X, ALU.max, negate=True).then_inc(S["max1"], 1)
                dve.wait_ge(S["pv1"], at(it, "pv1", 1))
                pv1 = [score_ps[0][:, b // 2, (D + 1) * (b % 2):(D + 1) * (b % 2 + 1)] for b in range(GROUP)]
                for s in range(2):
                    dve.reciprocal(pv1_rden[:, 2 * s:2 * s + 2], score_ps[0][:, s, D:2 * (D + 1):D + 1])\
                        .then_inc(S["pv1_rden"], 1)
                dve.wait_ge(S["pv1_rden"], at(it, "pv1_rden", 2))
                for b in range(GROUP):
                    last = dve.scalar_tensor_tensor(pv1_n[:, b, :], pv1[b][:, 0:D], pv1_rden[:, b:b + 1],
                                                    self_scale[:], ALU.mult, ALU.mult)
                last.then_inc(S["pv1_n"], 1)
                dve.wait_ge(S["pv1_n"], at(it, "pv1_n", 1))
                dve.wait_ge(S["skip"], at(it, "skip", 1))
                dve.tensor_tensor(x1[:], pv1_n[:], skip[:], ALU.add).then_inc(S["x1"], 1)
                dve.wait_ge(S["turned"], at(it, "turned", T_L1 + 1))
                dve.tensor_scalar(x1_neg[:], bank[4][:], 0.0, None, ALU.min).then_inc(S["x1_min"], 1)
                dve.wait_ge(S["x1_exp"], at(it, "x1_exp", 1))
                dve.scalar_tensor_tensor(x1_phi[:], x1_pow[:], -1.0, bank[4][:], ALU.add, ALU.max)\
                    .then_inc(S["x1_phi"], 1)
                dve.wait_ge(S["num"], at(it, "num", 1))
                num = [score_ps[1][:, b // 2, (D + 1) * (b % 2):(D + 1) * (b % 2 + 1)] for b in range(GROUP)]
                for s in range(2):
                    dve.tensor_scalar(num_den[:, 2 * s:2 * s + 2], score_ps[1][:, s, D:2 * (D + 1):D + 1], ATTN_EPS,
                                      None, ALU.add).then_inc(S["num_den"], 1)
                dve.wait_ge(S["num_den"], at(it, "num_den", 2))
                dve.reciprocal(num_rden[:], num_den[:]).then_inc(S["num_rden"], 2)
                dve.wait_ge(S["num_rden"], at(it, "num_rden", 2))
                for b in range(GROUP):
                    last = dve.scalar_tensor_tensor(l1_sum[:, b, :], num[b][:, 0:D], num_rden[:, b:b + 1], x1[:, b, :],
                                                    ALU.mult, ALU.add)
                last.then_inc(S["l1_sum"], 1)
                dve.wait_ge(S["l1_sum"], at(it, "l1_sum", 1))
                normalise(it, LN_L1, lambda b: l1_sum[:, b, :], hat_of)
                dve.wait_ge(S["ln_hat"], at(it, "ln_hat", LN_L1 + 1))
                dve.tensor_tensor(l1_scaled[:], hat[:], row("l1_gamma"), ALU.mult).then_inc(S["l1_scaled"], 1)
                dve.wait_ge(S["l1_scaled"], at(it, "l1_scaled", 1))
                dve.tensor_tensor(x_res[:], l1_scaled[:], row("l1_beta"), ALU.add).then_inc(S["x2"], 1)
                dve.wait_ge(S["x2"], at(it, "x2", 1))
                normalise(it, LN_SA, lambda b: x_res[:, b, :], hat_of)
                attention(it, SELF2)
                normalise(it, LN_CAQ, lambda b: x_res[:, b, :], hat_of)
                attention(it, CROSS2)
                normalise(it, LN_MOE, lambda b: x_res[:, b, :], hat_of)
                dve.wait_ge(S["router"], at(it, "router", 1))
                dve.tensor_tensor(logits[:], bank[5][:, 0:GROUP * EXPERTS].rearrange("q (b e) -> q b e", b=GROUP),
                                  router_b[:].unsqueeze(1).broadcast_to([P, GROUP, EXPERTS]), ALU.add)\
                    .then_inc(S["logits"], 1)
                dve.wait_ge(S["logits"], at(it, "logits", 1))
                dve.sem_inc(s_held, 1)
                for b in range(GROUP):
                    dve.max(top[:, b, :], logits[:, b, :]).then_inc(S["top"], 1)
                dve.wait_ge(S["top"], at(it, "top", GROUP))
                dve.sem_inc(s_held, 1)
                for b in range(GROUP):
                    dve.max_index(top_at[:, b, :], top[:, b, :], logits[:, b, :]).then_inc(S["top_at"], 1)
                dve.tensor_tensor(gap[:], top[:, :, 1], top[:, :, 0], ALU.subtract).then_inc(S["gap"], 1)
                dve.wait_ge(S["top_at"], at(it, "top_at", GROUP))
                dve.tensor_copy(top_f[:], top_at[:]).then_inc(S["top_f"], 1)
                dve.wait_ge(S["gap_exp"], at(it, "gap_exp", 1))
                dve.tensor_scalar(gap_den[:], gap_exp[:], 1.0, None, ALU.add).then_inc(S["gap_den"], 1)
                dve.wait_ge(S["gap_den"], at(it, "gap_den", 1))
                dve.reciprocal(gate1[:], gap_den[:]).then_inc(S["gate1"], 1)
                dve.wait_ge(S["gate1"], at(it, "gate1", 1))
                dve.tensor_tensor(gate2[:], gap_exp[:], gate1[:], ALU.mult).then_inc(S["gate2"], 1)
                dve.wait_ge(S["top_f"], at(it, "top_f", 1))
                experts = expert_id[:].unsqueeze(1).broadcast_to([P, GROUP, EXPERTS])

                def each(ap):
                    return ap.unsqueeze(2).broadcast_to([P, GROUP, EXPERTS])

                dve.tensor_tensor(hot1[:], experts, each(top_f[:, :, 0]), ALU.is_equal).then_inc(S["hot1"], 1)
                dve.tensor_tensor(hot2[:], experts, each(top_f[:, :, 1]), ALU.is_equal).then_inc(S["hot2"], 1)
                dve.wait_ge(S["hot1"], at(it, "hot1", 1))
                dve.tensor_tensor(pick1[:], hot1[:], each(gate1[:]), ALU.mult).then_inc(S["pick1"], 1)
                dve.wait_ge(S["hot2"], at(it, "hot2", 1))
                dve.wait_ge(S["gate2"], at(it, "gate2", 1))
                dve.tensor_tensor(pick2[:], hot2[:], each(gate2[:]), ALU.mult).then_inc(S["pick2"], 1)
                dve.wait_ge(S["pick1"], at(it, "pick1", 1))
                dve.wait_ge(S["pick2"], at(it, "pick2", 1))
                dve.tensor_tensor(gates[:], pick1[:], pick2[:], ALU.add).then_inc(S["gates"], 1)
                dve.wait_ge(S["gate_bias"], at(it, "gate_bias", 1))
                dve.tensor_tensor(x_res[:], bank[7][:].rearrange("q (b d) -> q b d", b=GROUP), x_res[:], ALU.add)\
                    .then_inc(S["moe_acc"], 1)
                for e in range(EXPERTS):
                    dve.wait_ge(S["fc2"], at(it, "fc2", e + 1))
                    dve.wait_ge(S["moe_acc"], at(it, "moe_acc", e + 1))
                    for b in range(GROUP):
                        last = dve.scalar_tensor_tensor(x_res[:, b, :], bank[6 + e % 2][:, seq_tok(b)],
                                                        gates[:, b, e:e + 1], x_res[:, b, :], ALU.mult, ALU.add)
                    last.then_inc(S["moe_acc"], 1)
                attention(it, SELF3)
                normalise(it, LN_31, lambda b: x_res[:, b, :], hat_of)
                attention(it, CROSS3)
                normalise(it, LN_32, lambda b: x_res[:, b, :], hat_of)
                dve.wait_ge(S["ffn2"], at(it, "ffn2", 1))
                dve.wait_ge(S["residual"], at(it, "residual", 5))
                dve.tensor_tensor(x_res[:], bank[5][:].rearrange("q (b d) -> q b d", b=GROUP), residual[:], ALU.add)\
                    .then_inc(S["ffn_sum"], 1)
                dve.wait_ge(S["ffn_sum"], at(it, "ffn_sum", 1))
                dve.wait_ge(S["out_ready"], at(it, "out_ready", 0))
                normalise(it, LN_33, lambda b: x_res[:, b, :], lambda b: out_hat[:, b, :])

        @block.tensor
        def _(pe):
            pe.wait_ge(s_weights, weights_in)
            pe.wait_ge(s_fill, filled)
            pe.wait_ge(s_select, selects)

            def turn(dst, src, n=P, width=P):
                for b in range(GROUP):
                    last = pe.transpose(dst[0:width, b * n:(b + 1) * n], src(b), ident[0:n, 0:n])
                return last

            def turn_hat(it, ln):
                pe.wait_ge(S["ln_hat"], at(it, "ln_hat", ln + 1))
                turn(bank[4], lambda b: hat[:, b, :]).then_inc(S["turned"], 1)

            def attention(it, m, q_src, k_src, t):
                nk = KEYS[m]
                keys = GROUP * nk
                pe.wait_ge(S["feat"], at(it, "feat", t + 1))
                pe.matmul(bank[6][:, 0:keys], mat(f"wk{m}"), k_src, start=True, stop=True).then_inc(S["k_proj"], 1)
                pe.matmul(bank[5][:], mat(f"wq{m}"), q_src, start=True, stop=True).then_inc(S["q_proj"], 1)
                for b in range(GROUP):
                    last = pe.matmul(bank[7][0:nk, b * D:(b + 1) * D], k_src[:, seq_keys(b, nk)], mat(f"wv{m}"),
                                     start=True, stop=True)
                last.then_inc(S["v_proj"], 1)

                pe.wait_ge(S["q_shift"], at(it, "q_shift", 64 * (m + 1)))
                pe.wait_ge(S["k_blk"], at(it, "k_blk", SLOTS * (m + 1)))
                for u in range(UNITS):
                    b = u // 2
                    if u >= 2:
                        pe.wait_ge(S["smax"], at(it, "smax", m * UNITS + u - 1))
                    for jj in range(2):
                        j, _ = head_at(u, jj, 0)
                        dst = score_ps[u % 2][:, jj, 0:SLOTS * nk]
                        if CAUSAL[m]:
                            pe.matmul(dst, ident_bf[:], mask_q[:].rearrange("q i k -> q (i k)"),
                                      start=True, stop=False)
                        last = pe.matmul(dst, q_int[:, j, seq_tok(b)], k_blk[:, j, :, seq_keys(b, nk)],
                                         start=not CAUSAL[m], stop=True)
                    last.then_inc(S["scores"], 1)
                pe.wait_ge(S["smax"], at(it, "smax", (m + 1) * UNITS))
                turn(bank[6], lambda b: smax[:, b, :]).then_inc(S["m_t"], 1)

                def scores_t(u):
                    b = u // 2
                    if u >= 2:
                        pe.wait_ge(S["probs"], at(it, "probs", m * UNITS + u - 1))
                    for jj in range(2):
                        if CAUSAL[m]:
                            pe.matmul(score_ps[u % 2][0:nk, jj, :], ident_bf[:],
                                      mask_k[:].rearrange("k i q -> k (i q)"), start=True, stop=True)
                        for i in range(SLOTS):
                            j, _ = head_at(u, jj, i)
                            last = pe.matmul(score_ps[u % 2][0:nk, jj, i * T:(i + 1) * T],
                                             k_blk[:, j, i, seq_keys(b, nk)], q_int[:, j, seq_tok(b)],
                                             start=not CAUSAL[m], stop=True, skip_group_check=True)
                    last.then_inc(S["scores_t"], 1)

                def weigh(u):
                    b = u // 2
                    pe.wait_ge(S["probs"], at(it, "probs", m * UNITS + u + 1))
                    if u % 2 == 0 and b >= 2:
                        pe.wait_ge(S["o_sb"], at(it, "o_sb", GROUP * m + b - 1))
                    for jj in range(2):
                        for i in range(SLOTS):
                            j, head = head_at(u, jj, i)
                            last = pe.matmul(bank[4 + b % 2][VW * i:VW * i + VW, j * T:(j + 1) * T],
                                             v_pad[0:nk, b, head, :], probs[u % 2][0:nk, jj, i * T:(i + 1) * T],
                                             start=True, stop=True)
                    last.then_inc(S["pv"], 1)

                def turn_out(b):
                    pe.wait_ge(S["o_sb"], at(it, "o_sb", GROUP * m + b + 1))
                    if b >= 2:
                        pe.wait_ge(S["o_norm"], at(it, "o_norm", GROUP * m + b - 1))
                    for j in range(TILES):
                        last = pe.transpose(bank[6 + b % 2][:, j * P:(j + 1) * P], o_sb[b % 2][:, j * T:(j + 1) * T],
                                            ident[:])
                    last.then_inc(S["o_t"], 1)

                pe.wait_ge(S["m_shift"], at(it, "m_shift", 64 * (m + 1)))
                pe.wait_ge(S["v_sb"], at(it, "v_sb", m + 1))
                scores_t(0)
                for u in range(UNITS):
                    if u + 1 < UNITS:
                        scores_t(u + 1)
                    weigh(u)
                    if u % 2 == 1 and u >= 3:
                        turn_out(u // 2 - 1)
                turn_out(GROUP - 1)
                pe.wait_ge(S["o_norm"], at(it, "o_norm", GROUP * (m + 1)))
                turn(bank[4], lambda b: o_norm[:, b, :]).then_inc(S["on_t"], 1)
                pe.wait_ge(S["on_sb"], at(it, "on_sb", m + 1))
                for b in range(GROUP):
                    last = pe.matmul(bank[5][:, b * D:(b + 1) * D], on_f[:, seq_tok(b)], mat(f"wo{m}"),
                                     start=True, stop=True)
                last.then_inc(S["attn"], 1)

            with pe.Fori(0, steps) as it:
                pe.wait_ge(S["ln_hat"], at(it, "ln_hat", LN_CTX + 1))
                turn(bank[4], lambda b: ctx_hat[:, b, :], C).then_inc(S["turned"], 1)
                pe.wait_ge(S["ffn_sum"], at(it, "ffn_sum", 0))
                turn(bank[5], lambda b: ctx_tok[:, b, 0:D], C).then_inc(S["turned"], 1)
                pe.wait_ge(S["feat"], at(it, "feat", T_CTX + 1))
                for b in range(GROUP):
                    last = pe.matmul(bank[6][0:C, 4 * b:4 * b + 4], norm1_f[:, seq_keys(b, C)], fc1_w[:],
                                     start=True, stop=True)
                last.then_inc(S["v0"], 1)
                turn_hat(it, LN_X)
                pe.wait_ge(S["feat"], at(it, "feat", T_X + 1))
                for b in range(GROUP):
                    last = pe.matmul(bank[7][:, seq_keys(b, C)], feat[:, seq_tok(b)], norm1_f[:, seq_keys(b, C)],
                                     start=True, stop=True)
                last.then_inc(S["s0"], 1)
                pe.wait_ge(S["ctx_phi"], at(it, "ctx_phi", 1))
                for b in range(GROUP):
                    last = pe.matmul(score_ps[0][:, b // 2, (D + 1) * (b % 2):(D + 1) * (b % 2 + 1)],
                                     ctx_phi[:, b, :], ctx_tok[:, b, :], start=True, stop=True)
                last.then_inc(S["kv"], 1)
                pe.wait_ge(S["max0"], at(it, "max0", 1))
                pe.transpose(bank[5][0:GROUP, 0:P], max0[:], ident[:]).then_inc(S["max0_t"], 1)
                pe.wait_ge(S["max0_sb"], at(it, "max0_sb", 1))
                for b in range(GROUP):
                    pe.matmul(low[2][0:C, seq_tok(b)], norm1_f[:, seq_keys(b, C)], feat[:, seq_tok(b)],
                              start=True, stop=False)
                    last = pe.matmul(low[2][0:C, seq_tok(b)], pick_seq[:, b, 0:C], max0_t[:], start=False, stop=True)
                last.then_inc(S["s0_t"], 1)
                pe.wait_ge(S["p0"], at(it, "p0", 1))
                pe.wait_ge(S["v0_sb"], at(it, "v0_sb", 1))
                for b in range(GROUP):
                    last = pe.matmul(low[3][:, 5 * b:5 * b + 5], p0[:, seq_tok(b)], v0[:, b, :],
                                     start=True, stop=True)
                last.then_inc(S["hpre"], 1)
                pe.wait_ge(S["h"], at(it, "h", 1))
                turn(bank[6], lambda b: h[:, b, :], P, 5).then_inc(S["h_t"], 1)
                pe.wait_ge(S["h_t_sb"], at(it, "h_t_sb", 1))
                for b in range(GROUP):
                    last = pe.matmul(bank[7][:, seq_tok(b)], h_t[:, seq_tok(b)], fc2_aug[:], start=True, stop=True)
                last.then_inc(S["cross"], 1)
                pe.wait_ge(S["ln_hat"], at(it, "ln_hat", LN_CROSS + 1))
                turn(bank[4], lambda b: cross_hat[:, b, 0:D]).then_inc(S["turned"], 1)
                pe.wait_ge(S["feat"], at(it, "feat", T_CROSS + 1))
                for b in range(GROUP):
                    last = pe.matmul(bank[5][:, seq_tok(b)], feat[:, seq_tok(b)], feat[:, seq_tok(b)],
                                     start=True, stop=True)
                last.then_inc(S["s1"], 1)
                pe.wait_ge(S["max1"], at(it, "max1", 1))
                pe.transpose(bank[6][0:GROUP, 0:P], max1[:], ident[:]).then_inc(S["max1_t"], 1)
                pe.wait_ge(S["max1_sb"], at(it, "max1_sb", 1))
                for b in range(GROUP):
                    pe.matmul(low[2][:, seq_tok(b)], feat[:, seq_tok(b)], feat[:, seq_tok(b)], start=True, stop=False)
                    last = pe.matmul(low[2][:, seq_tok(b)], pick_seq[:, b, :], max1_t[:], start=False, stop=True)
                last.then_inc(S["s1_t"], 1)
                pe.wait_ge(S["p1"], at(it, "p1", 1))
                pe.wait_ge(S["kv_sb"], at(it, "kv_sb", 1))
                for b in range(GROUP):
                    last = pe.matmul(score_ps[0][:, b // 2, (D + 1) * (b % 2):(D + 1) * (b % 2 + 1)],
                                     p1[:, seq_tok(b)], cross_hat[:, b, :], start=True, stop=True)
                last.then_inc(S["pv1"], 1)
                pe.wait_ge(S["x1"], at(it, "x1", 1))
                turn(bank[4], lambda b: x1[:, b, :]).then_inc(S["turned"], 1)
                pe.wait_ge(S["x1_phi"], at(it, "x1_phi", 1))
                for b in range(GROUP):
                    last = pe.matmul(score_ps[1][:, b // 2, (D + 1) * (b % 2):(D + 1) * (b % 2 + 1)],
                                     x1_phi[:, seq_tok(b)], kv[:, b, :], start=True, stop=True)
                last.then_inc(S["num"], 1)
                turn_hat(it, LN_SA)
                attention(it, SELF2, feat[:], feat[:], T_SA - 1)
                turn_hat(it, LN_CAQ)
                attention(it, CROSS2, feat[:], cakv_f[:], T_CAQ - 1)
                turn_hat(it, LN_MOE)
                pe.wait_ge(S["feat"], at(it, "feat", T_MOE))
                for b in range(GROUP):
                    last = pe.matmul(bank[5][:, EXPERTS * b:EXPERTS * (b + 1)], feat[:, seq_tok(b)], router_w[:],
                                     start=True, stop=True)
                last.then_inc(S["router"], 1)

                def expert_in(e):
                    for c in range(CHUNKS):
                        if e >= 1:
                            pe.wait_ge(S["gelu"], at(it, "gelu", CHUNKS * (e - 1) + c + 1))
                        pe.matmul(low[c], moe_w1[:, e, c, :], feat[:], start=True, stop=True).then_inc(S["fc1"], 1)

                def expert_out(e):
                    pe.wait_ge(S["gelu"], at(it, "gelu", CHUNKS * (e + 1)))
                    pe.wait_ge(S["moe_acc"], at(it, "moe_acc", max(e, 1)))
                    for b in range(GROUP):
                        for c in range(CHUNKS):
                            last = pe.matmul(bank[6 + e % 2][:, seq_tok(b)], hidden[e % 2][:, c, seq_tok(b)],
                                             moe_w2[:, e, c, :], start=(c == 0), stop=(c == CHUNKS - 1))
                    last.then_inc(S["fc2"], 1)

                expert_in(0)
                expert_in(1)
                pe.wait_ge(S["gates"], at(it, "gates", 1))
                turn(bank[6], lambda b: gates[:, b, :], P, EXPERTS).then_inc(S["gates_t"], 1)
                pe.wait_ge(S["gates_sb"], at(it, "gates_sb", 1))
                for b in range(GROUP):
                    last = pe.matmul(bank[7][:, seq_tok(b)], gates_t[:, seq_tok(b)], moe_b2[:], start=True, stop=True)
                last.then_inc(S["gate_bias"], 1)
                for e in range(EXPERTS):
                    if e >= 1 and e + 1 < EXPERTS:
                        expert_in(e + 1)
                    expert_out(e)
                pe.wait_ge(S["moe_acc"], at(it, "moe_acc", EXPERTS + 1))
                turn(bank[4], lambda b: x_res[:, b, :]).then_inc(S["turned"], 1)
                attention(it, SELF3, feat[:], feat[:], T_L3 - 1)
                turn_hat(it, LN_31)
                attention(it, CROSS3, feat[:], ctx_f[:], T_31 - 1)
                turn_hat(it, LN_32)
                pe.wait_ge(S["feat"], at(it, "feat", T_32))
                for c in range(CHUNKS):
                    pe.matmul(low[c], ffn_w1[:, c, :], feat[:], start=True, stop=True).then_inc(S["ffn1"], 1)
                pe.wait_ge(S["ffn_relu"], at(it, "ffn_relu", CHUNKS))
                for b in range(GROUP):
                    for c in range(CHUNKS):
                        last = pe.matmul(bank[5][:, seq_tok(b)], hidden[0][:, c, seq_tok(b)], ffn_w2[:, c, :],
                                         start=(c == 0), stop=(c == CHUNKS - 1))
                last.then_inc(S["ffn2"], 1)


def laid_out(inputs):
    import numpy as np

    def get(name):
        return np.asarray(inputs[name])

    def l0(n):
        return get(f"L0_xattn_{n}")

    def l1(n):
        return get(f"L1_xattn_{n}")

    def l2(n):
        return get(f"L2_xattn_{n}")

    def l3(n):
        return get(f"L3_xattn_{n}")

    f32 = np.float32
    col = {n: l0(n) for n in ("norm1_w", "norm1_b", "norm2_w", "norm2_b", "norm3_w", "norm3_b")}
    col |= {"sa_g": l2("sa_ln_g"), "sa_b": l2("sa_ln_b"), "caq_g": l2("ca_q_ln_g"), "caq_b": l2("ca_q_ln_b"),
            "cakv_g": l2("ca_kv_ln_g"), "cakv_b": l2("ca_kv_ln_b"), "moe_g": l2("moe_ln_g"), "moe_b": l2("moe_ln_b"),
            "g1": l3("g1"), "be1": l3("be1"), "g2": l3("g2"), "be2": l3("be2")}
    mat = {}
    for m, n in ((SELF2, "sa"), (CROSS2, "ca")):
        for k, w in enumerate("qkv"):
            mat[f"w{w}{m}"] = l2(f"{n}_in_w")[k * D:(k + 1) * D].T
            col[f"b{w}{m}"] = l2(f"{n}_in_b")[k * D:(k + 1) * D]
        mat[f"wo{m}"] = l2(f"{n}_out_w").T
    for m, n in ((SELF3, "s"), (CROSS3, "c")):
        for w in "qkv":
            mat[f"w{w}{m}"] = l3(f"W{w}_{n}").transpose(1, 0, 2).reshape(D, D)
            col[f"b{w}{m}"] = l3(f"b{w}_{n}").reshape(D)
        mat[f"wo{m}"] = l3(f"Wo_{n}")
    for c in range(CHUNKS):
        col[f"ffn_b1_{c}"] = l3("b1")[c * P:(c + 1) * P]
        for e in range(EXPERTS):
            col[f"moe_b1_{e}_{c}"] = l2("e_fc1_b")[e, c * P:(c + 1) * P]
    row = {n: l0(n) for n in ("norm2_w", "norm2_b", "gamma1", "gamma2", "norm3_w", "norm3_b")}
    row |= {"l1_gamma": l1("gamma"), "l1_beta": l1("beta"), "sa_out_b": l2("sa_out_b"), "ca_out_b": l2("ca_out_b"),
            "bo_s": l3("bo_s"), "bo_c": l3("bo_c"), "ffn_b2": l3("b2"), "g1": l3("g1"), "be1": l3("be1"),
            "g2": l3("g2"), "be2": l3("be2"), "g3": l3("g3"), "be3": l3("be3")}

    def groups(x):
        x = x.reshape(-1, GROUP, *x.shape[1:])
        return np.concatenate([x, np.zeros_like(x[:1])])

    def repeat(v):
        return np.broadcast_to(v, (P, *v.shape))

    feature = np.arange(P) // PARTS
    arrays = {
        "x": groups(get("x")), "ctx": groups(get("ctx_1024")),
        "cols": np.stack([col[n] for n in COLS], 1),
        "rows": repeat(np.stack([row[n] for n in ROWS])),
        "mats": np.stack([mat[n] for n in MATS], 1),
        "fc1_w": l0("fc1_w").T, "fc1_b": repeat(l0("fc1_b")),
        "fc2_aug": np.concatenate([l0("fc2_w").T, l0("fc2_b")[None]]),
        "router_w": l2("router_w").T, "router_b": repeat(l2("router_b")),
        "moe_w1": l2("e_fc1_w").reshape(EXPERTS, CHUNKS, P, D).transpose(3, 0, 1, 2),
        "moe_w2": l2("e_fc2_w").reshape(EXPERTS, D, CHUNKS, P).transpose(3, 0, 2, 1),
        "moe_b2": l2("e_fc2_b"),
        "ffn_w1": l3("W1").reshape(D, CHUNKS, P),
        "ffn_w2": l3("W2").reshape(CHUNKS, P, D).transpose(1, 0, 2),
        "slot_mask": (feature[:, None] // DH == np.arange(SLOTS)).astype(f32),
        "expert_id": repeat(np.arange(EXPERTS, dtype=f32)),
        "pick_seq": np.repeat(np.eye(GROUP, dtype=f32)[:, :, None], T, 2),
    }
    return {n: np.ascontiguousarray(v) for n, v in arrays.items()}


def kernel(**inputs):
    import concourse.bacc as bacc
    from concourse.bass_utils import run_bass_kernel_spmd
    arrays = laid_out(inputs)
    nc = bacc.Bacc("TRN2", target_bir_lowering=False, num_devices=1)
    aps = {n: nc.dram_tensor(f"in_{n}", v.shape, mybir.dt.from_np(v.dtype), kind="ExternalInput").ap()
           for n, v in arrays.items()}
    steps = arrays["x"].shape[0] - 1
    out = nc.dram_tensor("out", (steps, GROUP, T, D), F32, kind="ExternalOutput").ap()
    build(nc, aps, out, steps)
    r = run_bass_kernel_spmd(nc, [{f"in_{n}": v for n, v in arrays.items()}], core_ids=[0])
    return r.results[0]["out"].reshape(-1, T, D)
```

```python
from contextlib import ExitStack

import concourse.bass as bass
from concourse import mybir

F32 = mybir.dt.float32
F16 = mybir.dt.float16
BF16 = mybir.dt.bfloat16
U32 = mybir.dt.uint32
ACT = mybir.ActivationFunctionType
ALU = mybir.AluOpType
AX = mybir.AxisListType

P = 128
D = 128
T = 128
C = 77
GROUP = 4
N = GROUP * T
HEADS = 16
DH = D // HEADS
SLOTS = 4
PARTS = 4
TILES = HEADS // SLOTS
VW = 32
EXPERTS = 8
CHUNKS = 4
LN_EPS = 1e-5
ATTN_EPS = 1e-6
MAX_SCALE = 256.0
MASKED = -1e30
AHEAD = 2
RING = 12

COLS = ["norm1_w", "norm1_b", "norm2_w", "norm2_b", "norm3_w", "norm3_b", "sa_g", "sa_b", "caq_g", "caq_b",
        "cakv_g", "cakv_b", "moe_g", "moe_b", "g1", "be1", "g2", "be2"]
COLS += [f"b{w}{m}" for m in range(4) for w in "qkv"]
COLS += [f"ffn_b1_{c}" for c in range(CHUNKS)] + [f"moe_b1_{e}_{c}" for e in range(EXPERTS) for c in range(CHUNKS)]
ROWS = ["norm2_w", "norm2_b", "gamma1", "gamma2", "norm3_w", "norm3_b", "l1_gamma", "l1_beta",
        "sa_out_b", "ca_out_b", "bo_s", "bo_c", "ffn_b2", "g1", "be1", "g2", "be2", "g3", "be3"]
MATS = [f"w{w}{m}" for m in range(4) for w in "qkvo"]


SELF2, CROSS2, SELF3, CROSS3 = range(4)
KEYS = [T, C, T, C]
CAUSAL = [False, False, True, False]
LAG = 2
UNITS = GROUP * TILES

LN_CTX, LN_X, LN_CROSS, LN_L1, LN_SA, LN_CAQ = range(6)
LN_MOE, LN_31, LN_32, LN_33 = range(4)
F_CTX, F_RAW, F_X, F_CROSS, F_SA, F_CAQ = range(6)
F_MOE, F_L3, F_31, F_32 = range(4)

def attention_units(m):
    for t in range(TILES + LAG):
        for b in range(GROUP):
            if t < TILES:
                yield f"score{m}_{t}_{b}", t, b
            if t >= LAG:
                yield f"weigh{m}_{t - LAG}_{b}", t - LAG, b
        if t < TILES:
            yield f"max{m}_{t}", t, 0


def attention_phases(m):
    return [f"proj{m}"] + [p for p, _, _ in attention_units(m)] + [f"out{m}", f"sum{m}"]


def experts():
    for e in range(EXPERTS + 1):
        if e < EXPERTS:
            yield from (f"in{e}_0", f"in{e}_1")
        yield from ("gates",) if e == 0 else (f"out{e - 1}_0", f"out{e - 1}_1")


TOGETHER = [
    (["max0", "scores0_t", "values0", "hidden0", "cross", "cross_turn", "scores1", "max1", "scores1_t", "values1",
      "x1_turn", "linear", "l1_norm", "sa_norm", "sa_turn"] + attention_phases(SELF2)[:1],
     ["moe_norm", "moe_turn", "router", *experts(), "l3_turn"]),
    (attention_phases(SELF2)[1:] + ["caq_norm", "caq_turn"] + attention_phases(CROSS2)[:1],
     attention_phases(SELF3) + ["n31_norm", "n31_turn"]),
    (attention_phases(CROSS2)[1:] + ["norms", "ctx_turn", "x_turn", "scores0"],
     attention_phases(CROSS3) + ["n32_norm", "n32_turn", "ffn_in", "ffn_out", "result"]),
]
PLAN = {
    "max0": 3.0, "scores0_t": 3.0, "values0": 3.0, "hidden0": 3.0, "cross": 3.0, "cross_turn": 3.0, "scores1":
    3.0, "max1": 3.0, "scores1_t": 3.0, "values1": 3.0, "x1_turn": 3.48, "linear": 3.0, "l1_norm": 7.68,
    "sa_norm": 3.0, "sa_turn": 3.0, "proj0": 4.0, "moe_norm": 2.66, "moe_turn": 3.0, "router": 3.0, "expert0":
    1.8, "gates": 1.8, "expert1": 1.8, "l3_turn": 3.0, "score0": 0.6, "max0_0": 0.6, "max0_1": 0.6, "weigh0":
    0.7, "max0_2": 0.6, "max0_3": 0.6, "out0": 3.0, "sum0": 2.0, "caq_norm": 4.0, "caq_turn": 4.0, "proj1": 4.0,
    "proj2": 4.0, "score2": 0.6, "max2_0": 0.6, "max2_1": 0.6, "weigh2": 0.7, "max2_2": 0.6, "max2_3": 0.6,
    "out2": 3.0, "sum2": 2.0, "n31_norm": 4.0, "n31_turn": 4.0, "score1": 0.6, "max1_0": 0.53, "max1_1": 0.6,
    "weigh1": 0.7, "max1_2": 0.6, "max1_3": 0.6, "out1": 3.0, "sum1": 2.0, "norms": 4.0, "ctx_turn": 3.0,
    "x_turn": 3.0, "scores0": 3.0, "proj3": 4.0, "score3": 0.6, "max3_0": 0.6, "max3_1": 0.6, "weigh3": 0.7,
    "max3_2": 0.35, "max3_3": 0.6, "out3": 3.0, "sum3": 1.96, "n32_norm": 4.0, "n32_turn": 4.0, "ffn_in": 3.0,
    "ffn_out": 1.98, "result": 3.0
}


def planned(name):
    if name.startswith(("score", "weigh")) and "_" in name and name[5] in "0123" and name.count("_") == 2:
        return PLAN[name[:6]]
    if name.startswith(("in", "out")) and "_" in name:
        return PLAN["expert0" if int(name.split("_")[0][-1]) < EXPERTS // 2 else "expert1"]
    return PLAN[name]


def common_order(together):
    order = []
    for pair in together:
        when = []
        for which, phases in enumerate(pair):
            total, t = sum(planned(name) for name in phases), 0.0
            for k, name in enumerate(phases):
                when.append((t / total, which, k, name))
                t += planned(name)
        order += [name for *_, name in sorted(when)]
    return order


ORDER = common_order(TOGETHER)


def weave(*streams):
    upcoming = [next(s, None) for s in streams]
    for phase in ORDER:
        for i, s in enumerate(streams):
            if upcoming[i] == phase:
                upcoming[i] = next(s, None)


def alone(stream):
    for _ in stream:
        pass


STREAM = dict(
    k_proj=2, q_proj=2, v_proj=2, k_hi=2, q_hi=2, v_sb=2, k_split=4, q_split=4,
    k_blk=32,
    scores=2 * UNITS, smax=2 * UNITS, m_t=8, m_sb=8, scores_t=2 * UNITS, probs=2 * UNITS, pv=2 * UNITS,
    o_sb=8, o_t=8, o_rden=8, o_norm=8, on_t=2, on_sb=2, attn=2, attn_sum=2,

) | {f"kq_shift{j}": 2 * 32 for j in range(TILES)} | {f"m_shift{j}": 2 * 16 for j in range(TILES)}
PER = {s + n: c for s in ("a_", "b_") for n, c in STREAM.items()}
PER |= dict(
    a_ln_stats=24, a_ln_mean=24, a_ln_var=6, a_ln_rstd=6, a_ln_hat=6, a_turned=7, a_feat=6, a_residual=2,
    b_ln_stats=16, b_ln_mean=16, b_ln_var=4, b_ln_rstd=4, b_ln_hat=4, b_turned=4, b_feat=4, b_residual=3,
    x_in=16, ctx_in=16, out_stored=16, ctx_kept=1,
    ctx_min=1, ctx_exp=1, ctx_phi=1, v0=1, v0_sb=1, kv=1, kv_sb=2,
    s0=1, max0=1, max0_t=1, max0_sb=1, s0_t=1, p0=1, hpre=1, h_steps=2, h_in=1, h=1, h_t=1, h_t_sb=1,
    cross=1, cross_g=1, s1=1, max1=1, max1_t=1, max1_sb=1, s1_t=1, p1=1, pv1=1, pv1_steps=3, x1=1,
    x_steps=2, skip=1,
    x1_min=1, x1_exp=1, x1_phi=1, num=1, num_steps=3, l1_sum=1, l1_scaled=1, x2=1,
    res_scaled=3, moe_hi=1, moe_lo=1, router=1, logits=1, top=4, top_at=4, gap=1, gap_exp=1, gate_steps=8,
    gates=1, gates_t=1, gates_sb=1, gate_bias=1, fc1=32, gelu=32, fc2=8, moe_acc=9,
    ffn1=4, ffn_relu=4, ffn2=1, ffn_sum=1, out_ready=1,
)
START = dict(out_ready=1, out_stored=16)


def build(nc, a, out, steps):
    with ExitStack() as ctx:
        def sb(name, shape, dt=F32):
            return ctx.enter_context(nc.sbuf_tensor(name, shape, dt))

        S = {n: ctx.enter_context(nc.semaphore(n)) for n in PER}
        s_weights = ctx.enter_context(nc.semaphore("weights_in"))
        s_experts = ctx.enter_context(nc.semaphore("experts_in"))
        s_fill = ctx.enter_context(nc.semaphore("filled"))
        s_select = ctx.enter_context(nc.semaphore("selected"))
        s_held = ctx.enter_context(nc.semaphore("held"))
        s_split = ctx.enter_context(nc.semaphore("w1_split"))
        s_const = ctx.enter_context(nc.semaphore("row_constants"))
        FIRST = (0, 0)

        class Values:
            def __init__(self, eng, it):
                self.eng, self.it, self.base = eng, it, {}
                self.ring = [[None, eng.alloc_register(f"count{i}")] for i in range(RING)]

            def get(self, per, count):
                if per not in self.base:
                    self.base[per] = self.eng.alloc_register(f"step_x{per}")
                    self.eng.reg_mul(self.base[per], self.it, per)
                for k, (key, reg) in enumerate(self.ring):
                    if key == (per, count):
                        self.ring.append(self.ring.pop(k))
                        return reg
                _, reg = self.ring.pop(0)
                self.ring.append([(per, count), reg])
                self.eng.reg_add(reg, self.base[per], count)
                return reg

        class Group:
            def __init__(self, step, lead=0, values=None):
                self.step, self.lead, self.values = step, lead, values

        FIRST = Group(0)
        SECOND = Group(1)
        LAST = Group(steps - 1)

        def at(g, name, count):
            count += g.lead * PER[name] + START.get(name, 0)
            return g.values.get(PER[name], count) if g.values else g.step * PER[name] + count

        bank = {s: [ctx.enter_context(nc.psum_tensor(f"{s}bank{i}", [P, 512], F32)) for i in range(4)]
                for s in ("a_", "b_")}

        cols = sb("cols", [P, len(COLS)])
        rows = sb("rows", [P, len(ROWS), D])
        mats = sb("mats", [P, len(MATS), D])
        fc1_w = sb("fc1_w", [P, 4])
        fc1_b = sb("fc1_b", [P, 4])
        fc2_aug = sb("fc2_aug", [5, D])
        router_w = sb("router_w", [P, EXPERTS])
        router_b = sb("router_b", [P, EXPERTS])
        moe_w1 = [sb(f"moe_w1_{i}", [P, EXPERTS, CHUNKS, P], F16) for i in ("hi", "lo")]
        moe_w2 = sb("moe_w2", [P, EXPERTS, CHUNKS, D])
        moe_b2 = sb("moe_b2", [EXPERTS, D])
        ffn_w1 = sb("ffn_w1", [P, CHUNKS, P])
        ffn_w2 = sb("ffn_w2", [P, CHUNKS, D])
        slot_mask = sb("slot_mask", [P, SLOTS])
        expert_id = sb("expert_id", [P, EXPERTS])
        pick_seq = sb("pick_seq", [GROUP, GROUP, T])
        ident = sb("ident", [P, P])
        ident_bf = sb("ident_bf", [P, P], BF16)
        mask_q = sb("mask_q", [P, SLOTS, T], BF16)
        mask_k = sb("mask_k", [P, SLOTS, T], BF16)
        ln_eps = sb("ln_eps", [P, GROUP])
        minus_half = sb("minus_half", [P, GROUP])
        self_scale = sb("self_scale", [P, D])
        x_shift = sb("x_shift", [P, D])
        shift31 = sb("shift31", [P, D])
        shift32 = sb("shift32", [P, D])

        def col(name):
            i = COLS.index(name)
            return cols[:, i:i + 1]

        def row(name):
            return rows[:, ROWS.index(name), :].unsqueeze(1).broadcast_to([P, GROUP, D])

        def shifted(t):
            return t[:].unsqueeze(1).broadcast_to([P, GROUP, D])

        def mat(name):
            return mats[:, MATS.index(name), :]

        class Buffers:
            def __init__(self, s):
                self.stats = sb(s + "stats", [P, GROUP, 6])
                self.mean_var = sb(s + "mean_var", [P, GROUP, 2])
                self.rstd = sb(s + "rstd", [P, GROUP])
                self.var_eps = sb(s + "var_eps", [P, GROUP])
                self.hat = sb(s + "hat", [P, GROUP, D])
                self.feat = sb(s + "feat", [P, N])
                self.x_res = sb(s + "x_res", [P, GROUP, D])
                self.residual = sb(s + "residual", [P, GROUP, D])
                self.k_nat = sb(s + "k_nat", [P, PARTS, N], F16)
                self.q_nat = sb(s + "q_nat", [P, PARTS, N], F16)
                self.k_int = sb(s + "k_int", [P, TILES, N], F16)
                self.q_int = sb(s + "q_int", [P, TILES, N], F16)
                self.k_blk = sb(s + "k_blk", [P, TILES, SLOTS, N], F16)
                self.v_pad = sb(s + "v_pad", [P, GROUP, HEADS, VW])
                self.smax = sb(s + "smax", [P, GROUP, P])
                self.m_nat = sb(s + "m_nat", [P, N], F16)
                self.probs = [sb(f"{s}probs{i}", [P, SLOTS * T]) for i in range(2)]
                self.o_sb = sb(s + "o_sb", [P, TILES * T])
                self.o_rden = sb(s + "o_rden", [P, TILES, GROUP, SLOTS])
                self.o_norm = sb(s + "o_norm", [P, GROUP, D])

        buf = {s: Buffers(s) for s in ("a_", "b_")}
        fr, bk = buf["a_"], buf["b_"]

        x_tok = sb("x_tok", [P, GROUP, D])
        ctx_tok = sb("ctx_tok", [C, GROUP, D + 1])
        work = fr.k_blk[:].bitcast(F32).rearrange("p j i n -> p (j i) n")
        assert work.shape[2] == N // 2
        work = [work[:, 2 * i:2 * i + 2, :].rearrange("p i n -> p (i n)") for i in range(8)]

        def by_seq(ap, n=P):
            return ap.rearrange("p (b d) -> p b d", b=GROUP)[0:n]

        ctx_hat = by_seq(work[0], C)
        ctx_phi = by_seq(work[1], C)
        p0 = work[2][0:C, :]
        h_t = work[3][0:5, :]
        p1 = work[4]
        x1_phi = work[5]
        l1_sum = by_seq(work[6])
        pv1_n = by_seq(work[7])
        norm1_f = sb("norm1_f", [P, GROUP * C])
        cakv_f = sb("cakv_f", [P, GROUP * C])
        ctx_f = sb("ctx_f", [P, GROUP * C])
        v0 = sb("v0", [C, GROUP, 5])
        kv = sb("kv", [P, GROUP, D + 1])
        max0 = sb("max0", [P, GROUP])
        max0_t = sb("max0_t", [GROUP, P])
        h_rden = sb("h_rden", [P, GROUP])
        h_mul = sb("h_mul", [P, GROUP, 4])
        h_in = sb("h_in", [P, GROUP, 4])
        h = sb("h", [P, GROUP, 5])
        cross_g = sb("cross_g", [P, GROUP, D])
        cross_hat = sb("cross_hat", [P, GROUP, D + 1])
        max1 = sb("max1", [P, GROUP])
        max1_t = sb("max1_t", [GROUP, P])
        pv1_rden = sb("pv1_rden", [P, GROUP])
        skip = sb("skip", [P, GROUP, D])
        x1 = sb("x1", [P, GROUP, D])
        num_den = sb("num_den", [P, GROUP])
        num_rden = sb("num_rden", [P, GROUP])
        ctx_kept = sb("ctx_kept", [P, GROUP * C])
        logits = sb("logits", [P, GROUP, EXPERTS])
        top = sb("top", [P, GROUP, 8])
        top_at = sb("top_at", [P, GROUP, 8], U32)
        top_f = sb("top_f", [P, GROUP, 8])
        gap = sb("gap", [P, GROUP])
        gap_exp = sb("gap_exp", [P, GROUP])
        gap_den = sb("gap_den", [P, GROUP])
        gate1 = sb("gate1", [P, GROUP])
        gate2 = sb("gate2", [P, GROUP])
        hot = [sb(f"hot{i}", [P, GROUP, EXPERTS]) for i in range(2)]
        pick = [sb(f"pick{i}", [P, GROUP, EXPERTS]) for i in range(2)]
        gates = sb("gates", [P, GROUP, EXPERTS])
        gates_t = bk.o_sb[0:EXPERTS, :]
        hid = bk.k_blk[:].bitcast(F32).rearrange("p j i n -> p (j i n)").rearrange("p (e c n) -> p e c n", e=2, c=CHUNKS)
        hidden = [hid[:, i] for i in range(2)]
        w1_f32 = bk.k_blk[:].bitcast(F32).rearrange("p j i n -> p (j i n)")\
            .rearrange("p (e c f) -> p e c f", e=EXPERTS, c=CHUNKS)
        moe_hi, moe_lo = bk.q_nat[:, 0, :], bk.q_nat[:, 1, :]
        out_tok = sb("out_tok", [P, GROUP, D])

        loads = [(cols[:], a["cols"]), (fc1_w[:], a["fc1_w"]), (rows[:], a["rows"]), (mats[:], a["mats"]),
                 (fc1_b[:], a["fc1_b"]), (fc2_aug[:], a["fc2_aug"]), (pick_seq[:], a["pick_seq"]),
                 (slot_mask[:], a["slot_mask"])]
        expert_loads = [(router_w[:], a["router_w"]), (router_b[:], a["router_b"]), (expert_id[:], a["expert_id"]),
                        (moe_b2[:], a["moe_b2"]), (w1_f32, a["moe_w1"]), (moe_w2[:], a["moe_w2"]),
                        (ffn_w1[:], a["ffn_w1"]), (ffn_w2[:], a["ffn_w2"])]
        weights_in = 16 * len(loads)
        experts_in = 16 * len(expert_loads)
        fills = [(ident[:], 0.0), (ident_bf[:], 0.0), (mask_q[:], 0.0), (mask_k[:], 0.0),
                 (ctx_tok[:, :, D:], 1.0), (v0[:, :, 4:], 1.0), (h[:, :, 4:], 1.0), (cross_hat[:, :, D:], 1.0),
                 (ln_eps[:], LN_EPS), (minus_half[:], -0.5)]
        for x in (fr, bk):
            fills += [(x.k_nat[:, 3, :], MAX_SCALE), (x.q_nat[:, 3, :], 0.0), (x.v_pad[:], 0.0), (x.smax[:], 0.0)]
        selects = 4
        filled = len(fills) + 2

        block = ctx.enter_context(nc.Block())

        def seq_keys(b, nk):
            return slice(b * nk, (b + 1) * nk)

        def seq_tok(b):
            return slice(b * T, (b + 1) * T)

        def wide(s, b):
            first = 2 if s else 0
            return bank["a_"][first + b // 3][:, (D + 1) * (b % 3):(D + 1) * (b % 3 + 1)]

        def wide_bank(s, i):
            n = (3, 1)[i]
            first = 2 if s else 0
            return slice(3 * i, 3 * i + n), bank["a_"][first + i][:, 0:n * (D + 1)].rearrange("p (b e) -> p b e", b=n)

        def score_bank(s, j, b):
            return bank[s][b % 2 if j < LAG else 0]

        def weigh_bank(s, j, b):
            return bank[s][b % 2 if j >= TILES - LAG else 1]

        @block.sync
        def _(sp):
            sp.dma_start(ctx_tok[:, :, 0:D], a["ctx"][0].rearrange("b t d -> t b d")).then_inc(S["ctx_in"], 16)
            sp.dma_start(x_tok[:], a["x"][0].rearrange("b t d -> t b d")).then_inc(S["x_in"], 16)
            for dst, src in loads:
                sp.dma_start(dst, src).then_inc(s_weights, 16)
            for dst, src in expert_loads:
                sp.dma_start(dst, src).then_inc(s_experts, 16)

            def attention(g, s, m):
                x, n, keys = buf[s], m % 2, GROUP * KEYS[m]
                yield f"proj{m}"
                sp.wait_ge(S[s + "k_split"], at(g, s + "k_split", 2 * (n + 1)))
                sp.wait_ge(S[s + "q_split"], at(g, s + "q_split", 2 * (n + 1)))
                for j in range(TILES):
                    sp.dma_start(x.k_int[:, j, 0:keys],
                                 x.k_nat[32 * j:32 * j + 32, :, 0:keys]).then_inc(S[f"{s}kq_shift{j}"], 16)
                    sp.dma_start(x.q_int[:, j, :], x.q_nat[32 * j:32 * j + 32, :, :])\
                        .then_inc(S[f"{s}kq_shift{j}"], 16)
                for j in range(TILES):
                    yield f"max{m}_{j}"
                    sp.wait_ge(S[s + "m_sb"], at(g, s + "m_sb", TILES * n + j + 1))
                    sp.dma_start(x.q_int[3::4, j, :], x.m_nat[32 * j:32 * j + 32, :])\
                        .then_inc(S[f"{s}m_shift{j}"], 16)

            def head(g):
                yield "scores0"
                sp.wait_ge(S["kv"], at(g, "kv", 1))
                sp.dma_start(ctx_tok[:, :, 0:D],
                             a["ctx"][g.step + g.lead + 1].rearrange("b t d -> t b d")).then_inc(S["ctx_in"], 16)
                sp.dma_start(x_tok[:], a["x"][g.step + g.lead + 1].rearrange("b t d -> t b d")).then_inc(S["x_in"], 16)

            def tail(g):
                yield from attention(g, "a_", SELF2)
                yield from attention(g, "a_", CROSS2)

            def front(g, ahead):
                yield from tail(g)
                yield from head(ahead)

            def back(g):
                yield from attention(g, "b_", SELF3)
                yield from attention(g, "b_", CROSS3)
                yield "result"
                sp.wait_ge(S["out_ready"], at(g, "out_ready", 1))
                sp.dma_start(out[g.step].rearrange("b t d -> t b d"), out_tok[:]).then_inc(S["out_stored"], 16)

            sp.sem_inc(S["out_stored"], START["out_stored"])
            alone(head(FIRST))
            alone(tail(FIRST))
            alone(head(SECOND))
            with sp.Fori(0, steps - 1) as it:
                v = Values(sp, it)
                weave(front(Group(it, 1, v), Group(it, 2, v)), back(Group(it, 0, v)))
            alone(back(LAST))
            sp.wait_ge(S["out_stored"], START["out_stored"] + 16 * steps)
            sp.wait_ge(S["x_in"], 16 * (steps + 2))
            sp.wait_ge(S["ctx_in"], 16 * (steps + 2))

        @block.gpsimd
        def _(pool):
            for ap, value in fills:
                pool.memset(ap, value).then_inc(s_fill, 1)
            pool.wait_ge(s_fill, len(fills))
            for x in (fr, bk):
                pool.memset(x.v_pad[:, :, :, DH:DH + 1], 1.0).then_inc(s_fill, 1)
            for m in (ident, ident_bf):
                pool.affine_select(out=m[:], in_=m[:], compare_op=ALU.not_equal, fill=1.0, base=0,
                                   pattern=[[-1, P]], channel_multiplier=1).then_inc(s_select, 1)
            pool.affine_select(out=mask_q[:], in_=mask_q[:], compare_op=ALU.is_ge, fill=MASKED, base=0,
                               pattern=[[0, SLOTS], [-1, T]], channel_multiplier=1).then_inc(s_select, 1)
            pool.affine_select(out=mask_k[:], in_=mask_k[:], compare_op=ALU.is_ge, fill=MASKED, base=0,
                               pattern=[[0, SLOTS], [1, T]], channel_multiplier=-1).then_inc(s_select, 1)

            def root(g, s, n, p=P):
                x = buf[s]
                pool.wait_ge(S[s + "ln_mean"], at(g, s + "ln_mean", GROUP * (n + 1)))
                pool.tensor_tensor(x.var_eps[0:p, :], x.mean_var[0:p, :, 1], ln_eps[0:p, :], ALU.add)\
                    .then_inc(S[s + "ln_var"], 1)
                pool.wait_ge(S[s + "ln_var"], at(g, s + "ln_var", n + 1))
                pool.tensor_tensor(x.rstd[0:p, :], x.var_eps[0:p, :], minus_half[0:p, :], ALU.pow)\
                    .then_inc(S[s + "ln_rstd"], 1)

            def head(g):
                yield "norms"
                root(g, "a_", LN_CTX, C)
                root(g, "a_", LN_X)
                pool.wait_ge(S["a_ln_hat"], at(g, "a_ln_hat", LN_X + 1))
                pool.tensor_tensor(skip[:], fr.hat[:], row("norm2_w"), ALU.mult).then_inc(S["x_steps"], 1)
                pool.wait_ge(S["x_steps"], at(g, "x_steps", 1))
                pool.tensor_tensor(skip[:], skip[:], shifted(x_shift), ALU.add).then_inc(S["x_steps"], 1)

            def tail(g):
                yield "cross"
                root(g, "a_", LN_CROSS)
                pool.wait_ge(S["x_steps"], at(g, "x_steps", 2))
                pool.wait_ge(S["cross_g"], at(g, "cross_g", 1))
                pool.tensor_tensor(skip[:], skip[:], cross_g[:], ALU.add).then_inc(S["skip"], 1)
                yield "l1_norm"
                root(g, "a_", LN_L1)
                yield "sa_norm"
                root(g, "a_", LN_SA)
                pool.wait_ge(S["x2"], at(g, "x2", 1))
                pool.tensor_tensor(fr.residual[:], fr.x_res[:], row("sa_out_b"), ALU.add).then_inc(S["a_residual"], 1)
                yield "caq_norm"
                root(g, "a_", LN_CAQ)
                pool.wait_ge(S["a_attn_sum"], at(g, "a_attn_sum", 1))
                pool.tensor_tensor(fr.residual[:], fr.x_res[:], row("ca_out_b"), ALU.add).then_inc(S["a_residual"], 1)
                yield f"sum{CROSS2}"
                pool.wait_ge(S["a_feat"], at(g, "a_feat", F_RAW + 1))
                if g is not FIRST:
                    pool.wait_ge(S["b_v_proj"], at(g, "b_v_proj", 0))
                pool.sem_inc(s_held, 1)
                pool.tensor_copy(ctx_kept[:], ctx_f[:]).then_inc(S["ctx_kept"], 1)

            def front(g, ahead):
                yield from tail(g)
                yield from head(ahead)

            def back(g):
                yield "moe_norm"
                root(g, "b_", LN_MOE)
                yield "l3_turn"
                pool.wait_ge(S["moe_acc"], at(g, "moe_acc", EXPERTS + 1))
                pool.tensor_tensor(bk.residual[:], bk.x_res[:], row("bo_s"), ALU.add).then_inc(S["b_residual"], 1)
                for n, (ln, scale, shift) in enumerate(((LN_31, "g1", shift31), (LN_32, "g2", shift32))):
                    yield f"n3{n + 1}_norm"
                    root(g, "b_", ln)
                    pool.wait_ge(S["b_ln_hat"], at(g, "b_ln_hat", ln + 1))
                    pool.tensor_tensor(bk.residual[:], bk.hat[:], row(scale), ALU.mult).then_inc(S["res_scaled"], 1)
                    pool.wait_ge(S["res_scaled"], at(g, "res_scaled", n + 1))
                    pool.tensor_tensor(bk.residual[:], bk.residual[:], shifted(shift), ALU.add)\
                        .then_inc(S["b_residual"], 1)
                yield "result"
                root(g, "b_", LN_33)
                pool.wait_ge(S["out_stored"], at(g, "out_stored", 0))
                pool.wait_ge(S["b_ln_hat"], at(g, "b_ln_hat", LN_33 + 1))
                pool.tensor_tensor(out_tok[:], bk.hat[:], row("g3"), ALU.mult).then_inc(S["res_scaled"], 1)
                pool.wait_ge(S["res_scaled"], at(g, "res_scaled", 3))
                pool.tensor_tensor(out_tok[:], out_tok[:], row("be3"), ALU.add).then_inc(S["out_ready"], 1)

            pool.wait_ge(s_weights, weights_in)
            pool.wait_ge(s_const, 6)
            pool.sem_inc(S["out_ready"], START["out_ready"])
            alone(head(FIRST))
            alone(tail(FIRST))
            alone(head(SECOND))
            with pool.Fori(0, steps - 1) as it:
                v = Values(pool, it)
                weave(front(Group(it, 1, v), Group(it, 2, v)), back(Group(it, 0, v)))
            alone(back(LAST))

        @block.scalar
        def _(act):
            def affine(g, s, t, f, scale, shift):
                act.wait_ge(S[s + "turned"], at(g, s + "turned", t))
                act.activation(buf[s].feat[:], bank[s][2][:], ACT.Identity, bias=col(shift), scale=col(scale))\
                    .then_inc(S[s + "feat"], 1)

            def attention(g, s, m):
                x, n, nk, ps = buf[s], m % 2, KEYS[m], bank[s]
                keys = GROUP * nk
                yield f"proj{m}"
                act.wait_ge(S[s + "k_proj"], at(g, s + "k_proj", n + 1))
                act.activation(x.k_nat[:, 0, 0:keys], ps[3][:, 0:keys], ACT.Identity,
                               bias=col(f"bk{m}")).then_inc(S[s + "k_hi"], 1)
                act.wait_ge(S[s + "q_proj"], at(g, s + "q_proj", n + 1))
                act.activation(x.q_nat[:, 0, :], ps[1][:], ACT.Identity, bias=col(f"bq{m}")).then_inc(S[s + "q_hi"], 1)
                act.wait_ge(S[s + "v_proj"], at(g, s + "v_proj", n + 1))
                act.activation(x.v_pad[0:nk, :, :, 0:DH],
                               ps[0][0:nk, :].rearrange("k (b h d) -> k b h d", b=GROUP, h=HEADS),
                               ACT.Copy).then_inc(S[s + "v_sb"], 1)

                def copy_out(j):
                    act.wait_ge(S[s + "pv"], at(g, s + "pv", n * UNITS + GROUP * (j + 1)))
                    if j >= 1:
                        act.wait_ge(S[s + "o_t"], at(g, s + "o_t", TILES * n + j))
                    act.activation(x.o_sb[:], ps[2][:], ACT.Copy).then_inc(S[s + "o_sb"], 1)

                for phase, j, b in attention_units(m):
                    u = GROUP * j + b
                    yield phase
                    if phase.startswith("max"):
                        act.wait_ge(S[s + "m_t"], at(g, s + "m_t", TILES * n + j + 1))
                        act.activation(x.m_nat[32 * j:32 * j + 32, :], ps[3][0:32, :], ACT.Copy,
                                       scale=1.0 / MAX_SCALE).then_inc(S[s + "m_sb"], 1)
                    elif phase.startswith("weigh"):
                        if b == 0 and j >= 1:
                            copy_out(j - 1)
                        act.wait_ge(S[s + "scores_t"], at(g, s + "scores_t", n * UNITS + u + 1))
                        if u >= 2:
                            act.wait_ge(S[s + "pv"], at(g, s + "pv", n * UNITS + u - 1))
                        act.activation(x.probs[u % 2][0:nk], weigh_bank(s, j, b)[0:nk, :], ACT.Exp, scale=DH ** -0.5)\
                            .then_inc(S[s + "probs"], 1)
                yield f"out{m}"
                copy_out(TILES - 1)
                act.wait_ge(S[s + "on_t"], at(g, s + "on_t", n + 1))
                act.activation(x.feat[:], ps[2][:], ACT.Identity, bias=col(f"bv{m}")).then_inc(S[s + "on_sb"], 1)

            def head(g):
                yield "norms"
                act.wait_ge(S["ctx_min"], at(g, "ctx_min", 1))
                act.activation(ctx_phi, ctx_phi, ACT.Exp).then_inc(S["ctx_exp"], 1)
                yield "ctx_turn"
                act.wait_ge(S["a_turned"], at(g, "a_turned", 1))
                act.activation(norm1_f[:], bank["a_"][2][:, 0:GROUP * C], ACT.Identity, bias=col("norm1_b"),
                               scale=col("norm1_w"))
                act.activation(cakv_f[:], bank["a_"][2][:, 0:GROUP * C], ACT.Identity, bias=col("cakv_b"),
                               scale=col("cakv_g")).then_inc(S["a_feat"], 1)
                if g is not FIRST:
                    act.wait_ge(S["ctx_kept"], at(g, "ctx_kept", 0))
                act.wait_ge(S["a_turned"], at(g, "a_turned", 2))
                act.activation(ctx_f[:], bank["a_"][3][:, 0:GROUP * C], ACT.Copy).then_inc(S["a_feat"], 1)
                yield "x_turn"
                act.wait_ge(S["v0"], at(g, "v0", 1))
                act.activation(v0[:, :, 0:4], bank["a_"][1][0:C, 0:4 * GROUP].rearrange("k (b f) -> k b f", b=GROUP),
                               ACT.Copy).then_inc(S["v0_sb"], 1)
                affine(g, "a_", 3, F_X, "norm2_w", "norm2_b")
                yield "scores0"
                act.wait_ge(S["kv"], at(g, "kv", 1))
                for i in range(2):
                    seqs, src = wide_bank(0, i)
                    act.activation(kv[:, seqs, :], src, ACT.Copy).then_inc(S["kv_sb"], 1)

            def tail(g):
                yield "max0"
                act.wait_ge(S["max0_t"], at(g, "max0_t", 1))
                act.activation(max0_t[:], bank["a_"][2][0:GROUP, 0:P], ACT.Copy).then_inc(S["max0_sb"], 1)
                yield "scores0_t"
                act.wait_ge(S["s0_t"], at(g, "s0_t", 1))
                act.activation(p0, bank["a_"][3][0:C, :], ACT.Exp, scale=D ** -0.5).then_inc(S["p0"], 1)
                yield "values0"
                act.wait_ge(S["h_in"], at(g, "h_in", 1))
                act.activation(h[:, :, 0:4], h_in[:], ACT.Gelu).then_inc(S["h"], 1)
                yield "hidden0"
                act.wait_ge(S["h_t"], at(g, "h_t", 1))
                act.activation(h_t, bank["a_"][2][0:5, :], ACT.Copy).then_inc(S["h_t_sb"], 1)
                yield "cross_turn"
                affine(g, "a_", 4, F_CROSS, "norm3_w", "norm3_b")
                yield "max1"
                act.wait_ge(S["max1_t"], at(g, "max1_t", 1))
                act.activation(max1_t[:], bank["a_"][1][0:GROUP, 0:P], ACT.Copy).then_inc(S["max1_sb"], 1)
                yield "scores1_t"
                act.wait_ge(S["s1_t"], at(g, "s1_t", 1))
                act.activation(p1, bank["a_"][0][:], ACT.Exp, scale=D ** -0.5).then_inc(S["p1"], 1)
                yield "x1_turn"
                act.wait_ge(S["x1_min"], at(g, "x1_min", 1))
                act.activation(x1_phi, x1_phi, ACT.Exp).then_inc(S["x1_exp"], 1)
                yield "sa_turn"
                affine(g, "a_", 6, F_SA, "sa_g", "sa_b")
                yield from attention(g, "a_", SELF2)
                yield "caq_turn"
                affine(g, "a_", 7, F_CAQ, "caq_g", "caq_b")
                yield from attention(g, "a_", CROSS2)

            def front(g, ahead):
                yield from tail(g)
                yield from head(ahead)

            def back(g):
                yield "moe_turn"
                affine(g, "b_", 1, F_MOE, "moe_g", "moe_b")
                act.activation(moe_hi, bank["b_"][2][:], ACT.Identity, bias=col("moe_b"), scale=col("moe_g"))\
                    .then_inc(S["moe_hi"], 1)
                yield "router"
                act.wait_ge(S["gap"], at(g, "gap", 1))
                act.activation(gap_exp[:], gap[:], ACT.Exp).then_inc(S["gap_exp"], 1)
                for e in range(EXPERTS):
                    for i in range(2):
                        yield f"in{e}_{i}"
                        for c in (2 * i, 2 * i + 1):
                            if c == 0 and e >= 2:
                                act.wait_ge(S["fc2"], at(g, "fc2", e - 1))
                            act.wait_ge(S["fc1"], at(g, "fc1", CHUNKS * e + c + 1))
                            act.activation(hidden[e % 2][:, c, :], bank["b_"][c % 2][:], ACT.Gelu,
                                           bias=col(f"moe_b1_{e}_{c}")).then_inc(S["gelu"], 1)
                    if e == 0:
                        yield "gates"
                        act.wait_ge(S["gates_t"], at(g, "gates_t", 1))
                        act.activation(gates_t, bank["b_"][2][0:EXPERTS, :], ACT.Copy).then_inc(S["gates_sb"], 1)
                yield "l3_turn"
                act.wait_ge(S["b_turned"], at(g, "b_turned", 2))
                act.activation(bk.feat[:], bank["b_"][2][:], ACT.Copy).then_inc(S["b_feat"], 1)
                yield from attention(g, "b_", SELF3)
                yield "n31_turn"
                affine(g, "b_", 3, F_31, "g1", "be1")
                yield from attention(g, "b_", CROSS3)
                yield "n32_turn"
                affine(g, "b_", 4, F_32, "g2", "be2")
                yield "ffn_in"
                for c in range(CHUNKS):
                    act.wait_ge(S["ffn1"], at(g, "ffn1", c + 1))
                    act.activation(hidden[0][:, c, :], bank["b_"][c % 2][:], ACT.Relu, bias=col(f"ffn_b1_{c}"))\
                        .then_inc(S["ffn_relu"], 1)

            act.wait_ge(s_weights, weights_in)
            act.wait_ge(s_fill, filled)
            alone(head(FIRST))
            alone(tail(FIRST))
            alone(head(SECOND))
            act.wait_ge(s_experts, experts_in)
            act.activation(moe_w1[0][:], w1_f32, ACT.Copy).then_inc(s_split, 1)
            with act.Fori(0, steps - 1) as it:
                v = Values(act, it)
                weave(front(Group(it, 1, v), Group(it, 2, v)), back(Group(it, 0, v)))
            alone(back(LAST))

        @block.vector
        def _(dve):
            def normalise(g, s, n, src, dst, p=P):
                x = buf[s]
                for b in range(GROUP):
                    dve.bn_stats(x.stats[0:p, b, :], src(b)).then_inc(S[s + "ln_stats"], 1)
                dve.wait_ge(S[s + "ln_stats"], at(g, s + "ln_stats", GROUP * (n + 1)))
                dve.sem_inc(s_held, 1)
                for b in range(GROUP):
                    dve.bn_aggr(x.mean_var[0:p, b, :], x.stats[0:p, b, :]).then_inc(S[s + "ln_mean"], 1)
                dve.wait_ge(S[s + "ln_rstd"], at(g, s + "ln_rstd", n + 1))
                for b in range(GROUP):
                    last = dve.tensor_scalar(dst(b), src(b), x.mean_var[0:p, b, 0:1], x.rstd[0:p, b:b + 1],
                                             ALU.subtract, ALU.mult)
                last.then_inc(S[s + "ln_hat"], 1)

            def normalise_residual(g, s, n):
                normalise(g, s, n, lambda b: buf[s].x_res[:, b, :], lambda b: buf[s].hat[:, b, :])

            def attention(g, s, m):
                x, n, nk, ps = buf[s], m % 2, KEYS[m], bank[s]
                keys = GROUP * nk
                yield f"proj{m}"
                dve.wait_ge(S[s + "k_hi"], at(g, s + "k_hi", n + 1))
                dve.scalar_tensor_tensor(x.k_nat[:, 1, 0:keys], ps[3][:, 0:keys], col(f"bk{m}"),
                                         x.k_nat[:, 0, 0:keys], ALU.add, ALU.subtract).then_inc(S[s + "k_split"], 1)
                dve.tensor_copy(x.k_nat[:, 2, 0:keys], x.k_nat[:, 0, 0:keys]).then_inc(S[s + "k_split"], 1)
                dve.wait_ge(S[s + "q_hi"], at(g, s + "q_hi", n + 1))
                dve.scalar_tensor_tensor(x.q_nat[:, 2, :], ps[1][:], col(f"bq{m}"), x.q_nat[:, 0, :],
                                         ALU.add, ALU.subtract).then_inc(S[s + "q_split"], 1)
                dve.tensor_copy(x.q_nat[:, 1, :], x.q_nat[:, 0, :]).then_inc(S[s + "q_split"], 1)

                def block_keys(j):
                    dve.wait_ge(S[f"{s}kq_shift{j}"], at(g, f"{s}kq_shift{j}", 32 * (n + 1)))
                    for i in range(SLOTS):
                        dve.tensor_scalar(x.k_blk[:, j, i, 0:keys], x.k_int[:, j, 0:keys], slot_mask[:, i:i + 1], None,
                                          ALU.mult).then_inc(S[s + "k_blk"], 1)

                def divide(j):
                    c = TILES * n + j + 1
                    o_t = ps[3][:].rearrange("q (b i r) -> q b i r", b=GROUP, r=VW)
                    dve.wait_ge(S[s + "o_t"], at(g, s + "o_t", c))
                    dve.reciprocal(x.o_rden[:, j], o_t[:, :, :, DH]).then_inc(S[s + "o_rden"], 1)
                    dve.wait_ge(S[s + "o_rden"], at(g, s + "o_rden", c))
                    dve.tensor_tensor(x.o_norm[:, :, 32 * j:32 * j + 32].rearrange("q b (i d) -> q b i d", d=DH),
                                      o_t[:, :, :, 0:DH],
                                      x.o_rden[:, j].unsqueeze(3).broadcast_to([P, GROUP, SLOTS, DH]),
                                      ALU.mult).then_inc(S[s + "o_norm"], 1)

                for phase, j, b in attention_units(m):
                    u = GROUP * j + b
                    yield phase
                    if phase.startswith("score"):
                        if u == 0:
                            block_keys(0)
                        if b == 1 and j + 1 < TILES:
                            block_keys(j + 1)
                        dve.wait_ge(S[s + "scores"], at(g, s + "scores", n * UNITS + u + 1))
                        dve.tensor_reduce(x.smax[:, b, 32 * j:32 * j + 32:DH],
                                          score_bank(s, j, b)[:, 0:SLOTS * nk].rearrange("q (i k) -> q i k", i=SLOTS),
                                          AX.X, ALU.max, negate=True).then_inc(S[s + "smax"], 1)
                    elif phase.startswith("weigh"):
                        if b == 2 and j >= 1:
                            divide(j - 1)
                yield f"out{m}"
                divide(TILES - 1)
                yield f"sum{m}"
                dve.wait_ge(S[s + "attn"], at(g, s + "attn", n + 1))
                dve.wait_ge(S[s + "residual"], at(g, s + "residual", n + 1))
                dve.tensor_tensor(x.x_res[:], ps[1][:].rearrange("q (b d) -> q b d", b=GROUP), x.residual[:], ALU.add)\
                    .then_inc(S[s + "attn_sum"], 1)

            def head(g):
                yield "norms"
                dve.wait_ge(S["ctx_in"], at(g, "ctx_in", 16))
                if g is not FIRST:
                    dve.wait_ge(S["a_attn_sum"], at(g, "a_attn_sum", 0))
                dve.tensor_scalar(ctx_phi, ctx_tok[:, :, 0:D], 0.0, None, ALU.min).then_inc(S["ctx_min"], 1)
                normalise(g, "a_", LN_CTX, lambda b: ctx_tok[:, b, 0:D], lambda b: ctx_hat[:, b, :], C)
                dve.wait_ge(S["x_in"], at(g, "x_in", 16))
                normalise(g, "a_", LN_X, lambda b: x_tok[:, b, :], lambda b: fr.hat[:, b, :])
                dve.wait_ge(S["ctx_exp"], at(g, "ctx_exp", 1))
                dve.scalar_tensor_tensor(ctx_phi, ctx_phi, -1.0, ctx_tok[:, :, 0:D], ALU.add, ALU.max)\
                    .then_inc(S["ctx_phi"], 1)
                yield "scores0"
                dve.wait_ge(S["s0"], at(g, "s0", 1))
                dve.tensor_reduce(max0[:], bank["a_"][3][:, 0:GROUP * C].rearrange("q (b k) -> q b k", b=GROUP),
                                  AX.X, ALU.max, negate=True).then_inc(S["max0"], 1)

            def tail(g):
                yield "values0"
                dve.wait_ge(S["hpre"], at(g, "hpre", 1))
                hpre = bank["a_"][2][:, 0:5 * GROUP].rearrange("q (b f) -> q b f", b=GROUP)
                dve.reciprocal(h_rden[:], hpre[:, :, 4]).then_inc(S["h_steps"], 1)
                dve.wait_ge(S["h_steps"], at(g, "h_steps", 1))
                dve.tensor_tensor(h_mul[:], hpre[:, :, 0:4], h_rden[:].unsqueeze(2).broadcast_to([P, GROUP, 4]),
                                  ALU.mult).then_inc(S["h_steps"], 1)
                dve.wait_ge(S["h_steps"], at(g, "h_steps", 2))
                dve.tensor_tensor(h_in[:], h_mul[:], fc1_b[:].unsqueeze(1).broadcast_to([P, GROUP, 4]), ALU.add)\
                    .then_inc(S["h_in"], 1)
                yield "cross"
                dve.wait_ge(S["cross"], at(g, "cross", 1))
                cross = bank["a_"][3][:].rearrange("q (b d) -> q b d", b=GROUP)
                normalise(g, "a_", LN_CROSS, lambda b: cross[:, b, :], lambda b: cross_hat[:, b, 0:D])
                dve.tensor_tensor(cross_g[:], cross, row("gamma2"), ALU.mult).then_inc(S["cross_g"], 1)
                yield "scores1"
                dve.wait_ge(S["s1"], at(g, "s1", 1))
                dve.tensor_reduce(max1[:], bank["a_"][0][:].rearrange("q (b k) -> q b k", b=GROUP),
                                  AX.X, ALU.max, negate=True).then_inc(S["max1"], 1)
                yield "values1"
                dve.wait_ge(S["pv1"], at(g, "pv1", 1))
                for i in range(2):
                    seqs, src = wide_bank(1, i)
                    dve.reciprocal(pv1_rden[:, seqs], src[:, :, D]).then_inc(S["pv1_steps"], 1)
                dve.wait_ge(S["pv1_steps"], at(g, "pv1_steps", 2))
                for b in range(GROUP):
                    last = dve.scalar_tensor_tensor(pv1_n[:, b, :], wide(1, b)[:, 0:D], pv1_rden[:, b:b + 1],
                                                    self_scale[:], ALU.mult, ALU.mult)
                last.then_inc(S["pv1_steps"], 1)
                dve.wait_ge(S["pv1_steps"], at(g, "pv1_steps", 3))
                dve.wait_ge(S["skip"], at(g, "skip", 1))
                dve.tensor_tensor(x1[:], pv1_n, skip[:], ALU.add).then_inc(S["x1"], 1)
                yield "x1_turn"
                dve.wait_ge(S["a_turned"], at(g, "a_turned", 5))
                dve.tensor_scalar(x1_phi, bank["a_"][0][:], 0.0, None, ALU.min).then_inc(S["x1_min"], 1)
                dve.wait_ge(S["x1_exp"], at(g, "x1_exp", 1))
                dve.scalar_tensor_tensor(x1_phi, x1_phi, -1.0, bank["a_"][0][:], ALU.add, ALU.max)\
                    .then_inc(S["x1_phi"], 1)
                yield "linear"
                dve.wait_ge(S["num"], at(g, "num", 1))
                for i in range(2):
                    seqs, src = wide_bank(1, i)
                    dve.tensor_scalar(num_den[:, seqs], src[:, :, D], ATTN_EPS, None, ALU.add)\
                        .then_inc(S["num_steps"], 1)
                dve.wait_ge(S["num_steps"], at(g, "num_steps", 2))
                dve.reciprocal(num_rden[:], num_den[:]).then_inc(S["num_steps"], 1)
                dve.wait_ge(S["num_steps"], at(g, "num_steps", 3))
                for b in range(GROUP):
                    last = dve.scalar_tensor_tensor(l1_sum[:, b, :], wide(1, b)[:, 0:D], num_rden[:, b:b + 1],
                                                    x1[:, b, :], ALU.mult, ALU.add)
                last.then_inc(S["l1_sum"], 1)
                yield "l1_norm"
                dve.wait_ge(S["l1_sum"], at(g, "l1_sum", 1))
                normalise(g, "a_", LN_L1, lambda b: l1_sum[:, b, :], lambda b: fr.hat[:, b, :])
                dve.wait_ge(S["a_ln_hat"], at(g, "a_ln_hat", LN_L1 + 1))
                dve.tensor_tensor(l1_sum, fr.hat[:], row("l1_gamma"), ALU.mult).then_inc(S["l1_scaled"], 1)
                dve.wait_ge(S["l1_scaled"], at(g, "l1_scaled", 1))
                if g is not FIRST:
                    dve.wait_ge(S["moe_acc"], at(g, "moe_acc", 1 - PER["moe_acc"]))
                dve.tensor_tensor(fr.x_res[:], l1_sum, row("l1_beta"), ALU.add).then_inc(S["x2"], 1)
                yield "sa_norm"
                dve.wait_ge(S["x2"], at(g, "x2", 1))
                normalise_residual(g, "a_", LN_SA)
                yield from attention(g, "a_", SELF2)
                yield "caq_norm"
                dve.wait_ge(S["a_attn_sum"], at(g, "a_attn_sum", 1))
                normalise_residual(g, "a_", LN_CAQ)
                yield from attention(g, "a_", CROSS2)

            def front(g, ahead):
                yield from tail(g)
                yield from head(ahead)

            def back(g):
                yield "moe_norm"
                dve.wait_ge(S["a_attn_sum"], at(g, "a_attn_sum", 2))
                dve.wait_ge(S["out_ready"], at(g, "out_ready", 0))
                normalise(g, "b_", LN_MOE, lambda b: fr.x_res[:, b, :], lambda b: bk.hat[:, b, :])
                yield "moe_turn"
                dve.wait_ge(S["moe_hi"], at(g, "moe_hi", 1))
                dve.tensor_tensor(moe_lo, bk.feat[:], moe_hi, ALU.subtract).then_inc(S["moe_lo"], 1)
                yield "router"
                dve.wait_ge(S["router"], at(g, "router", 1))
                dve.tensor_tensor(logits[:], bank["b_"][3][:, 0:GROUP * EXPERTS].rearrange("q (b e) -> q b e", b=GROUP),
                                  router_b[:].unsqueeze(1).broadcast_to([P, GROUP, EXPERTS]), ALU.add)\
                    .then_inc(S["logits"], 1)
                dve.wait_ge(S["logits"], at(g, "logits", 1))
                dve.sem_inc(s_held, 1)
                for b in range(GROUP):
                    dve.max(top[:, b, :], logits[:, b, :]).then_inc(S["top"], 1)
                dve.wait_ge(S["top"], at(g, "top", GROUP))
                dve.sem_inc(s_held, 1)
                for b in range(GROUP):
                    dve.max_index(top_at[:, b, :], top[:, b, :], logits[:, b, :]).then_inc(S["top_at"], 1)
                dve.tensor_tensor(gap[:], top[:, :, 1], top[:, :, 0], ALU.subtract).then_inc(S["gap"], 1)
                dve.wait_ge(S["top_at"], at(g, "top_at", GROUP))
                dve.tensor_copy(top_f[:], top_at[:]).then_inc(S["gate_steps"], 1)
                dve.wait_ge(S["gap_exp"], at(g, "gap_exp", 1))
                dve.tensor_scalar(gap_den[:], gap_exp[:], 1.0, None, ALU.add).then_inc(S["gate_steps"], 1)
                dve.wait_ge(S["gate_steps"], at(g, "gate_steps", 2))
                dve.reciprocal(gate1[:], gap_den[:]).then_inc(S["gate_steps"], 1)
                dve.wait_ge(S["gate_steps"], at(g, "gate_steps", 3))
                dve.tensor_tensor(gate2[:], gap_exp[:], gate1[:], ALU.mult).then_inc(S["gate_steps"], 1)
                dve.wait_ge(S["gate_steps"], at(g, "gate_steps", 1))
                experts = expert_id[:].unsqueeze(1).broadcast_to([P, GROUP, EXPERTS])

                def each(ap):
                    return ap.unsqueeze(2).broadcast_to([P, GROUP, EXPERTS])

                for i in range(2):
                    dve.tensor_tensor(hot[i][:], experts, each(top_f[:, :, i]), ALU.is_equal).then_inc(S["gate_steps"], 1)
                dve.wait_ge(S["gate_steps"], at(g, "gate_steps", 6))
                dve.tensor_tensor(pick[0][:], hot[0][:], each(gate1[:]), ALU.mult).then_inc(S["gate_steps"], 1)
                dve.wait_ge(S["gate_steps"], at(g, "gate_steps", 4))
                dve.tensor_tensor(pick[1][:], hot[1][:], each(gate2[:]), ALU.mult).then_inc(S["gate_steps"], 1)
                dve.wait_ge(S["gate_steps"], at(g, "gate_steps", 8))
                dve.tensor_tensor(gates[:], pick[0][:], pick[1][:], ALU.add).then_inc(S["gates"], 1)
                yield "gates"
                dve.wait_ge(S["gate_bias"], at(g, "gate_bias", 1))
                dve.tensor_tensor(bk.x_res[:], bank["b_"][3][:].rearrange("q (b d) -> q b d", b=GROUP), fr.x_res[:],
                                  ALU.add).then_inc(S["moe_acc"], 1)
                for e in range(EXPERTS):
                    yield f"out{e}_1"
                    dve.wait_ge(S["fc2"], at(g, "fc2", e + 1))
                    dve.wait_ge(S["moe_acc"], at(g, "moe_acc", e + 1))
                    for b in range(GROUP):
                        last = dve.scalar_tensor_tensor(bk.x_res[:, b, :], bank["b_"][2 + e % 2][:, seq_tok(b)],
                                                        gates[:, b, e:e + 1], bk.x_res[:, b, :], ALU.mult, ALU.add)
                    last.then_inc(S["moe_acc"], 1)
                yield from attention(g, "b_", SELF3)
                yield "n31_norm"
                dve.wait_ge(S["b_attn_sum"], at(g, "b_attn_sum", 1))
                normalise_residual(g, "b_", LN_31)
                yield from attention(g, "b_", CROSS3)
                yield "n32_norm"
                dve.wait_ge(S["b_attn_sum"], at(g, "b_attn_sum", 2))
                normalise_residual(g, "b_", LN_32)
                yield "ffn_out"
                dve.wait_ge(S["ffn2"], at(g, "ffn2", 1))
                dve.wait_ge(S["b_residual"], at(g, "b_residual", 3))
                dve.tensor_tensor(bk.x_res[:], bank["b_"][3][:].rearrange("q (b d) -> q b d", b=GROUP), bk.residual[:],
                                  ALU.add).then_inc(S["ffn_sum"], 1)
                yield "result"
                dve.wait_ge(S["ffn_sum"], at(g, "ffn_sum", 1))
                normalise_residual(g, "b_", LN_33)

            dve.wait_ge(s_weights, weights_in)
            dve.wait_ge(s_fill, filled)
            r = {n: rows[:, i, :] for i, n in enumerate(ROWS)}
            dve.tensor_tensor(self_scale[:], r["gamma1"], r["gamma2"], ALU.mult).then_inc(s_const, 1)
            dve.wait_ge(s_const, 1)
            dve.tensor_tensor(x_shift[:], self_scale[:], r["norm3_b"], ALU.mult).then_inc(s_const, 1)
            dve.wait_ge(s_const, 2)
            dve.tensor_tensor(x_shift[:], x_shift[:], r["norm2_b"], ALU.add).then_inc(s_const, 1)
            dve.tensor_tensor(self_scale[:], self_scale[:], r["norm3_w"], ALU.mult).then_inc(s_const, 1)
            dve.tensor_tensor(shift31[:], r["be1"], r["bo_c"], ALU.add).then_inc(s_const, 1)
            dve.tensor_tensor(shift32[:], r["be2"], r["ffn_b2"], ALU.add).then_inc(s_const, 1)
            dve.wait_ge(s_const, 6)
            alone(head(FIRST))
            alone(tail(FIRST))
            alone(head(SECOND))
            dve.wait_ge(s_experts, experts_in)
            dve.wait_ge(s_split, 1)
            dve.tensor_tensor(moe_w1[1][:], w1_f32, moe_w1[0][:], ALU.subtract).then_inc(s_split, 1)
            with dve.Fori(0, steps - 1) as it:
                v = Values(dve, it)
                weave(front(Group(it, 1, v), Group(it, 2, v)), back(Group(it, 0, v)))
            alone(back(LAST))

        @block.tensor
        def _(pe):
            def turn(dst, src, n=P, width=P):
                for b in range(GROUP):
                    last = pe.transpose(dst[0:width, b * n:(b + 1) * n], src(b), ident[0:n, 0:n])
                return last

            def turn_hat(g, s, ln):
                pe.wait_ge(S[s + "ln_hat"], at(g, s + "ln_hat", ln + 1))
                turn(bank[s][2], lambda b: buf[s].hat[:, b, :]).then_inc(S[s + "turned"], 1)

            def attention(g, s, m, k_src, f):
                x, n, nk, ps = buf[s], m % 2, KEYS[m], bank[s]
                keys = GROUP * nk
                yield f"proj{m}"
                pe.wait_ge(S[s + "feat"], at(g, s + "feat", f + 1))
                pe.matmul(ps[3][:, 0:keys], mat(f"wk{m}"), k_src, start=True, stop=True)\
                    .then_inc(S[s + "k_proj"], 1)
                pe.matmul(ps[1][:], mat(f"wq{m}"), x.feat[:], start=True, stop=True).then_inc(S[s + "q_proj"], 1)
                for b in range(GROUP):
                    last = pe.matmul(ps[0][0:nk, b * D:(b + 1) * D], k_src[:, seq_keys(b, nk)], mat(f"wv{m}"),
                                     start=True, stop=True)
                last.then_inc(S[s + "v_proj"], 1)

                def scores(j, b):
                    u = GROUP * j + b
                    if u == 0:
                        pe.wait_ge(S[s + "v_sb"], at(g, s + "v_sb", n + 1))
                    elif j < LAG and u >= 2:
                        pe.wait_ge(S[s + "smax"], at(g, s + "smax", n * UNITS + u - 1))
                    elif j >= LAG:
                        pe.wait_ge(S[s + "smax"], at(g, s + "smax", n * UNITS + u))
                    if b == 0:
                        pe.wait_ge(S[f"{s}kq_shift{j}"], at(g, f"{s}kq_shift{j}", 32 * (n + 1)))
                        pe.wait_ge(S[s + "k_blk"], at(g, s + "k_blk", SLOTS * (TILES * n + j + 1)))
                    dst = score_bank(s, j, b)[:, 0:SLOTS * nk]
                    if CAUSAL[m]:
                        pe.matmul(dst, ident_bf[:], mask_q[:].rearrange("q i k -> q (i k)"), start=True, stop=False)
                    pe.matmul(dst, x.q_int[:, j, seq_tok(b)], x.k_blk[:, j, :, seq_keys(b, nk)],
                              start=not CAUSAL[m], stop=True).then_inc(S[s + "scores"], 1)

                def turn_max(j):
                    pe.wait_ge(S[s + "smax"], at(g, s + "smax", n * UNITS + GROUP * (j + 1)))
                    if j >= 1:
                        pe.wait_ge(S[s + "m_sb"], at(g, s + "m_sb", TILES * n + j))
                    if j > LAG:
                        pe.wait_ge(S[s + "o_norm"], at(g, s + "o_norm", TILES * n + j - LAG))
                    for b in range(GROUP):
                        last = pe.transpose(ps[3][0:32, b * T:(b + 1) * T],
                                            x.smax[:, b, 32 * j:32 * j + 32], ident[:])
                    last.then_inc(S[s + "m_t"], 1)

                def scores_t(j, b):
                    u = GROUP * j + b
                    if b == 0:
                        pe.wait_ge(S[f"{s}m_shift{j}"], at(g, f"{s}m_shift{j}", 16 * (n + 1)))
                    if u == 0:
                        pe.wait_ge(S[s + "smax"], at(g, s + "smax", n * UNITS + GROUP * LAG))
                    elif j < TILES - LAG:
                        pe.wait_ge(S[s + "probs"], at(g, s + "probs", n * UNITS + u))
                    else:
                        if u >= 2:
                            pe.wait_ge(S[s + "probs"], at(g, s + "probs", n * UNITS + u - 1))
                        if u == GROUP * (TILES - LAG):
                            pe.wait_ge(S[s + "smax"], at(g, s + "smax", (n + 1) * UNITS))
                    dst = weigh_bank(s, j, b)[0:nk, :]
                    if CAUSAL[m]:
                        pe.matmul(dst, ident_bf[:], mask_k[:].rearrange("k i q -> k (i q)"), start=True, stop=True)
                    for i in range(SLOTS):
                        last = pe.matmul(dst[:, i * T:(i + 1) * T], x.k_blk[:, j, i, seq_keys(b, nk)],
                                         x.q_int[:, j, seq_tok(b)], start=not CAUSAL[m], stop=True,
                                         skip_group_check=True)
                    last.then_inc(S[s + "scores_t"], 1)

                def weigh(j, b):
                    u = GROUP * j + b
                    if b == 0 and j >= 1:
                        pe.wait_ge(S[s + "o_sb"], at(g, s + "o_sb", TILES * n + j))
                    pe.wait_ge(S[s + "probs"], at(g, s + "probs", n * UNITS + u + 1))
                    for i in range(SLOTS):
                        last = pe.matmul(ps[2][VW * i:VW * i + VW, b * T:(b + 1) * T], x.v_pad[0:nk, b, SLOTS * j + i, :],
                                         x.probs[u % 2][0:nk, i * T:(i + 1) * T], start=True, stop=True)
                    last.then_inc(S[s + "pv"], 1)

                def turn_out(j):
                    pe.wait_ge(S[s + "o_sb"], at(g, s + "o_sb", TILES * n + j + 1))
                    pe.wait_ge(S[s + "m_sb"], at(g, s + "m_sb", TILES * n + min(j + LAG + 1, TILES)))
                    if j >= 1:
                        pe.wait_ge(S[s + "o_norm"], at(g, s + "o_norm", TILES * n + j))
                    for b in range(GROUP):
                        last = pe.transpose(ps[3][:, b * P:(b + 1) * P], x.o_sb[:, b * T:(b + 1) * T], ident[:])
                    last.then_inc(S[s + "o_t"], 1)

                for phase, j, b in attention_units(m):
                    yield phase
                    if phase.startswith("score"):
                        scores(j, b)
                    elif phase.startswith("max"):
                        turn_max(j)
                    else:
                        if (j, b) == (0, 0):
                            scores_t(0, 0)
                        if b + 1 < GROUP:
                            scores_t(j, b + 1)
                        elif j + 1 < TILES:
                            scores_t(j + 1, 0)
                        if j >= 1 and b == 1:
                            turn_out(j - 1)
                        weigh(j, b)
                yield f"out{m}"
                turn_out(TILES - 1)
                pe.wait_ge(S[s + "o_norm"], at(g, s + "o_norm", TILES * (n + 1)))
                turn(ps[2], lambda b: x.o_norm[:, b, :]).then_inc(S[s + "on_t"], 1)
                yield f"sum{m}"
                pe.wait_ge(S[s + "on_sb"], at(g, s + "on_sb", n + 1))
                for b in range(GROUP):
                    last = pe.matmul(ps[1][:, b * D:(b + 1) * D], x.feat[:, seq_tok(b)], mat(f"wo{m}"),
                                     start=True, stop=True)
                last.then_inc(S[s + "attn"], 1)

            def head(g):
                ps, feat = bank["a_"], fr.feat
                yield "ctx_turn"
                pe.wait_ge(S["a_ln_hat"], at(g, "a_ln_hat", LN_CTX + 1))
                turn(ps[2], lambda b: ctx_hat[:, b, :], C).then_inc(S["a_turned"], 1)
                turn(ps[3], lambda b: ctx_tok[:, b, 0:D], C).then_inc(S["a_turned"], 1)
                yield "x_turn"
                pe.wait_ge(S["a_feat"], at(g, "a_feat", F_CTX + 1))
                for b in range(GROUP):
                    last = pe.matmul(ps[1][0:C, 4 * b:4 * b + 4], norm1_f[:, seq_keys(b, C)], fc1_w[:],
                                     start=True, stop=True)
                last.then_inc(S["v0"], 1)
                turn_hat(g, "a_", LN_X)
                yield "scores0"
                pe.wait_ge(S["a_feat"], at(g, "a_feat", F_X + 1))
                for b in range(GROUP):
                    last = pe.matmul(ps[3][:, seq_keys(b, C)], feat[:, seq_tok(b)], norm1_f[:, seq_keys(b, C)],
                                     start=True, stop=True)
                last.then_inc(S["s0"], 1)
                pe.wait_ge(S["ctx_phi"], at(g, "ctx_phi", 1))
                for b in range(GROUP):
                    last = pe.matmul(wide(0, b), ctx_phi[:, b, :], ctx_tok[:, b, :], start=True, stop=True)
                last.then_inc(S["kv"], 1)

            def tail(g):
                ps, feat = bank["a_"], fr.feat
                yield "max0"
                pe.wait_ge(S["max0"], at(g, "max0", 1))
                pe.transpose(ps[2][0:GROUP, 0:P], max0[:], ident[:]).then_inc(S["max0_t"], 1)
                yield "scores0_t"
                pe.wait_ge(S["max0_sb"], at(g, "max0_sb", 1))
                for b in range(GROUP):
                    pe.matmul(ps[3][0:C, seq_tok(b)], norm1_f[:, seq_keys(b, C)], feat[:, seq_tok(b)],
                              start=True, stop=False)
                    last = pe.matmul(ps[3][0:C, seq_tok(b)], pick_seq[:, b, 0:C], max0_t[:], start=False, stop=True)
                last.then_inc(S["s0_t"], 1)
                yield "values0"
                pe.wait_ge(S["p0"], at(g, "p0", 1))
                pe.wait_ge(S["v0_sb"], at(g, "v0_sb", 1))
                for b in range(GROUP):
                    last = pe.matmul(ps[2][:, 5 * b:5 * b + 5], p0[:, seq_tok(b)], v0[:, b, :], start=True, stop=True)
                last.then_inc(S["hpre"], 1)
                yield "hidden0"
                pe.wait_ge(S["h"], at(g, "h", 1))
                turn(ps[2], lambda b: h[:, b, :], P, 5).then_inc(S["h_t"], 1)
                yield "cross"
                pe.wait_ge(S["h_t_sb"], at(g, "h_t_sb", 1))
                for b in range(GROUP):
                    last = pe.matmul(ps[3][:, seq_tok(b)], h_t[:, seq_tok(b)], fc2_aug[:], start=True, stop=True)
                last.then_inc(S["cross"], 1)
                yield "cross_turn"
                pe.wait_ge(S["a_ln_hat"], at(g, "a_ln_hat", LN_CROSS + 1))
                turn(ps[2], lambda b: cross_hat[:, b, 0:D]).then_inc(S["a_turned"], 1)
                yield "scores1"
                pe.wait_ge(S["a_feat"], at(g, "a_feat", F_CROSS + 1))
                pe.wait_ge(S["kv_sb"], at(g, "kv_sb", 2))
                for b in range(GROUP):
                    last = pe.matmul(ps[0][:, seq_tok(b)], feat[:, seq_tok(b)], feat[:, seq_tok(b)],
                                     start=True, stop=True)
                last.then_inc(S["s1"], 1)
                yield "max1"
                pe.wait_ge(S["max1"], at(g, "max1", 1))
                pe.transpose(ps[1][0:GROUP, 0:P], max1[:], ident[:]).then_inc(S["max1_t"], 1)
                yield "scores1_t"
                pe.wait_ge(S["max1_sb"], at(g, "max1_sb", 1))
                for b in range(GROUP):
                    pe.matmul(ps[0][:, seq_tok(b)], feat[:, seq_tok(b)], feat[:, seq_tok(b)], start=True, stop=False)
                    last = pe.matmul(ps[0][:, seq_tok(b)], pick_seq[:, b, :], max1_t[:], start=False, stop=True)
                last.then_inc(S["s1_t"], 1)
                yield "values1"
                pe.wait_ge(S["cross_g"], at(g, "cross_g", 1))
                pe.wait_ge(S["p1"], at(g, "p1", 1))
                for b in range(GROUP):
                    last = pe.matmul(wide(1, b), p1[:, seq_tok(b)], cross_hat[:, b, :], start=True, stop=True)
                last.then_inc(S["pv1"], 1)
                yield "x1_turn"
                pe.wait_ge(S["x1"], at(g, "x1", 1))
                turn(ps[0], lambda b: x1[:, b, :]).then_inc(S["a_turned"], 1)
                yield "linear"
                pe.wait_ge(S["x1_phi"], at(g, "x1_phi", 1))
                for b in range(GROUP):
                    last = pe.matmul(wide(1, b), x1_phi[:, seq_tok(b)], kv[:, b, :], start=True, stop=True)
                last.then_inc(S["num"], 1)
                yield "sa_turn"
                turn_hat(g, "a_", LN_SA)
                yield from attention(g, "a_", SELF2, feat[:], F_SA)
                yield "caq_turn"
                turn_hat(g, "a_", LN_CAQ)
                yield from attention(g, "a_", CROSS2, cakv_f[:], F_CAQ)

            def front(g, ahead):
                yield from tail(g)
                yield from head(ahead)

            def back(g):
                ps, feat = bank["b_"], bk.feat
                yield "moe_turn"
                turn_hat(g, "b_", LN_MOE)
                yield "router"
                pe.wait_ge(S["b_feat"], at(g, "b_feat", F_MOE + 1))
                for b in range(GROUP):
                    last = pe.matmul(ps[3][:, EXPERTS * b:EXPERTS * (b + 1)], feat[:, seq_tok(b)], router_w[:],
                                     start=True, stop=True)
                last.then_inc(S["router"], 1)

                def expert_in(e, half):
                    for c in (2 * half, 2 * half + 1):
                        k = CHUNKS * e + c
                        if k >= 2:
                            pe.wait_ge(S["gelu"], at(g, "gelu", k - 1))
                        pe.matmul(ps[c % 2][:], moe_w1[0][:, e, c, :], moe_hi, start=True, stop=False)
                        pe.matmul(ps[c % 2][:], moe_w1[0][:, e, c, :], moe_lo, start=False, stop=False)
                        pe.matmul(ps[c % 2][:], moe_w1[1][:, e, c, :], moe_hi, start=False, stop=True)\
                            .then_inc(S["fc1"], 1)

                def expert_out(e, half):
                    if half == 0:
                        pe.wait_ge(S["moe_acc"], at(g, "moe_acc", max(e, 1)))
                        pe.wait_ge(S["gelu"], at(g, "gelu", CHUNKS * (e + 1)))
                    for b in (2 * half, 2 * half + 1):
                        for c in range(CHUNKS):
                            last = pe.matmul(ps[2 + e % 2][:, seq_tok(b)], hidden[e % 2][:, c, seq_tok(b)],
                                             moe_w2[:, e, c, :], start=(c == 0), stop=(c == CHUNKS - 1))
                    if half == 1:
                        last.then_inc(S["fc2"], 1)

                for e in range(EXPERTS):
                    for half in range(2):
                        yield f"in{e}_{half}"
                        if e == 0 and half == 0:
                            pe.wait_ge(S["moe_lo"], at(g, "moe_lo", 1))
                        expert_in(e, half)
                    if e == 0:
                        yield "gates"
                        pe.wait_ge(S["gates"], at(g, "gates", 1))
                        turn(ps[2], lambda b: gates[:, b, :], P, EXPERTS).then_inc(S["gates_t"], 1)
                        pe.wait_ge(S["gates_sb"], at(g, "gates_sb", 1))
                        for b in range(GROUP):
                            last = pe.matmul(ps[3][:, seq_tok(b)], gates_t[:, seq_tok(b)], moe_b2[:],
                                             start=True, stop=True)
                        last.then_inc(S["gate_bias"], 1)
                    else:
                        for half in range(2):
                            yield f"out{e - 1}_{half}"
                            expert_out(e - 1, half)
                for half in range(2):
                    yield f"out{EXPERTS - 1}_{half}"
                    expert_out(EXPERTS - 1, half)
                yield "l3_turn"
                pe.wait_ge(S["moe_acc"], at(g, "moe_acc", EXPERTS + 1))
                turn(ps[2], lambda b: bk.x_res[:, b, :]).then_inc(S["b_turned"], 1)
                yield from attention(g, "b_", SELF3, feat[:], F_L3)
                yield "n31_turn"
                turn_hat(g, "b_", LN_31)
                pe.wait_ge(S["ctx_kept"], at(g, "ctx_kept", 1))
                yield from attention(g, "b_", CROSS3, ctx_kept[:], F_31)
                yield "n32_turn"
                turn_hat(g, "b_", LN_32)
                yield "ffn_in"
                pe.wait_ge(S["b_feat"], at(g, "b_feat", F_32 + 1))
                for c in range(CHUNKS):
                    if c >= 2:
                        pe.wait_ge(S["ffn_relu"], at(g, "ffn_relu", c - 1))
                    pe.matmul(ps[c % 2][:], ffn_w1[:, c, :], feat[:], start=True, stop=True).then_inc(S["ffn1"], 1)
                yield "ffn_out"
                pe.wait_ge(S["ffn_relu"], at(g, "ffn_relu", CHUNKS))
                for b in range(GROUP):
                    for c in range(CHUNKS):
                        last = pe.matmul(ps[3][:, seq_tok(b)], hidden[0][:, c, seq_tok(b)], ffn_w2[:, c, :],
                                         start=(c == 0), stop=(c == CHUNKS - 1))
                last.then_inc(S["ffn2"], 1)

            pe.wait_ge(s_weights, weights_in)
            pe.wait_ge(s_fill, filled)
            pe.wait_ge(s_select, selects)
            alone(head(FIRST))
            alone(tail(FIRST))
            alone(head(SECOND))
            pe.wait_ge(s_experts, experts_in)
            pe.wait_ge(s_split, 2)
            with pe.Fori(0, steps - 1) as it:
                v = Values(pe, it)
                weave(front(Group(it, 1, v), Group(it, 2, v)), back(Group(it, 0, v)))
            alone(back(LAST))


def laid_out(inputs):
    import numpy as np

    def get(name):
        return np.asarray(inputs[name])

    def l0(n):
        return get(f"L0_xattn_{n}")

    def l1(n):
        return get(f"L1_xattn_{n}")

    def l2(n):
        return get(f"L2_xattn_{n}")

    def l3(n):
        return get(f"L3_xattn_{n}")

    f32 = np.float32
    col = {n: l0(n) for n in ("norm1_w", "norm1_b", "norm2_w", "norm2_b", "norm3_w", "norm3_b")}
    col |= {"sa_g": l2("sa_ln_g"), "sa_b": l2("sa_ln_b"), "caq_g": l2("ca_q_ln_g"), "caq_b": l2("ca_q_ln_b"),
            "cakv_g": l2("ca_kv_ln_g"), "cakv_b": l2("ca_kv_ln_b"), "moe_g": l2("moe_ln_g"), "moe_b": l2("moe_ln_b"),
            "g1": l3("g1"), "be1": l3("be1"), "g2": l3("g2"), "be2": l3("be2")}
    mat = {}
    for m, n in ((SELF2, "sa"), (CROSS2, "ca")):
        for k, w in enumerate("qkv"):
            mat[f"w{w}{m}"] = l2(f"{n}_in_w")[k * D:(k + 1) * D].T
            col[f"b{w}{m}"] = l2(f"{n}_in_b")[k * D:(k + 1) * D]
        mat[f"wo{m}"] = l2(f"{n}_out_w").T
    for m, n in ((SELF3, "s"), (CROSS3, "c")):
        for w in "qkv":
            mat[f"w{w}{m}"] = l3(f"W{w}_{n}").transpose(1, 0, 2).reshape(D, D)
            col[f"b{w}{m}"] = l3(f"b{w}_{n}").reshape(D)
        mat[f"wo{m}"] = l3(f"Wo_{n}")
    for c in range(CHUNKS):
        col[f"ffn_b1_{c}"] = l3("b1")[c * P:(c + 1) * P]
        for e in range(EXPERTS):
            col[f"moe_b1_{e}_{c}"] = l2("e_fc1_b")[e, c * P:(c + 1) * P]
    row = {n: l0(n) for n in ("norm2_w", "norm2_b", "gamma1", "gamma2", "norm3_w", "norm3_b")}
    row |= {"l1_gamma": l1("gamma"), "l1_beta": l1("beta"), "sa_out_b": l2("sa_out_b"), "ca_out_b": l2("ca_out_b"),
            "bo_s": l3("bo_s"), "bo_c": l3("bo_c"), "ffn_b2": l3("b2"), "g1": l3("g1"), "be1": l3("be1"),
            "g2": l3("g2"), "be2": l3("be2"), "g3": l3("g3"), "be3": l3("be3")}

    def groups(x):
        x = x.reshape(-1, GROUP, *x.shape[1:])
        return np.concatenate([x, np.zeros_like(x[:AHEAD])])

    def repeat(v):
        return np.broadcast_to(v, (P, *v.shape))

    feature = np.arange(P) // PARTS
    arrays = {
        "x": groups(get("x")), "ctx": groups(get("ctx_1024")),
        "cols": np.stack([col[n] for n in COLS], 1),
        "rows": repeat(np.stack([row[n] for n in ROWS])),
        "mats": np.stack([mat[n] for n in MATS], 1),
        "fc1_w": l0("fc1_w").T, "fc1_b": repeat(l0("fc1_b")),
        "fc2_aug": np.concatenate([l0("fc2_w").T, l0("fc2_b")[None]]),
        "router_w": l2("router_w").T, "router_b": repeat(l2("router_b")),
        "moe_w1": l2("e_fc1_w").reshape(EXPERTS, CHUNKS, P, D).transpose(3, 0, 1, 2),
        "moe_w2": l2("e_fc2_w").reshape(EXPERTS, D, CHUNKS, P).transpose(3, 0, 2, 1),
        "moe_b2": l2("e_fc2_b"),
        "ffn_w1": l3("W1").reshape(D, CHUNKS, P),
        "ffn_w2": l3("W2").reshape(CHUNKS, P, D).transpose(1, 0, 2),
        "slot_mask": (feature[:, None] // DH == np.arange(SLOTS)).astype(f32),
        "expert_id": repeat(np.arange(EXPERTS, dtype=f32)),
        "pick_seq": np.repeat(np.eye(GROUP, dtype=f32)[:, :, None], T, 2),
    }
    return {n: np.ascontiguousarray(v) for n, v in arrays.items()}


def kernel(**inputs):
    import concourse.bacc as bacc
    from concourse.bass_utils import run_bass_kernel_spmd
    arrays = laid_out(inputs)
    nc = bacc.Bacc("TRN2", target_bir_lowering=False, num_devices=1)
    aps = {n: nc.dram_tensor(f"in_{n}", v.shape, mybir.dt.from_np(v.dtype), kind="ExternalInput").ap()
           for n, v in arrays.items()}
    steps = arrays["x"].shape[0] - AHEAD
    out = nc.dram_tensor("out", (steps, GROUP, T, D), F32, kind="ExternalOutput").ap()
    build(nc, aps, out, steps)
    r = run_bass_kernel_spmd(nc, [{f"in_{n}": v for n, v in arrays.items()}], core_ids=[0])
    return r.results[0]["out"].reshape(-1, T, D)
```

```python
from contextlib import ExitStack

import concourse.bass as bass
from concourse import mybir

F32 = mybir.dt.float32
F16 = mybir.dt.float16
BF16 = mybir.dt.bfloat16
U32 = mybir.dt.uint32
ACT = mybir.ActivationFunctionType
ALU = mybir.AluOpType
AX = mybir.AxisListType

P = 128
D = 128
T = 128
C = 77
GROUP = 4
N = GROUP * T
HEADS = 16
DH = D // HEADS
SLOTS = 4
PARTS = 4
TILES = HEADS // SLOTS
VW = 32
EXPERTS = 8
CHUNKS = 4
LN_EPS = 1e-5
ATTN_EPS = 1e-6
MAX_SCALE = 256.0
MASKED = -1e30
AHEAD = 2
RING = 36

COLS = ["norm1_w", "norm1_b", "norm2_w", "norm2_b", "norm3_w", "norm3_b", "sa_g", "sa_b", "caq_g", "caq_b",
        "cakv_g", "cakv_b", "moe_g", "moe_b", "g1", "be1", "g2", "be2"]
COLS += [f"b{w}{m}" for m in range(4) for w in "qkv"]
COLS += [f"ffn_b1_{c}" for c in range(CHUNKS)] + [f"moe_b1_{e}_{c}" for e in range(EXPERTS) for c in range(CHUNKS)]
ROWS = ["norm2_w", "norm2_b", "gamma1", "gamma2", "norm3_w", "norm3_b", "l1_gamma", "l1_beta",
        "sa_out_b", "ca_out_b", "bo_s", "bo_c", "ffn_b2", "g1", "be1", "g2", "be2", "g3", "be3"]
MATS = [f"w{w}{m}" for m in range(4) for w in "qkvo"]


SELF2, CROSS2, SELF3, CROSS3 = range(4)
KEYS = [T, C, T, C]
CAUSAL = [False, False, True, False]
LAG = 2
EARLY = 2
UNITS = GROUP * TILES

LN_CTX, LN_X, LN_MOE_BEFORE, LN_CROSS, LN_L1, LN_SA, LN_CAQ, _, _, LN_MOE = range(10)
LN_31, LN_32, LN_33 = range(3)
F_CTX, F_RAW, F_X, F_CROSS, F_SA, F_CAQ, F_MOE = range(7)
F_L3, F_31, F_32 = range(3)

def attention_units(m):
    for t in range(TILES + LAG):
        for b in range(GROUP):
            if t < TILES:
                yield f"score{m}_{t}_{b}", t, b
            if t >= LAG:
                yield f"weigh{m}_{t - LAG}_{b}", t - LAG, b
        if t < TILES:
            yield f"max{m}_{t}", t, 0


def attention_phases(m):
    return ([f"proj{m}", f"query{m}", f"value{m}"] + [p for p, _, _ in attention_units(m)] +
            [f"out{m}", f"norm{m}", f"sum{m}"])


def experts():
    for e in range(EXPERTS + 1):
        if e < EXPERTS:
            yield from (f"in{e}_0", f"in{e}_1")
        yield from ("gates",) if e == 0 else (f"out{e - 1}_0", f"out{e - 1}_1")


FRONT = ["max0", "scores0_t", "values0", "hidden0", "cross", "cross_hat", "cross_turn", "scores1", "max1", "scores1_t",
         "values1", "x1_turn", "x1_elu", "linear", "l1_norm", "l1_hat", "sa_norm", "sa_hat", "sa_turn",
         *attention_phases(SELF2), "caq_norm", "caq_hat", "caq_turn", *attention_phases(CROSS2),
         "moe_norm", "moe_hat", "moe_turn", "router", "gate", "ctx_turn", "x_turn", "scores0"]
NORMS = ["ctx_norm", "ctx_hat", "x_norm", "x_hat", "ctx_elu"]
BACK = [*experts(), "l3_turn", *attention_phases(SELF3), "n31_norm", "n31_hat", "n31_turn",
        *attention_phases(CROSS3), "n32_norm", "n32_hat", "n32_turn", "ffn_in", "ffn_out", "result", "result_hat"]
TURNS = ("fbbbbfbbffbfbfbbbfbfbbfbbfbfbbbfbbfffbbfbbfbfbbbfbffbbfbffbbfffffffbbffbfbfbfffbbfbfbfbffbfbbbfffbfb"
         "bfbbbfbfbfbffbfffbbbffbfbbbbbbbbbfbbffbfbbfffbbfbfbffbbffffffffbfbfbbffbffbbfbbbffbbffbffbfbbffnbbfb"
         "fffnbnffnfbbbfbbffbnbbbbfbbfbbbbfbbbfbfffbfbfbb")


def common_order():
    upcoming = {"f": iter(FRONT), "n": iter(NORMS), "b": iter(BACK)}
    return [next(upcoming[turn]) for turn in TURNS]


ORDER = common_order()


def weave(*streams):
    upcoming = [next(s, None) for s in streams]
    for phase in ORDER:
        for i, s in enumerate(streams):
            if upcoming[i] == phase:
                upcoming[i] = next(s, None)


def alone(stream):
    for _ in stream:
        pass


STREAM = dict(
    k_proj=2, q_proj=2, v_proj=2, k_hi=2, q_hi=2, v_sb=2, k_split=4, q_split=4,
    k_blk=2 * SLOTS * EARLY, k_blk_late=2 * SLOTS * (TILES - EARLY),
    scores=2 * UNITS, smax=2 * UNITS, m_t=8, m_sb=8, scores_t=2 * UNITS, probs=2 * UNITS, pv=2 * UNITS,
    k_shift0=2 * 16, q_shift0=2 * 16, o_sb=8, o_t=8, o_rden=8, o_norm=8, on_t=2, on_sb=2, attn=2, attn_sum=2,

) | {f"kq_shift{j}": 2 * 32 for j in range(1, TILES)} | {f"m_shift{j}": 2 * 16 for j in range(TILES)}
PER = {s + n: c for s in ("a_", "b_") for n, c in STREAM.items()}
PER |= dict(
    a_ln_stats=28, a_ln_mean=28, a_ln_var=7, a_ln_rstd=7, a_ln_hat=7, a_turned=8, a_feat=7, a_residual=2,
    b_ln_stats=12, b_ln_mean=12, b_ln_var=3, b_ln_rstd=3, b_ln_hat=3, b_turned=3, b_feat=3, b_residual=3,
    x_in=16, ctx_in=16, out_stored=16, ctx_kept=1,
    ctx_min=1, ctx_exp=1, ctx_phi=1, v0=1, v0_sb=1, kv=1, kv_sb=2,
    s0=1, max0=1, max0_t=1, max0_sb=1, s0_t=1, p0=1, hpre=1, h_steps=2, h_in=1, h=1, h_t=1, h_t_sb=1,
    cross=1, cross_g=1, s1=1, max1=1, max1_t=1, max1_sb=1, s1_t=1, p1=1, pv1=1, pv1_steps=3, x1=1,
    x_steps=2, skip=1,
    x1_min=1, x1_exp=1, x1_phi=1, num=1, num_steps=3, l1_steps=2, x2=1,
    res_scaled=3, moe_hi=1, moe_lo=1, router=1, logits=1, top=4, top_at=4, gap=1, gap_exp=1, gate_steps=8,
    gates=1, gates_t=1, gates_sb=1, gate_bias=1, fc1=32, gelu=32, fc2=8, moe_acc=9,
    ffn1=4, ffn_relu=4, ffn2=1, ffn_sum=1, out_ready=1,
)
START = dict(out_ready=1, ffn_sum=1, out_stored=16)


def build(nc, a, out, steps):
    with ExitStack() as ctx:
        def sb(name, shape, dt=F32):
            return ctx.enter_context(nc.sbuf_tensor(name, shape, dt))

        S = {n: ctx.enter_context(nc.semaphore(n)) for n in PER}
        s_weights = ctx.enter_context(nc.semaphore("weights_in"))
        s_experts = ctx.enter_context(nc.semaphore("experts_in"))
        s_fill = ctx.enter_context(nc.semaphore("filled"))
        s_held = ctx.enter_context(nc.semaphore("held"))
        s_split = ctx.enter_context(nc.semaphore("w1_split"))
        s_const = ctx.enter_context(nc.semaphore("row_constants"))
        FIRST = (0, 0)

        class Values:
            def __init__(self, eng, it):
                self.eng, self.it, self.base = eng, it, {}
                self.ring = [[None, eng.alloc_register(f"count{i}")] for i in range(RING)]

            def get(self, per, count):
                if per not in self.base:
                    self.base[per] = self.eng.alloc_register(f"step_x{per}")
                    self.eng.reg_mul(self.base[per], self.it, per)
                for k, (key, reg) in enumerate(self.ring):
                    if key == (per, count):
                        self.ring.append(self.ring.pop(k))
                        return reg
                _, reg = self.ring.pop(0)
                self.ring.append([(per, count), reg])
                self.eng.reg_add(reg, self.base[per], count)
                return reg

        class Group:
            def __init__(self, step, lead=0, values=None):
                self.step, self.lead, self.values = step, lead, values

        FIRST = Group(0)
        SECOND = Group(1)
        LAST = Group(steps - 1)

        def at(g, name, count):
            count += g.lead * PER[name] + START.get(name, 0)
            return g.values.get(PER[name], count) if g.values else g.step * PER[name] + count

        bank = {s: [ctx.enter_context(nc.psum_tensor(f"{s}bank{i}", [P, 512], F32)) for i in range(4)]
                for s in ("a_", "b_")}

        cols = sb("cols", [P, len(COLS)])
        rows = sb("rows", [P, len(ROWS), D])
        mats = sb("mats", [P, len(MATS), D])
        fc1_w = sb("fc1_w", [P, 4])
        fc1_b = sb("fc1_b", [P, 4])
        fc2_aug = sb("fc2_aug", [5, D])
        router_w = sb("router_w", [P, EXPERTS])
        router_b = sb("router_b", [P, EXPERTS])
        moe_w1 = [sb(f"moe_w1_{i}", [P, EXPERTS, CHUNKS, P], F16) for i in ("hi", "lo")]
        moe_w2 = sb("moe_w2", [P, EXPERTS, CHUNKS, D])
        moe_b2 = sb("moe_b2", [EXPERTS, D])
        ffn_w1 = sb("ffn_w1", [P, CHUNKS, P])
        ffn_w2 = sb("ffn_w2", [P, CHUNKS, D])
        slot_mask = sb("slot_mask", [P, SLOTS])
        expert_id = sb("expert_id", [P, EXPERTS])
        pick_seq = sb("pick_seq", [GROUP, GROUP, T])
        ident = sb("ident", [P, P])
        ident_bf = sb("ident_bf", [P, P], BF16)
        mask_q = sb("mask_q", [P, SLOTS, T], BF16)
        mask_k = sb("mask_k", [P, SLOTS, T], BF16)
        ln_eps = sb("ln_eps", [P, GROUP])
        minus_half = sb("minus_half", [P, GROUP])
        self_scale = sb("self_scale", [P, D])
        x_shift = sb("x_shift", [P, D])
        shift31 = sb("shift31", [P, D])
        shift32 = sb("shift32", [P, D])

        def col(name):
            i = COLS.index(name)
            return cols[:, i:i + 1]

        def row(name):
            return rows[:, ROWS.index(name), :].unsqueeze(1).broadcast_to([P, GROUP, D])

        def shifted(t):
            return t[:].unsqueeze(1).broadcast_to([P, GROUP, D])

        def mat(name):
            return mats[:, MATS.index(name), :]

        class Buffers:
            def __init__(self, s):
                self.stats = sb(s + "stats", [P, GROUP, 6])
                self.mean_var = sb(s + "mean_var", [P, GROUP, 2])
                self.rstd = sb(s + "rstd", [P, GROUP])
                self.var_eps = sb(s + "var_eps", [P, GROUP])
                self.hat = sb(s + "hat", [P, GROUP, D])
                self.feat = sb(s + "feat", [P, N])
                self.x_res = sb(s + "x_res", [P, GROUP, D])
                self.residual = sb(s + "residual", [P, GROUP, D])
                self.k_nat = sb(s + "k_nat", [P, PARTS, N], F16)
                self.q_nat = sb(s + "q_nat", [P, PARTS, N], F16)
                self.k_int = sb(s + "k_int", [P, TILES, N], F16)
                self.q_int = sb(s + "q_int", [P, TILES, N], F16)
                self.k_blk = sb(s + "k_blk", [P, TILES, SLOTS, N], F16)
                self.v_pad = sb(s + "v_pad", [P, GROUP, HEADS, VW])
                self.smax = sb(s + "smax", [P, GROUP, P])
                self.m_nat = sb(s + "m_nat", [P, N], F16)
                self.probs = [sb(f"{s}probs{i}", [P, SLOTS * T]) for i in range(2)]
                self.o_sb = sb(s + "o_sb", [P, TILES * T])
                self.o_rden = sb(s + "o_rden", [P, TILES, GROUP, SLOTS])
                self.o_norm = sb(s + "o_norm", [P, GROUP, D])

        buf = {s: Buffers(s) for s in ("a_", "b_")}
        fr, bk = buf["a_"], buf["b_"]

        x_tok = sb("x_tok", [P, GROUP, D])
        x_hat = sb("x_hat", [P, GROUP, D])
        ctx_tok = sb("ctx_tok", [C, GROUP, D + 1])
        work = fr.k_blk[:].bitcast(F32).rearrange("p j i n -> p (j i) n")
        assert work.shape[2] == N // 2
        work = [work[:, 2 * i:2 * i + 2, :].rearrange("p i n -> p (i n)") for i in range(8)]

        def by_seq(ap, n=P):
            return ap.rearrange("p (b d) -> p b d", b=GROUP)[0:n]

        ctx_hat = by_seq(work[0], C)
        ctx_phi = by_seq(work[1], C)
        p0 = work[2][0:C, :]
        h_t = work[3][0:5, :]
        p1 = work[4]
        x1_phi = work[5]
        l1_sum = by_seq(work[6])
        pv1_n = by_seq(work[7])
        norm1_f = sb("norm1_f", [P, GROUP * C])
        cakv_f = sb("cakv_f", [P, GROUP * C])
        ctx_f = sb("ctx_f", [P, GROUP * C])
        v0 = sb("v0", [C, GROUP, 5])
        kv = sb("kv", [P, GROUP, D + 1])
        max0 = sb("max0", [P, GROUP])
        max0_t = sb("max0_t", [GROUP, P])
        h_rden = sb("h_rden", [P, GROUP])
        h_mul = sb("h_mul", [P, GROUP, 4])
        h_in = sb("h_in", [P, GROUP, 4])
        h = sb("h", [P, GROUP, 5])
        cross_g = sb("cross_g", [P, GROUP, D])
        cross_hat = sb("cross_hat", [P, GROUP, D + 1])
        max1 = sb("max1", [P, GROUP])
        max1_t = sb("max1_t", [GROUP, P])
        pv1_rden = sb("pv1_rden", [P, GROUP])
        skip = sb("skip", [P, GROUP, D])
        x1 = sb("x1", [P, GROUP, D])
        num_den = sb("num_den", [P, GROUP])
        num_rden = sb("num_rden", [P, GROUP])
        ctx_kept = sb("ctx_kept", [P, GROUP * C])
        logits = sb("logits", [P, GROUP, EXPERTS])
        top = sb("top", [P, GROUP, 8])
        top_at = sb("top_at", [P, GROUP, 8], U32)
        top_f = sb("top_f", [P, GROUP, 8])
        gap = sb("gap", [P, GROUP])
        gap_exp = sb("gap_exp", [P, GROUP])
        gap_den = sb("gap_den", [P, GROUP])
        gate1 = sb("gate1", [P, GROUP])
        gate2 = sb("gate2", [P, GROUP])
        hot = [sb(f"hot{i}", [P, GROUP, EXPERTS]) for i in range(2)]
        pick = [sb(f"pick{i}", [P, GROUP, EXPERTS]) for i in range(2)]
        gates = sb("gates", [P, GROUP, EXPERTS])
        gates_t = bk.o_sb[0:EXPERTS, :]
        hid = bk.k_blk[:].bitcast(F32).rearrange("p j i n -> p (j i n)").rearrange("p (e c n) -> p e c n", e=2, c=CHUNKS)
        hidden = [hid[:, i] for i in range(2)]
        w1_f32 = bk.k_blk[:].bitcast(F32).rearrange("p j i n -> p (j i n)")\
            .rearrange("p (e c f) -> p e c f", e=EXPERTS, c=CHUNKS)
        moe_hi, moe_lo = bk.q_nat[:, 0, :], bk.q_nat[:, 1, :]
        out_tok = sb("out_tok", [P, GROUP, D])

        loads = [(cols[:], a["cols"]), (fc1_w[:], a["fc1_w"]), (rows[:], a["rows"]), (mats[:], a["mats"]),
                 (fc1_b[:], a["fc1_b"]), (fc2_aug[:], a["fc2_aug"]), (pick_seq[:], a["pick_seq"]),
                 (slot_mask[:], a["slot_mask"])]
        expert_loads = [(router_w[:], a["router_w"]), (router_b[:], a["router_b"]), (expert_id[:], a["expert_id"]),
                        (moe_b2[:], a["moe_b2"]), (w1_f32, a["moe_w1"]), (moe_w2[:], a["moe_w2"]),
                        (ffn_w1[:], a["ffn_w1"]), (ffn_w2[:], a["ffn_w2"])]
        weights_in = 16 * len(loads)
        experts_in = 16 * len(expert_loads)
        fills = [(ident[:], 0.0), (ident_bf[:], 0.0), (mask_q[:], 0.0), (mask_k[:], 0.0),
                 (ctx_tok[:, :, D:], 1.0), (v0[:, :, 4:], 1.0), (h[:, :, 4:], 1.0), (cross_hat[:, :, D:], 1.0),
                 (ln_eps[:], LN_EPS), (minus_half[:], -0.5)]
        for x in (fr, bk):
            fills += [(x.k_nat[:, 3, :], MAX_SCALE), (x.q_nat[:, 3, :], 0.0), (x.v_pad[:], 0.0), (x.smax[:], 0.0)]
        filled = len(fills) + 2 + 4

        block = ctx.enter_context(nc.Block())

        def seq_keys(b, nk):
            return slice(b * nk, (b + 1) * nk)

        def seq_tok(b):
            return slice(b * T, (b + 1) * T)

        def wide(s, b):
            first = 2 if s else 0
            return bank["a_"][first + b // 3][:, (D + 1) * (b % 3):(D + 1) * (b % 3 + 1)]

        def wide_bank(s, i):
            n = (3, 1)[i]
            first = 2 if s else 0
            return slice(3 * i, 3 * i + n), bank["a_"][first + i][:, 0:n * (D + 1)].rearrange("p (b e) -> p b e", b=n)

        def score_bank(s, j, b):
            return bank[s][2 - (GROUP * j + b) % 3 if j < LAG else 0]

        def weigh_bank(s, j, b):
            return bank[s][b % 2 if j >= TILES - LAG else 1]

        @block.sync
        def _(sp):
            sp.dma_start(ctx_tok[:, :, 0:D], a["ctx"][0].rearrange("b t d -> t b d")).then_inc(S["ctx_in"], 16)
            sp.dma_start(x_tok[:], a["x"][0].rearrange("b t d -> t b d")).then_inc(S["x_in"], 16)
            for dst, src in loads:
                sp.dma_start(dst, src).then_inc(s_weights, 16)
            for dst, src in expert_loads:
                sp.dma_start(dst, src).then_inc(s_experts, 16)

            def attention(g, s, m):
                x, n, keys = buf[s], m % 2, GROUP * KEYS[m]
                yield f"proj{m}"
                sp.wait_ge(S[s + "k_split"], at(g, s + "k_split", 2 * (n + 1)))
                sp.dma_start(x.k_int[:, 0, 0:keys], x.k_nat[0:32, :, 0:keys]).then_inc(S[s + "k_shift0"], 16)
                yield f"query{m}"
                sp.wait_ge(S[s + "q_split"], at(g, s + "q_split", 2 * (n + 1)))
                sp.dma_start(x.q_int[:, 0, :], x.q_nat[0:32, :, :]).then_inc(S[s + "q_shift0"], 16)
                for j in range(1, TILES):
                    sp.dma_start(x.k_int[:, j, 0:keys],
                                 x.k_nat[32 * j:32 * j + 32, :, 0:keys]).then_inc(S[f"{s}kq_shift{j}"], 16)
                    sp.dma_start(x.q_int[:, j, :],
                                 x.q_nat[32 * j:32 * j + 32, :, :]).then_inc(S[f"{s}kq_shift{j}"], 16)
                for j in range(TILES):
                    yield f"max{m}_{j}"
                    sp.wait_ge(S[s + "m_sb"], at(g, s + "m_sb", TILES * n + j + 1))
                    sp.dma_start(x.q_int[3::4, j, :], x.m_nat[32 * j:32 * j + 32, :])\
                        .then_inc(S[f"{s}m_shift{j}"], 16)

            def head(g):
                yield "scores0"
                sp.wait_ge(S["kv"], at(g, "kv", 1))
                sp.dma_start(ctx_tok[:, :, 0:D],
                             a["ctx"][g.step + g.lead + 1].rearrange("b t d -> t b d")).then_inc(S["ctx_in"], 16)
                sp.dma_start(x_tok[:], a["x"][g.step + g.lead + 1].rearrange("b t d -> t b d")).then_inc(S["x_in"], 16)

            def tail(g):
                yield from attention(g, "a_", SELF2)
                yield from attention(g, "a_", CROSS2)

            def front(g, ahead):
                yield from tail(g)
                yield from head(ahead)

            def back(g):
                yield from attention(g, "b_", SELF3)
                yield from attention(g, "b_", CROSS3)
                yield "result"
                sp.wait_ge(S["out_ready"], at(g, "out_ready", 1))
                sp.dma_start(out[g.step].rearrange("b t d -> t b d"), out_tok[:]).then_inc(S["out_stored"], 16)

            sp.sem_inc(S["out_stored"], START["out_stored"])
            alone(head(FIRST))
            weave(front(FIRST, SECOND))
            with sp.Fori(0, steps - 1) as it:
                v = Values(sp, it)
                weave(front(Group(it, 1, v), Group(it, 2, v)), back(Group(it, 0, v)))
            alone(back(LAST))
            sp.wait_ge(S["out_stored"], START["out_stored"] + 16 * steps)
            sp.wait_ge(S["x_in"], 16 * (steps + 2))
            sp.wait_ge(S["ctx_in"], 16 * (steps + 2))

        @block.gpsimd
        def _(pool):
            for ap, value in fills:
                pool.memset(ap, value).then_inc(s_fill, 1)
            pool.wait_ge(s_fill, len(fills))
            for x in (fr, bk):
                pool.memset(x.v_pad[:, :, :, DH:DH + 1], 1.0).then_inc(s_fill, 1)
            for m in (ident, ident_bf):
                pool.affine_select(out=m[:], in_=m[:], compare_op=ALU.not_equal, fill=1.0, base=0,
                                   pattern=[[-1, P]], channel_multiplier=1).then_inc(s_fill, 1)
            pool.affine_select(out=mask_q[:], in_=mask_q[:], compare_op=ALU.is_ge, fill=MASKED, base=0,
                               pattern=[[0, SLOTS], [-1, T]], channel_multiplier=1).then_inc(s_fill, 1)
            pool.affine_select(out=mask_k[:], in_=mask_k[:], compare_op=ALU.is_ge, fill=MASKED, base=0,
                               pattern=[[0, SLOTS], [1, T]], channel_multiplier=-1).then_inc(s_fill, 1)

            def root(g, s, n, p=P):
                x = buf[s]
                pool.wait_ge(S[s + "ln_mean"], at(g, s + "ln_mean", GROUP * (n + 1)))
                pool.tensor_tensor(x.var_eps[0:p, :], x.mean_var[0:p, :, 1], ln_eps[0:p, :], ALU.add)\
                    .then_inc(S[s + "ln_var"], 1)
                pool.wait_ge(S[s + "ln_var"], at(g, s + "ln_var", n + 1))
                pool.tensor_tensor(x.rstd[0:p, :], x.var_eps[0:p, :], minus_half[0:p, :], ALU.pow)\
                    .then_inc(S[s + "ln_rstd"], 1)

            def norms(g):
                yield "ctx_norm"
                root(g, "a_", LN_CTX, C)
                yield "x_norm"
                root(g, "a_", LN_X)
                yield "ctx_elu"
                pool.wait_ge(S["a_ln_hat"], at(g, "a_ln_hat", LN_X + 1))
                pool.tensor_tensor(skip[:], x_hat[:], row("norm2_w"), ALU.mult).then_inc(S["x_steps"], 1)
                pool.wait_ge(S["x_steps"], at(g, "x_steps", 1))
                pool.tensor_tensor(skip[:], skip[:], shifted(x_shift), ALU.add).then_inc(S["x_steps"], 1)

            def tail(g):
                yield "cross"
                root(g, "a_", LN_CROSS)
                pool.wait_ge(S["x_steps"], at(g, "x_steps", 2))
                pool.wait_ge(S["cross_g"], at(g, "cross_g", 1))
                pool.tensor_tensor(skip[:], skip[:], cross_g[:], ALU.add).then_inc(S["skip"], 1)
                yield "l1_norm"
                root(g, "a_", LN_L1)
                yield "sa_norm"
                root(g, "a_", LN_SA)
                pool.wait_ge(S["x2"], at(g, "x2", 1))
                pool.tensor_tensor(fr.residual[:], fr.x_res[:], row("sa_out_b"), ALU.add).then_inc(S["a_residual"], 1)
                yield "caq_norm"
                root(g, "a_", LN_CAQ)
                pool.wait_ge(S["a_attn_sum"], at(g, "a_attn_sum", 1))
                pool.tensor_tensor(fr.residual[:], fr.x_res[:], row("ca_out_b"), ALU.add).then_inc(S["a_residual"], 1)
                yield "moe_norm"
                root(g, "a_", LN_MOE)
                pool.wait_ge(S["a_feat"], at(g, "a_feat", F_RAW + 1))
                if g is not FIRST:
                    pool.wait_ge(S["b_v_proj"], at(g, "b_v_proj", 0))
                pool.sem_inc(s_held, 1)
                pool.tensor_copy(ctx_kept[:], ctx_f[:]).then_inc(S["ctx_kept"], 1)

            def front(g, ahead):
                yield from tail(g)

            def back(g):
                yield "l3_turn"
                pool.wait_ge(S["moe_acc"], at(g, "moe_acc", EXPERTS + 1))
                pool.tensor_tensor(bk.residual[:], bk.x_res[:], row("bo_s"), ALU.add).then_inc(S["b_residual"], 1)
                for n, (ln, scale, shift) in enumerate(((LN_31, "g1", shift31), (LN_32, "g2", shift32))):
                    yield f"n3{n + 1}_norm"
                    root(g, "b_", ln)
                    pool.wait_ge(S["b_ln_hat"], at(g, "b_ln_hat", ln + 1))
                    pool.tensor_tensor(bk.residual[:], bk.hat[:], row(scale), ALU.mult).then_inc(S["res_scaled"], 1)
                    pool.wait_ge(S["res_scaled"], at(g, "res_scaled", n + 1))
                    pool.tensor_tensor(bk.residual[:], bk.residual[:], shifted(shift), ALU.add)\
                        .then_inc(S["b_residual"], 1)
                yield "result"
                root(g, "b_", LN_33)
                pool.wait_ge(S["out_stored"], at(g, "out_stored", 0))
                pool.wait_ge(S["b_ln_hat"], at(g, "b_ln_hat", LN_33 + 1))
                pool.tensor_tensor(out_tok[:], bk.hat[:], row("g3"), ALU.mult).then_inc(S["res_scaled"], 1)
                pool.wait_ge(S["res_scaled"], at(g, "res_scaled", 3))
                pool.tensor_tensor(out_tok[:], out_tok[:], row("be3"), ALU.add).then_inc(S["out_ready"], 1)

            pool.wait_ge(s_weights, weights_in)
            pool.wait_ge(s_const, 6)
            pool.sem_inc(S["out_ready"], START["out_ready"])
            alone(norms(FIRST))
            pool.wait_ge(S["a_ln_rstd"], at(FIRST, "a_ln_rstd", LN_X + 1))
            for name in ("a_ln_var", "a_ln_rstd"):
                pool.sem_inc(S[name], 1)
            weave(front(FIRST, SECOND), norms(SECOND))
            with pool.Fori(0, steps - 1) as it:
                v = Values(pool, it)
                weave(front(Group(it, 1, v), Group(it, 2, v)), norms(Group(it, 2, v)), back(Group(it, 0, v)))
            alone(back(LAST))

        @block.scalar
        def _(act):
            def affine(g, s, t, f, scale, shift):
                act.wait_ge(S[s + "turned"], at(g, s + "turned", t))
                act.activation(buf[s].feat[:], bank[s][2][:], ACT.Identity, bias=col(shift), scale=col(scale))\
                    .then_inc(S[s + "feat"], 1)

            def attention(g, s, m):
                x, n, nk, ps = buf[s], m % 2, KEYS[m], bank[s]
                keys = GROUP * nk
                yield f"proj{m}"
                act.wait_ge(S[s + "k_proj"], at(g, s + "k_proj", n + 1))
                act.activation(x.k_nat[:, 0, 0:keys], ps[3][:, 0:keys], ACT.Identity,
                               bias=col(f"bk{m}")).then_inc(S[s + "k_hi"], 1)
                yield f"query{m}"
                act.wait_ge(S[s + "q_proj"], at(g, s + "q_proj", n + 1))
                act.activation(x.q_nat[:, 0, :], ps[1][:], ACT.Identity, bias=col(f"bq{m}")).then_inc(S[s + "q_hi"], 1)
                yield f"value{m}"
                act.wait_ge(S[s + "v_proj"], at(g, s + "v_proj", n + 1))
                act.activation(x.v_pad[0:nk, :, :, 0:DH],
                               ps[0][0:nk, :].rearrange("k (b h d) -> k b h d", b=GROUP, h=HEADS),
                               ACT.Copy).then_inc(S[s + "v_sb"], 1)

                def copy_out(j):
                    act.wait_ge(S[s + "pv"], at(g, s + "pv", n * UNITS + GROUP * (j + 1)))
                    if j >= 1:
                        act.wait_ge(S[s + "o_t"], at(g, s + "o_t", TILES * n + j))
                    act.activation(x.o_sb[:], ps[2][:], ACT.Copy).then_inc(S[s + "o_sb"], 1)

                for phase, j, b in attention_units(m):
                    u = GROUP * j + b
                    yield phase
                    if phase.startswith("max"):
                        act.wait_ge(S[s + "m_t"], at(g, s + "m_t", TILES * n + j + 1))
                        act.activation(x.m_nat[32 * j:32 * j + 32, :], ps[3][0:32, :], ACT.Copy,
                                       scale=1.0 / MAX_SCALE).then_inc(S[s + "m_sb"], 1)
                    elif phase.startswith("score") and b == 2 and EARLY <= j + 2 < TILES:
                        act.wait_ge(S[f"{s}kq_shift{j + 2}"], at(g, f"{s}kq_shift{j + 2}", 32 * (n + 1)))
                        for i in range(SLOTS):
                            act.activation(x.k_blk[:, j + 2, i, 0:keys], x.k_int[:, j + 2, 0:keys], ACT.Copy,
                                           scale=slot_mask[:, i:i + 1]).then_inc(S[s + "k_blk_late"], 1)
                    elif phase.startswith("weigh"):
                        if b == 0 and j >= 1:
                            copy_out(j - 1)
                        act.wait_ge(S[s + "scores_t"], at(g, s + "scores_t", n * UNITS + u + 1))
                        if u >= 2:
                            act.wait_ge(S[s + "pv"], at(g, s + "pv", n * UNITS + u - 1))
                        act.activation(x.probs[u % 2][0:nk], weigh_bank(s, j, b)[0:nk, :], ACT.Exp, scale=DH ** -0.5)\
                            .then_inc(S[s + "probs"], 1)
                yield f"out{m}"
                copy_out(TILES - 1)
                yield f"norm{m}"
                act.wait_ge(S[s + "on_t"], at(g, s + "on_t", n + 1))
                act.activation(x.feat[:], ps[2][:], ACT.Identity, bias=col(f"bv{m}")).then_inc(S[s + "on_sb"], 1)

            def norms(g):
                yield "x_norm"
                act.wait_ge(S["ctx_min"], at(g, "ctx_min", 1))
                act.activation(ctx_phi, ctx_phi, ACT.Exp).then_inc(S["ctx_exp"], 1)

            def head(g):
                yield "ctx_turn"
                act.wait_ge(S["a_turned"], at(g, "a_turned", 1))
                act.activation(norm1_f[:], bank["a_"][2][:, 0:GROUP * C], ACT.Identity, bias=col("norm1_b"),
                               scale=col("norm1_w"))
                act.activation(cakv_f[:], bank["a_"][2][:, 0:GROUP * C], ACT.Identity, bias=col("cakv_b"),
                               scale=col("cakv_g")).then_inc(S["a_feat"], 1)
                if g is not FIRST:
                    act.wait_ge(S["ctx_kept"], at(g, "ctx_kept", 0))
                act.wait_ge(S["a_turned"], at(g, "a_turned", 2))
                act.activation(ctx_f[:], bank["a_"][3][:, 0:GROUP * C], ACT.Copy).then_inc(S["a_feat"], 1)
                yield "x_turn"
                act.wait_ge(S["v0"], at(g, "v0", 1))
                act.activation(v0[:, :, 0:4], bank["a_"][1][0:C, 0:4 * GROUP].rearrange("k (b f) -> k b f", b=GROUP),
                               ACT.Copy).then_inc(S["v0_sb"], 1)
                affine(g, "a_", 3, F_X, "norm2_w", "norm2_b")
                yield "scores0"
                act.wait_ge(S["kv"], at(g, "kv", 1))
                for i in range(2):
                    seqs, src = wide_bank(0, i)
                    act.activation(kv[:, seqs, :], src, ACT.Copy).then_inc(S["kv_sb"], 1)

            def tail(g):
                yield "max0"
                act.wait_ge(S["max0_t"], at(g, "max0_t", 1))
                act.activation(max0_t[:], bank["a_"][2][0:GROUP, 0:P], ACT.Copy).then_inc(S["max0_sb"], 1)
                yield "scores0_t"
                act.wait_ge(S["s0_t"], at(g, "s0_t", 1))
                act.activation(p0, bank["a_"][3][0:C, :], ACT.Exp, scale=D ** -0.5).then_inc(S["p0"], 1)
                yield "values0"
                act.wait_ge(S["h_in"], at(g, "h_in", 1))
                act.activation(h[:, :, 0:4], h_in[:], ACT.Gelu).then_inc(S["h"], 1)
                yield "hidden0"
                act.wait_ge(S["h_t"], at(g, "h_t", 1))
                act.activation(h_t, bank["a_"][2][0:5, :], ACT.Copy).then_inc(S["h_t_sb"], 1)
                yield "cross_turn"
                affine(g, "a_", 4, F_CROSS, "norm3_w", "norm3_b")
                yield "max1"
                act.wait_ge(S["max1_t"], at(g, "max1_t", 1))
                act.activation(max1_t[:], bank["a_"][1][0:GROUP, 0:P], ACT.Copy).then_inc(S["max1_sb"], 1)
                yield "scores1_t"
                act.wait_ge(S["s1_t"], at(g, "s1_t", 1))
                act.activation(p1, bank["a_"][0][:], ACT.Exp, scale=D ** -0.5).then_inc(S["p1"], 1)
                yield "x1_turn"
                act.wait_ge(S["x1_min"], at(g, "x1_min", 1))
                act.activation(x1_phi, x1_phi, ACT.Exp).then_inc(S["x1_exp"], 1)
                yield "sa_turn"
                affine(g, "a_", 6, F_SA, "sa_g", "sa_b")
                yield from attention(g, "a_", SELF2)
                yield "caq_turn"
                affine(g, "a_", 7, F_CAQ, "caq_g", "caq_b")
                yield from attention(g, "a_", CROSS2)
                yield "moe_turn"
                affine(g, "a_", 8, F_MOE, "moe_g", "moe_b")
                if g is not FIRST:
                    act.wait_ge(S["b_q_shift0"], at(g, "b_q_shift0", 0))
                    for j in range(1, TILES):
                        act.wait_ge(S[f"b_kq_shift{j}"], at(g, f"b_kq_shift{j}", 0))
                act.activation(moe_hi, bank["a_"][2][:], ACT.Identity, bias=col("moe_b"), scale=col("moe_g"))\
                    .then_inc(S["moe_hi"], 1)
                yield "gate"
                act.wait_ge(S["gap"], at(g, "gap", 1))
                act.activation(gap_exp[:], gap[:], ACT.Exp).then_inc(S["gap_exp"], 1)

            def front(g, ahead):
                yield from tail(g)
                yield from head(ahead)

            def back(g):
                for e in range(EXPERTS):
                    for i in range(2):
                        yield f"in{e}_{i}"
                        for c in (2 * i, 2 * i + 1):
                            if c == 0 and e >= 2:
                                act.wait_ge(S["fc2"], at(g, "fc2", e - 1))
                            act.wait_ge(S["fc1"], at(g, "fc1", CHUNKS * e + c + 1))
                            act.activation(hidden[e % 2][:, c, :], bank["b_"][c % 2][:], ACT.Gelu,
                                           bias=col(f"moe_b1_{e}_{c}")).then_inc(S["gelu"], 1)
                    if e == 0:
                        yield "gates"
                        act.wait_ge(S["gates_t"], at(g, "gates_t", 1))
                        act.activation(gates_t, bank["b_"][2][0:EXPERTS, :], ACT.Copy).then_inc(S["gates_sb"], 1)
                yield "l3_turn"
                act.wait_ge(S["b_turned"], at(g, "b_turned", 1))
                act.activation(bk.feat[:], bank["b_"][2][:], ACT.Copy).then_inc(S["b_feat"], 1)
                yield from attention(g, "b_", SELF3)
                yield "n31_turn"
                affine(g, "b_", 2, F_31, "g1", "be1")
                yield from attention(g, "b_", CROSS3)
                yield "n32_turn"
                affine(g, "b_", 3, F_32, "g2", "be2")
                yield "ffn_in"
                for c in range(CHUNKS):
                    act.wait_ge(S["ffn1"], at(g, "ffn1", c + 1))
                    act.activation(hidden[0][:, c, :], bank["b_"][c % 2][:], ACT.Relu, bias=col(f"ffn_b1_{c}"))\
                        .then_inc(S["ffn_relu"], 1)

            act.wait_ge(s_weights, weights_in)
            act.wait_ge(s_fill, filled)
            alone(norms(FIRST))
            alone(head(FIRST))
            weave(front(FIRST, SECOND), norms(SECOND))
            act.wait_ge(s_experts, experts_in)
            act.activation(moe_w1[0][:], w1_f32, ACT.Copy).then_inc(s_split, 1)
            with act.Fori(0, steps - 1) as it:
                v = Values(act, it)
                weave(front(Group(it, 1, v), Group(it, 2, v)), norms(Group(it, 2, v)), back(Group(it, 0, v)))
            alone(back(LAST))

        @block.vector
        def _(dve):
            def normalise(g, s, n, phase, src, dst, p=P):
                x = buf[s]
                for b in range(GROUP):
                    dve.bn_stats(x.stats[0:p, b, :], src(b)).then_inc(S[s + "ln_stats"], 1)
                dve.wait_ge(S[s + "ln_stats"], at(g, s + "ln_stats", GROUP * (n + 1)))
                dve.sem_inc(s_held, 1)
                for b in range(GROUP):
                    dve.bn_aggr(x.mean_var[0:p, b, :], x.stats[0:p, b, :]).then_inc(S[s + "ln_mean"], 1)
                yield phase
                dve.wait_ge(S[s + "ln_rstd"], at(g, s + "ln_rstd", n + 1))
                for b in range(GROUP):
                    last = dve.tensor_scalar(dst(b), src(b), x.mean_var[0:p, b, 0:1], x.rstd[0:p, b:b + 1],
                                             ALU.subtract, ALU.mult)
                last.then_inc(S[s + "ln_hat"], 1)

            def normalise_residual(g, s, n, phase):
                yield from normalise(g, s, n, phase, lambda b: buf[s].x_res[:, b, :], lambda b: buf[s].hat[:, b, :])

            def attention(g, s, m):
                x, n, nk, ps = buf[s], m % 2, KEYS[m], bank[s]
                keys = GROUP * nk
                yield f"proj{m}"
                dve.wait_ge(S[s + "k_hi"], at(g, s + "k_hi", n + 1))
                dve.scalar_tensor_tensor(x.k_nat[:, 1, 0:keys], ps[3][:, 0:keys], col(f"bk{m}"),
                                         x.k_nat[:, 0, 0:keys], ALU.add, ALU.subtract).then_inc(S[s + "k_split"], 1)
                dve.tensor_copy(x.k_nat[:, 2, 0:keys], x.k_nat[:, 0, 0:keys]).then_inc(S[s + "k_split"], 1)
                yield f"query{m}"
                dve.wait_ge(S[s + "q_hi"], at(g, s + "q_hi", n + 1))
                dve.scalar_tensor_tensor(x.q_nat[:, 2, :], ps[1][:], col(f"bq{m}"), x.q_nat[:, 0, :],
                                         ALU.add, ALU.subtract).then_inc(S[s + "q_split"], 1)
                dve.tensor_copy(x.q_nat[:, 1, :], x.q_nat[:, 0, :]).then_inc(S[s + "q_split"], 1)

                def block_keys(j):
                    if j == 0:
                        dve.wait_ge(S[s + "k_shift0"], at(g, s + "k_shift0", 16 * (n + 1)))
                    else:
                        dve.wait_ge(S[f"{s}kq_shift{j}"], at(g, f"{s}kq_shift{j}", 32 * (n + 1)))
                    for i in range(SLOTS):
                        dve.tensor_scalar(x.k_blk[:, j, i, 0:keys], x.k_int[:, j, 0:keys], slot_mask[:, i:i + 1], None,
                                          ALU.mult).then_inc(S[s + "k_blk"], 1)

                def divide(j):
                    c = TILES * n + j + 1
                    o_t = ps[3][:].rearrange("q (b i r) -> q b i r", b=GROUP, r=VW)
                    dve.wait_ge(S[s + "o_t"], at(g, s + "o_t", c))
                    dve.reciprocal(x.o_rden[:, j], o_t[:, :, :, DH]).then_inc(S[s + "o_rden"], 1)
                    dve.wait_ge(S[s + "o_rden"], at(g, s + "o_rden", c))
                    dve.tensor_tensor(x.o_norm[:, :, 32 * j:32 * j + 32].rearrange("q b (i d) -> q b i d", d=DH),
                                      o_t[:, :, :, 0:DH],
                                      x.o_rden[:, j].unsqueeze(3).broadcast_to([P, GROUP, SLOTS, DH]),
                                      ALU.mult).then_inc(S[s + "o_norm"], 1)

                for phase, j, b in attention_units(m):
                    u = GROUP * j + b
                    yield phase
                    if phase.startswith("score"):
                        if u == 0:
                            block_keys(0)
                        if b == 1 and j + 1 < EARLY:
                            block_keys(j + 1)
                        dve.wait_ge(S[s + "scores"], at(g, s + "scores", n * UNITS + u + 1))
                        dve.tensor_reduce(x.smax[:, b, 32 * j:32 * j + 32:DH],
                                          score_bank(s, j, b)[:, 0:SLOTS * nk].rearrange("q (i k) -> q i k", i=SLOTS),
                                          AX.X, ALU.max, negate=True).then_inc(S[s + "smax"], 1)
                    elif phase.startswith("weigh"):
                        if b == 2 and j >= 1:
                            divide(j - 1)
                yield f"out{m}"
                divide(TILES - 1)
                yield f"sum{m}"
                dve.wait_ge(S[s + "attn"], at(g, s + "attn", n + 1))
                dve.wait_ge(S[s + "residual"], at(g, s + "residual", n + 1))
                dve.tensor_tensor(x.x_res[:], ps[1][:].rearrange("q (b d) -> q b d", b=GROUP), x.residual[:], ALU.add)\
                    .then_inc(S[s + "attn_sum"], 1)

            def norms(g):
                yield "ctx_norm"
                dve.wait_ge(S["ctx_in"], at(g, "ctx_in", 16))
                if g is not FIRST:
                    dve.wait_ge(S["a_scores_t"], at(g, "a_scores_t", UNITS + GROUP - PER["a_scores_t"]))
                dve.tensor_scalar(ctx_phi, ctx_tok[:, :, 0:D], 0.0, None, ALU.min).then_inc(S["ctx_min"], 1)
                yield from normalise(g, "a_", LN_CTX, "ctx_hat", lambda b: ctx_tok[:, b, 0:D], lambda b: ctx_hat[:, b, :], C)
                yield "x_norm"
                dve.wait_ge(S["x_in"], at(g, "x_in", 16))
                yield from normalise(g, "a_", LN_X, "x_hat", lambda b: x_tok[:, b, :], lambda b: x_hat[:, b, :])
                yield "ctx_elu"
                dve.wait_ge(S["ctx_exp"], at(g, "ctx_exp", 1))
                dve.scalar_tensor_tensor(ctx_phi, ctx_phi, -1.0, ctx_tok[:, :, 0:D], ALU.add, ALU.max)\
                    .then_inc(S["ctx_phi"], 1)

            def head(g):
                yield "scores0"
                dve.wait_ge(S["s0"], at(g, "s0", 1))
                dve.tensor_reduce(max0[:], bank["a_"][3][:, 0:GROUP * C].rearrange("q (b k) -> q b k", b=GROUP),
                                  AX.X, ALU.max, negate=True).then_inc(S["max0"], 1)

            def tail(g):
                yield "values0"
                dve.wait_ge(S["hpre"], at(g, "hpre", 1))
                hpre = bank["a_"][2][:, 0:5 * GROUP].rearrange("q (b f) -> q b f", b=GROUP)
                dve.reciprocal(h_rden[:], hpre[:, :, 4]).then_inc(S["h_steps"], 1)
                dve.wait_ge(S["h_steps"], at(g, "h_steps", 1))
                dve.tensor_tensor(h_mul[:], hpre[:, :, 0:4], h_rden[:].unsqueeze(2).broadcast_to([P, GROUP, 4]),
                                  ALU.mult).then_inc(S["h_steps"], 1)
                dve.wait_ge(S["h_steps"], at(g, "h_steps", 2))
                dve.tensor_tensor(h_in[:], h_mul[:], fc1_b[:].unsqueeze(1).broadcast_to([P, GROUP, 4]), ALU.add)\
                    .then_inc(S["h_in"], 1)
                yield "cross"
                dve.wait_ge(S["cross"], at(g, "cross", 1))
                cross = bank["a_"][3][:].rearrange("q (b d) -> q b d", b=GROUP)
                yield from normalise(g, "a_", LN_CROSS, "cross_hat", lambda b: cross[:, b, :], lambda b: cross_hat[:, b, 0:D])
                dve.tensor_tensor(cross_g[:], cross, row("gamma2"), ALU.mult).then_inc(S["cross_g"], 1)
                yield "scores1"
                dve.wait_ge(S["s1"], at(g, "s1", 1))
                dve.tensor_reduce(max1[:], bank["a_"][0][:].rearrange("q (b k) -> q b k", b=GROUP),
                                  AX.X, ALU.max, negate=True).then_inc(S["max1"], 1)
                yield "values1"
                dve.wait_ge(S["pv1"], at(g, "pv1", 1))
                for i in range(2):
                    seqs, src = wide_bank(1, i)
                    dve.reciprocal(pv1_rden[:, seqs], src[:, :, D]).then_inc(S["pv1_steps"], 1)
                dve.wait_ge(S["pv1_steps"], at(g, "pv1_steps", 2))
                for b in range(GROUP):
                    last = dve.scalar_tensor_tensor(pv1_n[:, b, :], wide(1, b)[:, 0:D], pv1_rden[:, b:b + 1],
                                                    self_scale[:], ALU.mult, ALU.mult)
                last.then_inc(S["pv1_steps"], 1)
                dve.wait_ge(S["pv1_steps"], at(g, "pv1_steps", 3))
                dve.wait_ge(S["skip"], at(g, "skip", 1))
                dve.tensor_tensor(x1[:], pv1_n, skip[:], ALU.add).then_inc(S["x1"], 1)
                yield "x1_turn"
                dve.wait_ge(S["a_turned"], at(g, "a_turned", 5))
                dve.tensor_scalar(x1_phi, bank["a_"][0][:], 0.0, None, ALU.min).then_inc(S["x1_min"], 1)
                yield "x1_elu"
                dve.wait_ge(S["x1_exp"], at(g, "x1_exp", 1))
                dve.scalar_tensor_tensor(x1_phi, x1_phi, -1.0, bank["a_"][0][:], ALU.add, ALU.max)\
                    .then_inc(S["x1_phi"], 1)
                yield "linear"
                dve.wait_ge(S["num"], at(g, "num", 1))
                for i in range(2):
                    seqs, src = wide_bank(1, i)
                    dve.tensor_scalar(num_den[:, seqs], src[:, :, D], ATTN_EPS, None, ALU.add)\
                        .then_inc(S["num_steps"], 1)
                dve.wait_ge(S["num_steps"], at(g, "num_steps", 2))
                dve.reciprocal(num_rden[:], num_den[:]).then_inc(S["num_steps"], 1)
                dve.wait_ge(S["num_steps"], at(g, "num_steps", 3))
                for b in range(GROUP):
                    last = dve.scalar_tensor_tensor(l1_sum[:, b, :], wide(1, b)[:, 0:D], num_rden[:, b:b + 1],
                                                    x1[:, b, :], ALU.mult, ALU.add)
                last.then_inc(S["l1_steps"], 1)
                yield "l1_norm"
                dve.wait_ge(S["l1_steps"], at(g, "l1_steps", 1))
                yield from normalise(g, "a_", LN_L1, "l1_hat", lambda b: l1_sum[:, b, :], lambda b: fr.hat[:, b, :])
                dve.wait_ge(S["a_ln_hat"], at(g, "a_ln_hat", LN_L1 + 1))
                dve.tensor_tensor(l1_sum, fr.hat[:], row("l1_gamma"), ALU.mult).then_inc(S["l1_steps"], 1)
                dve.wait_ge(S["l1_steps"], at(g, "l1_steps", 2))
                if g is not FIRST:
                    dve.wait_ge(S["moe_acc"], at(g, "moe_acc", 1 - PER["moe_acc"]))
                dve.tensor_tensor(fr.x_res[:], l1_sum, row("l1_beta"), ALU.add).then_inc(S["x2"], 1)
                yield "sa_norm"
                dve.wait_ge(S["x2"], at(g, "x2", 1))
                yield from normalise_residual(g, "a_", LN_SA, "sa_hat")
                yield from attention(g, "a_", SELF2)
                yield "caq_norm"
                dve.wait_ge(S["a_attn_sum"], at(g, "a_attn_sum", 1))
                yield from normalise_residual(g, "a_", LN_CAQ, "caq_hat")
                yield from attention(g, "a_", CROSS2)
                yield "moe_norm"
                dve.wait_ge(S["a_attn_sum"], at(g, "a_attn_sum", 2))
                yield from normalise_residual(g, "a_", LN_MOE, "moe_hat")
                yield "moe_turn"
                dve.wait_ge(S["moe_hi"], at(g, "moe_hi", 1))
                dve.tensor_tensor(moe_lo, fr.feat[:], moe_hi, ALU.subtract).then_inc(S["moe_lo"], 1)
                yield "router"
                if g is not FIRST:
                    dve.wait_ge(S["moe_acc"], at(g, "moe_acc", 0))
                dve.wait_ge(S["router"], at(g, "router", 1))
                dve.tensor_tensor(logits[:], bank["a_"][3][:, 0:GROUP * EXPERTS].rearrange("q (b e) -> q b e", b=GROUP),
                                  router_b[:].unsqueeze(1).broadcast_to([P, GROUP, EXPERTS]), ALU.add)\
                    .then_inc(S["logits"], 1)
                dve.wait_ge(S["logits"], at(g, "logits", 1))
                dve.sem_inc(s_held, 1)
                for b in range(GROUP):
                    dve.max(top[:, b, :], logits[:, b, :]).then_inc(S["top"], 1)
                dve.wait_ge(S["top"], at(g, "top", GROUP))
                dve.sem_inc(s_held, 1)
                for b in range(GROUP):
                    dve.max_index(top_at[:, b, :], top[:, b, :], logits[:, b, :]).then_inc(S["top_at"], 1)
                dve.tensor_tensor(gap[:], top[:, :, 1], top[:, :, 0], ALU.subtract).then_inc(S["gap"], 1)
                dve.wait_ge(S["top_at"], at(g, "top_at", GROUP))
                dve.tensor_copy(top_f[:], top_at[:]).then_inc(S["gate_steps"], 1)
                yield "gate"
                dve.wait_ge(S["gap_exp"], at(g, "gap_exp", 1))
                dve.tensor_scalar(gap_den[:], gap_exp[:], 1.0, None, ALU.add).then_inc(S["gate_steps"], 1)
                dve.wait_ge(S["gate_steps"], at(g, "gate_steps", 2))
                dve.reciprocal(gate1[:], gap_den[:]).then_inc(S["gate_steps"], 1)
                dve.wait_ge(S["gate_steps"], at(g, "gate_steps", 3))
                dve.tensor_tensor(gate2[:], gap_exp[:], gate1[:], ALU.mult).then_inc(S["gate_steps"], 1)
                dve.wait_ge(S["gate_steps"], at(g, "gate_steps", 1))
                experts = expert_id[:].unsqueeze(1).broadcast_to([P, GROUP, EXPERTS])

                def each(ap):
                    return ap.unsqueeze(2).broadcast_to([P, GROUP, EXPERTS])

                for i in range(2):
                    dve.tensor_tensor(hot[i][:], experts, each(top_f[:, :, i]), ALU.is_equal).then_inc(S["gate_steps"], 1)
                dve.wait_ge(S["gate_steps"], at(g, "gate_steps", 6))
                dve.tensor_tensor(pick[0][:], hot[0][:], each(gate1[:]), ALU.mult).then_inc(S["gate_steps"], 1)
                dve.wait_ge(S["gate_steps"], at(g, "gate_steps", 4))
                dve.tensor_tensor(pick[1][:], hot[1][:], each(gate2[:]), ALU.mult).then_inc(S["gate_steps"], 1)
                dve.wait_ge(S["gate_steps"], at(g, "gate_steps", 8))
                dve.tensor_tensor(gates[:], pick[0][:], pick[1][:], ALU.add).then_inc(S["gates"], 1)

            def front(g, ahead):
                yield from tail(g)
                yield from head(ahead)

            def back(g):
                yield "gates"
                dve.wait_ge(S["out_ready"], at(g, "out_ready", 0))
                dve.wait_ge(S["gate_bias"], at(g, "gate_bias", 1))
                dve.tensor_tensor(bk.x_res[:], bank["b_"][3][:].rearrange("q (b d) -> q b d", b=GROUP), fr.x_res[:],
                                  ALU.add).then_inc(S["moe_acc"], 1)
                for e in range(EXPERTS):
                    yield f"out{e}_1"
                    dve.wait_ge(S["fc2"], at(g, "fc2", e + 1))
                    dve.wait_ge(S["moe_acc"], at(g, "moe_acc", e + 1))
                    for b in range(GROUP):
                        last = dve.scalar_tensor_tensor(bk.x_res[:, b, :], bank["b_"][2 + e % 2][:, seq_tok(b)],
                                                        gates[:, b, e:e + 1], bk.x_res[:, b, :], ALU.mult, ALU.add)
                    last.then_inc(S["moe_acc"], 1)
                yield from attention(g, "b_", SELF3)
                yield "n31_norm"
                dve.wait_ge(S["b_attn_sum"], at(g, "b_attn_sum", 1))
                yield from normalise_residual(g, "b_", LN_31, "n31_hat")
                yield from attention(g, "b_", CROSS3)
                yield "n32_norm"
                dve.wait_ge(S["b_attn_sum"], at(g, "b_attn_sum", 2))
                yield from normalise_residual(g, "b_", LN_32, "n32_hat")
                yield "ffn_out"
                dve.wait_ge(S["ffn2"], at(g, "ffn2", 1))
                dve.wait_ge(S["b_residual"], at(g, "b_residual", 3))
                dve.tensor_tensor(bk.x_res[:], bank["b_"][3][:].rearrange("q (b d) -> q b d", b=GROUP), bk.residual[:],
                                  ALU.add).then_inc(S["ffn_sum"], 1)
                yield "result"
                dve.wait_ge(S["ffn_sum"], at(g, "ffn_sum", 1))
                yield from normalise_residual(g, "b_", LN_33, "result_hat")

            dve.wait_ge(s_weights, weights_in)
            dve.wait_ge(s_fill, filled)
            r = {n: rows[:, i, :] for i, n in enumerate(ROWS)}
            dve.tensor_tensor(self_scale[:], r["gamma1"], r["gamma2"], ALU.mult).then_inc(s_const, 1)
            dve.wait_ge(s_const, 1)
            dve.tensor_tensor(x_shift[:], self_scale[:], r["norm3_b"], ALU.mult).then_inc(s_const, 1)
            dve.wait_ge(s_const, 2)
            dve.tensor_tensor(x_shift[:], x_shift[:], r["norm2_b"], ALU.add).then_inc(s_const, 1)
            dve.tensor_tensor(self_scale[:], self_scale[:], r["norm3_w"], ALU.mult).then_inc(s_const, 1)
            dve.tensor_tensor(shift31[:], r["be1"], r["bo_c"], ALU.add).then_inc(s_const, 1)
            dve.tensor_tensor(shift32[:], r["be2"], r["ffn_b2"], ALU.add).then_inc(s_const, 1)
            dve.wait_ge(s_const, 6)
            dve.sem_inc(S["ffn_sum"], START["ffn_sum"])
            alone(norms(FIRST))
            dve.wait_ge(S["a_ln_hat"], at(FIRST, "a_ln_hat", LN_X + 1))
            for name, count in (("a_ln_stats", GROUP), ("a_ln_mean", GROUP), ("a_ln_hat", 1)):
                dve.sem_inc(S[name], count)
            alone(head(FIRST))
            weave(front(FIRST, SECOND), norms(SECOND))
            dve.wait_ge(s_experts, experts_in)
            dve.wait_ge(s_split, 1)
            dve.tensor_tensor(moe_w1[1][:], w1_f32, moe_w1[0][:], ALU.subtract).then_inc(s_split, 1)
            with dve.Fori(0, steps - 1) as it:
                v = Values(dve, it)
                weave(front(Group(it, 1, v), Group(it, 2, v)), norms(Group(it, 2, v)), back(Group(it, 0, v)))
            alone(back(LAST))

        @block.tensor
        def _(pe):
            def turn(dst, src, n=P, width=P):
                for b in range(GROUP):
                    last = pe.transpose(dst[0:width, b * n:(b + 1) * n], src(b), ident[0:n, 0:n])
                return last

            def turn_hat(g, s, ln):
                pe.wait_ge(S[s + "ln_hat"], at(g, s + "ln_hat", ln + 1))
                turn(bank[s][2], lambda b: buf[s].hat[:, b, :]).then_inc(S[s + "turned"], 1)

            def attention(g, s, m, k_src, f):
                x, n, nk, ps = buf[s], m % 2, KEYS[m], bank[s]
                keys = GROUP * nk
                yield f"proj{m}"
                pe.wait_ge(S[s + "feat"], at(g, s + "feat", f + 1))
                pe.matmul(ps[3][:, 0:keys], mat(f"wk{m}"), k_src, start=True, stop=True)\
                    .then_inc(S[s + "k_proj"], 1)
                yield f"query{m}"
                pe.matmul(ps[1][:], mat(f"wq{m}"), x.feat[:], start=True, stop=True).then_inc(S[s + "q_proj"], 1)
                yield f"value{m}"
                for b in range(GROUP):
                    last = pe.matmul(ps[0][0:nk, b * D:(b + 1) * D], k_src[:, seq_keys(b, nk)], mat(f"wv{m}"),
                                     start=True, stop=True)
                last.then_inc(S[s + "v_proj"], 1)

                def scores(j, b):
                    u = GROUP * j + b
                    if u == 2:
                        pe.wait_ge(S[s + "v_sb"], at(g, s + "v_sb", n + 1))
                    elif j < LAG and u >= 3:
                        pe.wait_ge(S[s + "smax"], at(g, s + "smax", n * UNITS + u - 2))
                    elif j >= LAG:
                        pe.wait_ge(S[s + "smax"], at(g, s + "smax", n * UNITS + u))
                    if b == 0:
                        if j == 0:
                            pe.wait_ge(S[s + "q_shift0"], at(g, s + "q_shift0", 16 * (n + 1)))
                        else:
                            pe.wait_ge(S[f"{s}kq_shift{j}"], at(g, f"{s}kq_shift{j}", 32 * (n + 1)))
                        if j < EARLY:
                            pe.wait_ge(S[s + "k_blk"], at(g, s + "k_blk", SLOTS * (EARLY * n + j + 1)))
                        else:
                            pe.wait_ge(S[s + "k_blk_late"],
                                       at(g, s + "k_blk_late", SLOTS * ((TILES - EARLY) * (n + 1) - TILES + j + 1)))
                    dst = score_bank(s, j, b)[:, 0:SLOTS * nk]
                    if CAUSAL[m]:
                        pe.matmul(dst, ident_bf[:], mask_q[:].rearrange("q i k -> q (i k)"), start=True, stop=False)
                    pe.matmul(dst, x.q_int[:, j, seq_tok(b)], x.k_blk[:, j, :, seq_keys(b, nk)],
                              start=not CAUSAL[m], stop=True).then_inc(S[s + "scores"], 1)

                def turn_max(j):
                    pe.wait_ge(S[s + "smax"], at(g, s + "smax", n * UNITS + GROUP * (j + 1)))
                    if j >= 1:
                        pe.wait_ge(S[s + "m_sb"], at(g, s + "m_sb", TILES * n + j))
                    if j > LAG:
                        pe.wait_ge(S[s + "o_norm"], at(g, s + "o_norm", TILES * n + j - LAG))
                    for b in range(GROUP):
                        last = pe.transpose(ps[3][0:32, b * T:(b + 1) * T],
                                            x.smax[:, b, 32 * j:32 * j + 32], ident[:])
                    last.then_inc(S[s + "m_t"], 1)

                def scores_t(j, b):
                    u = GROUP * j + b
                    if b == 0:
                        pe.wait_ge(S[f"{s}m_shift{j}"], at(g, f"{s}m_shift{j}", 16 * (n + 1)))
                    if u == 0:
                        pe.wait_ge(S[s + "smax"], at(g, s + "smax", n * UNITS + GROUP * LAG))
                    elif j < TILES - LAG:
                        pe.wait_ge(S[s + "probs"], at(g, s + "probs", n * UNITS + u))
                    else:
                        if u >= 2:
                            pe.wait_ge(S[s + "probs"], at(g, s + "probs", n * UNITS + u - 1))
                        if u == GROUP * (TILES - LAG):
                            pe.wait_ge(S[s + "smax"], at(g, s + "smax", (n + 1) * UNITS))
                    dst = weigh_bank(s, j, b)[0:nk, :]
                    if CAUSAL[m]:
                        pe.matmul(dst, ident_bf[:], mask_k[:].rearrange("k i q -> k (i q)"), start=True, stop=True)
                    for i in range(SLOTS):
                        last = pe.matmul(dst[:, i * T:(i + 1) * T], x.k_blk[:, j, i, seq_keys(b, nk)],
                                         x.q_int[:, j, seq_tok(b)], start=not CAUSAL[m], stop=True,
                                         skip_group_check=True)
                    last.then_inc(S[s + "scores_t"], 1)

                def weigh(j, b):
                    u = GROUP * j + b
                    if b == 0 and j >= 1:
                        pe.wait_ge(S[s + "o_sb"], at(g, s + "o_sb", TILES * n + j))
                    pe.wait_ge(S[s + "probs"], at(g, s + "probs", n * UNITS + u + 1))
                    for i in range(SLOTS):
                        last = pe.matmul(ps[2][VW * i:VW * i + VW, b * T:(b + 1) * T], x.v_pad[0:nk, b, SLOTS * j + i, :],
                                         x.probs[u % 2][0:nk, i * T:(i + 1) * T], start=True, stop=True)
                    last.then_inc(S[s + "pv"], 1)

                def turn_out(j):
                    pe.wait_ge(S[s + "o_sb"], at(g, s + "o_sb", TILES * n + j + 1))
                    pe.wait_ge(S[s + "m_sb"], at(g, s + "m_sb", TILES * n + min(j + LAG + 1, TILES)))
                    if j >= 1:
                        pe.wait_ge(S[s + "o_norm"], at(g, s + "o_norm", TILES * n + j))
                    for b in range(GROUP):
                        last = pe.transpose(ps[3][:, b * P:(b + 1) * P], x.o_sb[:, b * T:(b + 1) * T], ident[:])
                    last.then_inc(S[s + "o_t"], 1)

                for phase, j, b in attention_units(m):
                    yield phase
                    if phase.startswith("score"):
                        scores(j, b)
                    elif phase.startswith("max"):
                        turn_max(j)
                    else:
                        if (j, b) == (0, 0):
                            scores_t(0, 0)
                        if b + 1 < GROUP:
                            scores_t(j, b + 1)
                        elif j + 1 < TILES:
                            scores_t(j + 1, 0)
                        if j >= 1 and b == 1:
                            turn_out(j - 1)
                        weigh(j, b)
                yield f"out{m}"
                turn_out(TILES - 1)
                yield f"norm{m}"
                pe.wait_ge(S[s + "o_norm"], at(g, s + "o_norm", TILES * (n + 1)))
                turn(ps[2], lambda b: x.o_norm[:, b, :]).then_inc(S[s + "on_t"], 1)
                yield f"sum{m}"
                pe.wait_ge(S[s + "on_sb"], at(g, s + "on_sb", n + 1))
                for b in range(GROUP):
                    last = pe.matmul(ps[1][:, b * D:(b + 1) * D], x.feat[:, seq_tok(b)], mat(f"wo{m}"),
                                     start=True, stop=True)
                last.then_inc(S[s + "attn"], 1)

            def head(g):
                ps, feat = bank["a_"], fr.feat
                yield "ctx_turn"
                pe.wait_ge(S["a_ln_hat"], at(g, "a_ln_hat", LN_CTX + 1))
                if g is not FIRST:
                    pe.wait_ge(S["moe_hi"], at(g, "moe_hi", 0))
                turn(ps[2], lambda b: ctx_hat[:, b, :], C).then_inc(S["a_turned"], 1)
                if g is not FIRST:
                    pe.wait_ge(S["logits"], at(g, "logits", 0))
                turn(ps[3], lambda b: ctx_tok[:, b, 0:D], C).then_inc(S["a_turned"], 1)
                yield "x_turn"
                pe.wait_ge(S["a_feat"], at(g, "a_feat", F_CTX + 1))
                for b in range(GROUP):
                    last = pe.matmul(ps[1][0:C, 4 * b:4 * b + 4], norm1_f[:, seq_keys(b, C)], fc1_w[:],
                                     start=True, stop=True)
                last.then_inc(S["v0"], 1)
                pe.wait_ge(S["a_ln_hat"], at(g, "a_ln_hat", LN_X + 1))
                turn(ps[2], lambda b: x_hat[:, b, :]).then_inc(S["a_turned"], 1)
                yield "scores0"
                pe.wait_ge(S["a_feat"], at(g, "a_feat", F_X + 1))
                for b in range(GROUP):
                    last = pe.matmul(ps[3][:, seq_keys(b, C)], feat[:, seq_tok(b)], norm1_f[:, seq_keys(b, C)],
                                     start=True, stop=True)
                last.then_inc(S["s0"], 1)
                pe.wait_ge(S["ctx_phi"], at(g, "ctx_phi", 1))
                for b in range(GROUP):
                    last = pe.matmul(wide(0, b), ctx_phi[:, b, :], ctx_tok[:, b, :], start=True, stop=True)
                last.then_inc(S["kv"], 1)

            def tail(g):
                ps, feat = bank["a_"], fr.feat
                yield "max0"
                pe.wait_ge(S["max0"], at(g, "max0", 1))
                pe.transpose(ps[2][0:GROUP, 0:P], max0[:], ident[:]).then_inc(S["max0_t"], 1)
                yield "scores0_t"
                pe.wait_ge(S["max0_sb"], at(g, "max0_sb", 1))
                for b in range(GROUP):
                    pe.matmul(ps[3][0:C, seq_tok(b)], norm1_f[:, seq_keys(b, C)], feat[:, seq_tok(b)],
                              start=True, stop=False)
                    last = pe.matmul(ps[3][0:C, seq_tok(b)], pick_seq[:, b, 0:C], max0_t[:], start=False, stop=True)
                last.then_inc(S["s0_t"], 1)
                yield "values0"
                pe.wait_ge(S["p0"], at(g, "p0", 1))
                pe.wait_ge(S["v0_sb"], at(g, "v0_sb", 1))
                for b in range(GROUP):
                    last = pe.matmul(ps[2][:, 5 * b:5 * b + 5], p0[:, seq_tok(b)], v0[:, b, :], start=True, stop=True)
                last.then_inc(S["hpre"], 1)
                yield "hidden0"
                pe.wait_ge(S["h"], at(g, "h", 1))
                turn(ps[2], lambda b: h[:, b, :], P, 5).then_inc(S["h_t"], 1)
                yield "cross"
                pe.wait_ge(S["h_t_sb"], at(g, "h_t_sb", 1))
                for b in range(GROUP):
                    last = pe.matmul(ps[3][:, seq_tok(b)], h_t[:, seq_tok(b)], fc2_aug[:], start=True, stop=True)
                last.then_inc(S["cross"], 1)
                yield "cross_turn"
                pe.wait_ge(S["a_ln_hat"], at(g, "a_ln_hat", LN_CROSS + 1))
                turn(ps[2], lambda b: cross_hat[:, b, 0:D]).then_inc(S["a_turned"], 1)
                yield "scores1"
                pe.wait_ge(S["a_feat"], at(g, "a_feat", F_CROSS + 1))
                pe.wait_ge(S["kv_sb"], at(g, "kv_sb", 2))
                for b in range(GROUP):
                    last = pe.matmul(ps[0][:, seq_tok(b)], feat[:, seq_tok(b)], feat[:, seq_tok(b)],
                                     start=True, stop=True)
                last.then_inc(S["s1"], 1)
                yield "max1"
                pe.wait_ge(S["max1"], at(g, "max1", 1))
                pe.transpose(ps[1][0:GROUP, 0:P], max1[:], ident[:]).then_inc(S["max1_t"], 1)
                yield "scores1_t"
                pe.wait_ge(S["max1_sb"], at(g, "max1_sb", 1))
                for b in range(GROUP):
                    pe.matmul(ps[0][:, seq_tok(b)], feat[:, seq_tok(b)], feat[:, seq_tok(b)], start=True, stop=False)
                    last = pe.matmul(ps[0][:, seq_tok(b)], pick_seq[:, b, :], max1_t[:], start=False, stop=True)
                last.then_inc(S["s1_t"], 1)
                yield "values1"
                pe.wait_ge(S["cross_g"], at(g, "cross_g", 1))
                pe.wait_ge(S["p1"], at(g, "p1", 1))
                for b in range(GROUP):
                    last = pe.matmul(wide(1, b), p1[:, seq_tok(b)], cross_hat[:, b, :], start=True, stop=True)
                last.then_inc(S["pv1"], 1)
                yield "x1_turn"
                pe.wait_ge(S["x1"], at(g, "x1", 1))
                turn(ps[0], lambda b: x1[:, b, :]).then_inc(S["a_turned"], 1)
                yield "linear"
                pe.wait_ge(S["x1_phi"], at(g, "x1_phi", 1))
                for b in range(GROUP):
                    last = pe.matmul(wide(1, b), x1_phi[:, seq_tok(b)], kv[:, b, :], start=True, stop=True)
                last.then_inc(S["num"], 1)
                yield "sa_turn"
                turn_hat(g, "a_", LN_SA)
                yield from attention(g, "a_", SELF2, feat[:], F_SA)
                yield "caq_turn"
                turn_hat(g, "a_", LN_CAQ)
                yield from attention(g, "a_", CROSS2, cakv_f[:], F_CAQ)
                yield "moe_turn"
                turn_hat(g, "a_", LN_MOE)
                yield "router"
                pe.wait_ge(S["a_feat"], at(g, "a_feat", F_MOE + 1))
                for b in range(GROUP):
                    last = pe.matmul(ps[3][:, EXPERTS * b:EXPERTS * (b + 1)], feat[:, seq_tok(b)], router_w[:],
                                     start=True, stop=True)
                last.then_inc(S["router"], 1)

            def front(g, ahead):
                yield from tail(g)
                yield from head(ahead)

            def back(g):
                ps, feat = bank["b_"], bk.feat
                def expert_in(e, half):
                    for c in (2 * half, 2 * half + 1):
                        k = CHUNKS * e + c
                        if k >= 2:
                            pe.wait_ge(S["gelu"], at(g, "gelu", k - 1))
                        pe.matmul(ps[c % 2][:], moe_w1[0][:, e, c, :], moe_hi, start=True, stop=False)
                        pe.matmul(ps[c % 2][:], moe_w1[0][:, e, c, :], moe_lo, start=False, stop=False)
                        pe.matmul(ps[c % 2][:], moe_w1[1][:, e, c, :], moe_hi, start=False, stop=True)\
                            .then_inc(S["fc1"], 1)

                def expert_out(e, half):
                    if half == 0:
                        pe.wait_ge(S["moe_acc"], at(g, "moe_acc", max(e, 1)))
                        pe.wait_ge(S["gelu"], at(g, "gelu", CHUNKS * (e + 1)))
                    for b in (2 * half, 2 * half + 1):
                        for c in range(CHUNKS):
                            last = pe.matmul(ps[2 + e % 2][:, seq_tok(b)], hidden[e % 2][:, c, seq_tok(b)],
                                             moe_w2[:, e, c, :], start=(c == 0), stop=(c == CHUNKS - 1))
                    if half == 1:
                        last.then_inc(S["fc2"], 1)

                for e in range(EXPERTS):
                    for half in range(2):
                        yield f"in{e}_{half}"
                        if e == 0 and half == 0:
                            pe.wait_ge(S["moe_lo"], at(g, "moe_lo", 1))
                        expert_in(e, half)
                    if e == 0:
                        yield "gates"
                        pe.wait_ge(S["gates"], at(g, "gates", 1))
                        turn(ps[2], lambda b: gates[:, b, :], P, EXPERTS).then_inc(S["gates_t"], 1)
                        pe.wait_ge(S["gates_sb"], at(g, "gates_sb", 1))
                        pe.wait_ge(S["ffn_sum"], at(g, "ffn_sum", 0))
                        for b in range(GROUP):
                            last = pe.matmul(ps[3][:, seq_tok(b)], gates_t[:, seq_tok(b)], moe_b2[:],
                                             start=True, stop=True)
                        last.then_inc(S["gate_bias"], 1)
                    else:
                        for half in range(2):
                            yield f"out{e - 1}_{half}"
                            expert_out(e - 1, half)
                for half in range(2):
                    yield f"out{EXPERTS - 1}_{half}"
                    expert_out(EXPERTS - 1, half)
                yield "l3_turn"
                pe.wait_ge(S["moe_acc"], at(g, "moe_acc", EXPERTS + 1))
                turn(ps[2], lambda b: bk.x_res[:, b, :]).then_inc(S["b_turned"], 1)
                yield from attention(g, "b_", SELF3, feat[:], F_L3)
                yield "n31_turn"
                turn_hat(g, "b_", LN_31)
                pe.wait_ge(S["ctx_kept"], at(g, "ctx_kept", 1))
                yield from attention(g, "b_", CROSS3, ctx_kept[:], F_31)
                yield "n32_turn"
                turn_hat(g, "b_", LN_32)
                yield "ffn_in"
                pe.wait_ge(S["b_feat"], at(g, "b_feat", F_32 + 1))
                for c in range(CHUNKS):
                    if c >= 2:
                        pe.wait_ge(S["ffn_relu"], at(g, "ffn_relu", c - 1))
                    pe.matmul(ps[c % 2][:], ffn_w1[:, c, :], feat[:], start=True, stop=True).then_inc(S["ffn1"], 1)
                yield "ffn_out"
                pe.wait_ge(S["ffn_relu"], at(g, "ffn_relu", CHUNKS))
                for b in range(GROUP):
                    for c in range(CHUNKS):
                        last = pe.matmul(ps[3][:, seq_tok(b)], hidden[0][:, c, seq_tok(b)], ffn_w2[:, c, :],
                                         start=(c == 0), stop=(c == CHUNKS - 1))
                last.then_inc(S["ffn2"], 1)

            pe.wait_ge(s_weights, weights_in)
            pe.wait_ge(s_fill, filled)
            alone(head(FIRST))
            weave(front(FIRST, SECOND))
            pe.wait_ge(s_experts, experts_in)
            pe.wait_ge(s_split, 2)
            with pe.Fori(0, steps - 1) as it:
                v = Values(pe, it)
                weave(front(Group(it, 1, v), Group(it, 2, v)), back(Group(it, 0, v)))
            alone(back(LAST))


def laid_out(inputs):
    import numpy as np

    def get(name):
        return np.asarray(inputs[name])

    def l0(n):
        return get(f"L0_xattn_{n}")

    def l1(n):
        return get(f"L1_xattn_{n}")

    def l2(n):
        return get(f"L2_xattn_{n}")

    def l3(n):
        return get(f"L3_xattn_{n}")

    f32 = np.float32
    col = {n: l0(n) for n in ("norm1_w", "norm1_b", "norm2_w", "norm2_b", "norm3_w", "norm3_b")}
    col |= {"sa_g": l2("sa_ln_g"), "sa_b": l2("sa_ln_b"), "caq_g": l2("ca_q_ln_g"), "caq_b": l2("ca_q_ln_b"),
            "cakv_g": l2("ca_kv_ln_g"), "cakv_b": l2("ca_kv_ln_b"), "moe_g": l2("moe_ln_g"), "moe_b": l2("moe_ln_b"),
            "g1": l3("g1"), "be1": l3("be1"), "g2": l3("g2"), "be2": l3("be2")}
    mat = {}
    for m, n in ((SELF2, "sa"), (CROSS2, "ca")):
        for k, w in enumerate("qkv"):
            mat[f"w{w}{m}"] = l2(f"{n}_in_w")[k * D:(k + 1) * D].T
            col[f"b{w}{m}"] = l2(f"{n}_in_b")[k * D:(k + 1) * D]
        mat[f"wo{m}"] = l2(f"{n}_out_w").T
    for m, n in ((SELF3, "s"), (CROSS3, "c")):
        for w in "qkv":
            mat[f"w{w}{m}"] = l3(f"W{w}_{n}").transpose(1, 0, 2).reshape(D, D)
            col[f"b{w}{m}"] = l3(f"b{w}_{n}").reshape(D)
        mat[f"wo{m}"] = l3(f"Wo_{n}")
    for c in range(CHUNKS):
        col[f"ffn_b1_{c}"] = l3("b1")[c * P:(c + 1) * P]
        for e in range(EXPERTS):
            col[f"moe_b1_{e}_{c}"] = l2("e_fc1_b")[e, c * P:(c + 1) * P]
    row = {n: l0(n) for n in ("norm2_w", "norm2_b", "gamma1", "gamma2", "norm3_w", "norm3_b")}
    row |= {"l1_gamma": l1("gamma"), "l1_beta": l1("beta"), "sa_out_b": l2("sa_out_b"), "ca_out_b": l2("ca_out_b"),
            "bo_s": l3("bo_s"), "bo_c": l3("bo_c"), "ffn_b2": l3("b2"), "g1": l3("g1"), "be1": l3("be1"),
            "g2": l3("g2"), "be2": l3("be2"), "g3": l3("g3"), "be3": l3("be3")}

    def groups(x):
        x = x.reshape(-1, GROUP, *x.shape[1:])
        return np.concatenate([x, np.zeros_like(x[:AHEAD])])

    def repeat(v):
        return np.broadcast_to(v, (P, *v.shape))

    feature = np.arange(P) // PARTS
    arrays = {
        "x": groups(get("x")), "ctx": groups(get("ctx_1024")),
        "cols": np.stack([col[n] for n in COLS], 1),
        "rows": repeat(np.stack([row[n] for n in ROWS])),
        "mats": np.stack([mat[n] for n in MATS], 1),
        "fc1_w": l0("fc1_w").T, "fc1_b": repeat(l0("fc1_b")),
        "fc2_aug": np.concatenate([l0("fc2_w").T, l0("fc2_b")[None]]),
        "router_w": l2("router_w").T, "router_b": repeat(l2("router_b")),
        "moe_w1": l2("e_fc1_w").reshape(EXPERTS, CHUNKS, P, D).transpose(3, 0, 1, 2),
        "moe_w2": l2("e_fc2_w").reshape(EXPERTS, D, CHUNKS, P).transpose(3, 0, 2, 1),
        "moe_b2": l2("e_fc2_b"),
        "ffn_w1": l3("W1").reshape(D, CHUNKS, P),
        "ffn_w2": l3("W2").reshape(CHUNKS, P, D).transpose(1, 0, 2),
        "slot_mask": (feature[:, None] // DH == np.arange(SLOTS)).astype(f32),
        "expert_id": repeat(np.arange(EXPERTS, dtype=f32)),
        "pick_seq": np.repeat(np.eye(GROUP, dtype=f32)[:, :, None], T, 2),
    }
    return {n: np.ascontiguousarray(v) for n, v in arrays.items()}


def kernel(**inputs):
    import concourse.bacc as bacc
    from concourse.bass_utils import run_bass_kernel_spmd
    arrays = laid_out(inputs)
    nc = bacc.Bacc("TRN2", target_bir_lowering=False, num_devices=1)
    aps = {n: nc.dram_tensor(f"in_{n}", v.shape, mybir.dt.from_np(v.dtype), kind="ExternalInput").ap()
           for n, v in arrays.items()}
    steps = arrays["x"].shape[0] - AHEAD
    out = nc.dram_tensor("out", (steps, GROUP, T, D), F32, kind="ExternalOutput").ap()
    build(nc, aps, out, steps)
    r = run_bass_kernel_spmd(nc, [{f"in_{n}": v for n, v in arrays.items()}], core_ids=[0])
    return r.results[0]["out"].reshape(-1, T, D)
```
